# Optimizing a Trainium2 kernel written in Bass

```python
import numpy as np
import jax
import jax.numpy as jnp

def _softmax(x, axis=-1):
    return jax.nn.softmax(x, axis=axis)

def _gelu(x):
    return jax.nn.gelu(x, approximate=True)

def _silu(x):
    return jax.nn.silu(x)

def _sigmoid(x):
    return jax.nn.sigmoid(x)

def _layernorm(x, axis=-1, eps=1e-05):
    m = jnp.mean(x, axis=axis, keepdims=True)
    v = jnp.var(x, axis=axis, keepdims=True)
    return (x - m) / jnp.sqrt(v + eps)

def _scatter_add(tgt, idx, src, axis=0):
    return tgt.at[idx].add(src)

def _segment_sum(src, seg, n):
    return jax.ops.segment_sum(src, seg, n)
kernel_name = 'mk_decoder_postln_d2_seqx_r8_e1784d'

def setup_inputs(seed: int=0):
    np.random.seed(seed)
    _w = jnp.asarray

    def _rec_inputs():
        import jax
        import jax.numpy as jnp
        _rk = jax.random.key(seed)
        x = -0.0003929 + 0.9999 * jax.random.normal(jax.random.fold_in(_rk, 1), (8, 128, 256), jnp.float32)
        _lenS = 128 - jax.random.randint(jax.random.fold_in(_rk, 7), (8,), 0, max(1, 128 // 4) + 1, jnp.int32)
        _lenS2 = 128 - jax.random.randint(jax.random.fold_in(_rk, 8), (8,), 0, max(1, 128 // 4) + 1, jnp.int32)
        _ctx_2048P = jax.random.normal(jax.random.fold_in(_rk, 11), (8, 16, 256), jnp.float32)
        _ctx_2048c = jax.random.dirichlet(jax.random.fold_in(_rk, 511), 0.3 * jnp.ones((16,), jnp.float32), (8, 128))
        _ctx_2048t = jnp.einsum('bsk,bkd->bsd', _ctx_2048c, _ctx_2048P)
        _ctx_2048t = _ctx_2048t * jax.lax.rsqrt(jnp.mean(jnp.square(_ctx_2048t)) + 1e-12) * 0.953939
        ctx_2048 = -0.000514642 + 1.00011 * (_ctx_2048t + 0.3 * jax.random.normal(jax.random.fold_in(_rk, 611), (8, 128, 256), jnp.float32))
        _validS = jnp.arange(128)[None, :] < _lenS[:, None]
        _validS2 = jnp.arange(128)[None, :] < _lenS2[:, None]
        _causal = jnp.tril(jnp.ones((128, 128), dtype=bool))
        mask_BxS2_bk0 = jnp.logical_not(jnp.broadcast_to(_validS2[:, :], (8, 128)))
        return (x, ctx_2048, mask_BxS2_bk0)
    x, ctx_2048, mask_BxS2_bk0 = _rec_inputs()

    def _L0_attn_setup():
        import jax, jax.numpy as jnp
        import numpy as np
        import math
        N_HEAD = 16
        LAYER = 1
        LAMBDA_INIT = 0.8 - 0.6 * math.exp(-0.3 * (LAYER - 1))
        key = jax.random.key(seed)
        ks = jax.random.split(key, 7)
        B, T, E = (2, 256, 256)
        s = 0.02
        return {'x': jax.random.normal(ks[0], (B, T, E), dtype=jnp.float32), 'W_attn': jax.random.normal(ks[1], (E, 3 * E), dtype=jnp.float32) * s, 'W_proj': jax.random.normal(ks[2], (E, E), dtype=jnp.float32) * s, 'lambda_q1': jax.random.normal(ks[3], (E,), dtype=jnp.float32) * 0.1, 'lambda_k1': jax.random.normal(ks[4], (E,), dtype=jnp.float32) * 0.1, 'lambda_q2': jax.random.normal(ks[5], (E,), dtype=jnp.float32) * 0.1, 'lambda_k2': jax.random.normal(ks[6], (E,), dtype=jnp.float32) * 0.1}
    _L0_attn_all = _L0_attn_setup()
    _L0_attn_in = {k: v for k, v in _L0_attn_all.items() if k in ('W_attn', 'W_proj', 'lambda_q1', 'lambda_k1', 'lambda_q2', 'lambda_k2')}
    del _L0_attn_all

    def _L0_xattn_setup():
        import jax, jax.numpy as jnp
        import numpy as np
        FEAT = 256
        G = 16
        DG = FEAT // G
        key = jax.random.key(seed)
        ks = jax.random.split(key, 8)
        bs, N1, N2 = (2, 512, 64)
        s = 1.0 / np.sqrt(FEAT)
        return {'ref_feat': jax.random.normal(ks[0], (bs, N1, FEAT), jnp.float32), 'sup_feat': jax.random.normal(ks[1], (bs, N2, FEAT), jnp.float32), 'W_fc': jax.random.normal(ks[2], (FEAT, FEAT), jnp.float32) * s, 'b_fc': jnp.zeros((FEAT,), jnp.float32), 'W_q': jax.random.normal(ks[3], (FEAT, FEAT), jnp.float32) * s, 'b_q': jnp.zeros((FEAT,), jnp.float32), 'W_k': jax.random.normal(ks[4], (FEAT, FEAT), jnp.float32) * s, 'b_k': jnp.zeros((FEAT,), jnp.float32), 'W_v': jax.random.normal(ks[5], (FEAT, FEAT, 1, 1), jnp.float32) * 0.01, 'b_v': jnp.zeros((FEAT,), jnp.float32)}
    _L0_xattn_all = _L0_xattn_setup()
    _L0_xattn_in = {k: v for k, v in _L0_xattn_all.items() if k in ('W_fc', 'b_fc', 'W_q', 'b_q', 'W_k', 'b_k', 'W_v', 'b_v')}
    del _L0_xattn_all

    def _L0_ffn_setup():
        import jax, jax.numpy as jnp
        import numpy as np
        B, S, H = (4, 128, 256)
        NH = 16
        HD = H // NH
        RD = HD // 2
        LAT = H // 4
        I = 128
        NE = 8
        NSH = 1
        NR = NE - NSH
        TOPK = 2
        EPS = 1e-05
        SCALING = 8.0

        def _w(key, shape, fan_in):
            return jax.random.normal(key, shape, dtype=jnp.float32) / np.sqrt(fan_in)

        def rmsnorm(x, w):
            rms = jax.lax.rsqrt(jnp.mean(x * x, axis=-1, keepdims=True) + EPS)
            return w * rms * x

        def rope_cos_sin(seq_len):
            inv_freq = 1.0 / 10000.0 ** (jnp.arange(0, RD, 2, dtype=jnp.float32) / RD)
            t = jnp.arange(seq_len, dtype=jnp.float32)
            ang = jnp.outer(t, inv_freq)
            emb = jnp.concatenate([ang, ang], axis=-1)
            return (jnp.cos(emb), jnp.sin(emb))

        def apply_rope(x, cos, sin):
            c = cos[None, :, None, :]
            s = sin[None, :, None, :]
            x1, x2 = jnp.split(x, 2, axis=-1)
            rot = jnp.concatenate([-x2, x1], axis=-1)
            return x * c + rot * s

        def expert_ffn(x, wg, wu, wd):
            h = jax.nn.silu(x @ wg) * (x @ wu) / SCALING
            return h @ wd

        def attention(x, kv_d_w, q_d_w, k_u_w, v_u_w, q_u_w, rope_k_w, rope_q_w, o_w):
            b, s, _ = x.shape
            kv_d = x @ kv_d_w
            q_d = x @ q_d_w
            k_p = (kv_d @ k_u_w).reshape(b, s, NH, RD)
            q_p = (q_d @ q_u_w).reshape(b, s, NH, RD)
            v = (kv_d @ v_u_w).reshape(b, s, NH, HD)
            k_r = (x @ rope_k_w).reshape(b, s, NH, RD)
            q_r = (q_d @ rope_q_w).reshape(b, s, NH, RD)
            cos, sin = rope_cos_sin(s)
            k_r = apply_rope(k_r, cos, sin)
            q_r = apply_rope(q_r, cos, sin)
            k = jnp.concatenate([k_p, k_r], axis=-1)
            q = jnp.concatenate([q_p, q_r], axis=-1)
            scale = 1.0 / np.sqrt(HD)
            scores = jnp.einsum('bqhd,bkhd->bhqk', q, k) * scale
            causal = jnp.tril(jnp.ones((s, s), dtype=bool))
            scores = jnp.where(causal[None, None], scores, jnp.finfo(scores.dtype).min)
            probs = jax.nn.softmax(scores, axis=-1)
            out = jnp.einsum('bhqk,bkhd->bqhd', probs, v).reshape(b, s, H)
            return out @ o_w

        def moe(x, sh_gate, sh_up, sh_down, r_gate, r_up, r_down, router_w, router_b):
            shared = expert_ffn(x, sh_gate, sh_up, sh_down)
            logits = x @ router_w + router_b
            probs = jax.nn.sigmoid(logits)
            scores, idx = jax.lax.top_k(probs, TOPK)
            scores = scores / jnp.sum(scores, axis=-1, keepdims=True)
            w = jnp.sum(jax.nn.one_hot(idx, NR, dtype=x.dtype) * scores[..., None], axis=-2)
            combined = jnp.zeros_like(x)
            for e in range(NR):
                combined = combined + w[..., e:e + 1] * expert_ffn(x, r_gate[e], r_up[e], r_down[e])
            return shared + combined
        key = jax.random.key(seed)
        ks = jax.random.split(key, 24)
        return {'x': jax.random.normal(ks[0], (B, S, H), dtype=jnp.float32), 'ln1_w': jnp.ones((H,), jnp.float32), 'ln2_w': jnp.ones((H,), jnp.float32), 'kv_d_w': _w(ks[1], (H, LAT), H), 'q_d_w': _w(ks[2], (H, LAT), H), 'k_u_w': _w(ks[3], (LAT, H // 2), LAT), 'v_u_w': _w(ks[4], (LAT, H), LAT), 'q_u_w': _w(ks[5], (LAT, H // 2), LAT), 'rope_k_w': _w(ks[6], (H, H // 2), H), 'rope_q_w': _w(ks[7], (LAT, H // 2), LAT), 'o_w': _w(ks[8], (H, H), H), 'sh_gate': _w(ks[9], (H, I), H), 'sh_up': _w(ks[10], (H, I), H), 'sh_down': _w(ks[11], (I, H), I), 'r_gate': _w(ks[12], (NR, H, I), H), 'r_up': _w(ks[13], (NR, H, I), H), 'r_down': _w(ks[14], (NR, I, H), I), 'router_w': _w(ks[15], (H, NR), H), 'router_b': jnp.zeros((NR,), jnp.float32)}
    _L0_ffn_all = _L0_ffn_setup()
    _L0_ffn_in = {k: v for k, v in _L0_ffn_all.items() if k in ('ln1_w', 'ln2_w', 'kv_d_w', 'q_d_w', 'k_u_w', 'v_u_w', 'q_u_w', 'rope_k_w', 'rope_q_w', 'o_w', 'sh_gate', 'sh_up', 'sh_down', 'r_gate', 'r_up', 'r_down', 'router_w', 'router_b')}
    del _L0_ffn_all

    def _L1_attn_setup():
        import jax, jax.numpy as jnp
        import numpy as np
        B, T, HID = (1, 256, 256)
        H = 16
        D = HID // H
        EPS = 1e-05

        def _layer_norm(x, eps=1e-05):
            mu = jnp.mean(x, axis=-1, keepdims=True)
            var = jnp.mean((x - mu) ** 2, axis=-1, keepdims=True)
            return (x - mu) * jax.lax.rsqrt(var + eps)

        def _feature_map(x, gamma, beta):
            return _layer_norm(x * gamma + beta)
        key = jax.random.key(seed)
        ks = jax.random.split(key, 8)
        s = HID ** (-0.5)
        return {'hidden_states': jax.random.normal(ks[0], (B, T, HID), jnp.float32), 'Wq': jax.random.normal(ks[1], (HID, HID), jnp.float32) * s, 'Wk': jax.random.normal(ks[2], (HID, HID), jnp.float32) * s, 'Wv': jax.random.normal(ks[3], (HID, HID), jnp.float32) * s, 'Wo': jax.random.normal(ks[4], (HID, HID), jnp.float32) * s, 'gamma': 1.0 + 0.1 * jax.random.normal(ks[5], (D,), jnp.float32), 'beta': 0.1 * jax.random.normal(ks[6], (D,), jnp.float32)}
    _L1_attn_all = _L1_attn_setup()
    _L1_attn_in = {k: v for k, v in _L1_attn_all.items() if k in ('Wq', 'Wk', 'Wv', 'Wo', 'gamma', 'beta')}
    del _L1_attn_all

    def _L1_xattn_setup():
        import jax, jax.numpy as jnp
        import numpy as np
        key = jax.random.key(seed)
        k1, k2, k3 = jax.random.split(key, 3)
        B, S, D, M = (8, 256, 256, 128)
        hidden_states = jax.random.normal(k1, (B, S, D), dtype=jnp.float32)
        memory_tokens = jax.random.normal(k2, (B, M, D), dtype=jnp.float32)
        memory_mask = jax.random.randint(k3, (B, M), 0, 2).astype(jnp.bool_)
        return {'hidden_states': hidden_states, 'memory_tokens': memory_tokens, 'memory_mask': memory_mask}
    _L1_xattn_all = _L1_xattn_setup()
    _L1_xattn_in = {k: v for k, v in _L1_xattn_all.items() if k in ()}
    del _L1_xattn_all

    def _L1_ffn_setup():
        import jax, jax.numpy as jnp
        import numpy as np
        from jax import lax
        B, S, H = (1, 256, 256)
        E, I, TOP_K = (64, 64, 8)
        SHARED_I = 64
        key = jax.random.key(seed)
        ks = jax.random.split(key, 8)
        sc = 0.02
        return {'hidden_states': jax.random.normal(ks[0], (B, S, H), jnp.float32), 'router_w': jax.random.normal(ks[1], (E, H), jnp.float32) * sc, 'gate_up_proj': jax.random.normal(ks[2], (E, 2 * I, H), jnp.float32) * sc, 'down_proj': jax.random.normal(ks[3], (E, H, I), jnp.float32) * sc, 'shared_gate_w': jax.random.normal(ks[4], (SHARED_I, H), jnp.float32) * sc, 'shared_up_w': jax.random.normal(ks[5], (SHARED_I, H), jnp.float32) * sc, 'shared_down_w': jax.random.normal(ks[6], (H, SHARED_I), jnp.float32) * sc, 'shared_expert_gate_w': jax.random.normal(ks[7], (1, H), jnp.float32) * sc}
    _L1_ffn_all = _L1_ffn_setup()
    _L1_ffn_in = {k: v for k, v in _L1_ffn_all.items() if k in ('router_w', 'gate_up_proj', 'down_proj', 'shared_gate_w', 'shared_up_w', 'shared_down_w', 'shared_expert_gate_w')}
    del _L1_ffn_all
    return {'x': x, 'ctx_2048': ctx_2048, 'mask_BxS2_bk0': mask_BxS2_bk0, 'L0_attn_W_attn': _L0_attn_in['W_attn'], 'L0_attn_W_proj': _L0_attn_in['W_proj'], 'L0_attn_lambda_q1': _L0_attn_in['lambda_q1'], 'L0_attn_lambda_k1': _L0_attn_in['lambda_k1'], 'L0_attn_lambda_q2': _L0_attn_in['lambda_q2'], 'L0_attn_lambda_k2': _L0_attn_in['lambda_k2'], 'L0_xattn_W_fc': _L0_xattn_in['W_fc'], 'L0_xattn_b_fc': _L0_xattn_in['b_fc'], 'L0_xattn_W_q': _L0_xattn_in['W_q'], 'L0_xattn_b_q': _L0_xattn_in['b_q'], 'L0_xattn_W_k': _L0_xattn_in['W_k'], 'L0_xattn_b_k': _L0_xattn_in['b_k'], 'L0_xattn_W_v': _L0_xattn_in['W_v'], 'L0_xattn_b_v': _L0_xattn_in['b_v'], 'L0_ffn_ln1_w': _L0_ffn_in['ln1_w'], 'L0_ffn_ln2_w': _L0_ffn_in['ln2_w'], 'L0_ffn_kv_d_w': _L0_ffn_in['kv_d_w'], 'L0_ffn_q_d_w': _L0_ffn_in['q_d_w'], 'L0_ffn_k_u_w': _L0_ffn_in['k_u_w'], 'L0_ffn_v_u_w': _L0_ffn_in['v_u_w'], 'L0_ffn_q_u_w': _L0_ffn_in['q_u_w'], 'L0_ffn_rope_k_w': _L0_ffn_in['rope_k_w'], 'L0_ffn_rope_q_w': _L0_ffn_in['rope_q_w'], 'L0_ffn_o_w': _L0_ffn_in['o_w'], 'L0_ffn_sh_gate': _L0_ffn_in['sh_gate'], 'L0_ffn_sh_up': _L0_ffn_in['sh_up'], 'L0_ffn_sh_down': _L0_ffn_in['sh_down'], 'L0_ffn_r_gate': _L0_ffn_in['r_gate'], 'L0_ffn_r_up': _L0_ffn_in['r_up'], 'L0_ffn_r_down': _L0_ffn_in['r_down'], 'L0_ffn_router_w': _L0_ffn_in['router_w'], 'L0_ffn_router_b': _L0_ffn_in['router_b'], 'L1_attn_Wq': _L1_attn_in['Wq'], 'L1_attn_Wk': _L1_attn_in['Wk'], 'L1_attn_Wv': _L1_attn_in['Wv'], 'L1_attn_Wo': _L1_attn_in['Wo'], 'L1_attn_gamma': _L1_attn_in['gamma'], 'L1_attn_beta': _L1_attn_in['beta'], 'L1_ffn_router_w': _L1_ffn_in['router_w'], 'L1_ffn_gate_up_proj': _L1_ffn_in['gate_up_proj'], 'L1_ffn_down_proj': _L1_ffn_in['down_proj'], 'L1_ffn_shared_gate_w': _L1_ffn_in['shared_gate_w'], 'L1_ffn_shared_up_w': _L1_ffn_in['shared_up_w'], 'L1_ffn_shared_down_w': _L1_ffn_in['shared_down_w'], 'L1_ffn_shared_expert_gate_w': _L1_ffn_in['shared_expert_gate_w']}

def reference(x, ctx_2048, mask_BxS2_bk0, L0_attn_W_attn, L0_attn_W_proj, L0_attn_lambda_q1, L0_attn_lambda_k1, L0_attn_lambda_q2, L0_attn_lambda_k2, L0_xattn_W_fc, L0_xattn_b_fc, L0_xattn_W_q, L0_xattn_b_q, L0_xattn_W_k, L0_xattn_b_k, L0_xattn_W_v, L0_xattn_b_v, L0_ffn_ln1_w, L0_ffn_ln2_w, L0_ffn_kv_d_w, L0_ffn_q_d_w, L0_ffn_k_u_w, L0_ffn_v_u_w, L0_ffn_q_u_w, L0_ffn_rope_k_w, L0_ffn_rope_q_w, L0_ffn_o_w, L0_ffn_sh_gate, L0_ffn_sh_up, L0_ffn_sh_down, L0_ffn_r_gate, L0_ffn_r_up, L0_ffn_r_down, L0_ffn_router_w, L0_ffn_router_b, L1_attn_Wq, L1_attn_Wk, L1_attn_Wv, L1_attn_Wo, L1_attn_gamma, L1_attn_beta, L1_ffn_router_w, L1_ffn_gate_up_proj, L1_ffn_down_proj, L1_ffn_shared_gate_w, L1_ffn_shared_up_w, L1_ffn_shared_down_w, L1_ffn_shared_expert_gate_w):
    import jax
    import jax.numpy as jnp

    def _L0_attn_ref(x, W_attn, W_proj, lambda_q1, lambda_k1, lambda_q2, lambda_k2):
        import jax, jax.numpy as jnp
        import numpy as np
        import math
        N_HEAD = 16
        LAYER = 1
        LAMBDA_INIT = 0.8 - 0.6 * math.exp(-0.3 * (LAYER - 1))
        B, T, E = x.shape
        C = E // 2
        H = N_HEAD
        hd = E // H // 2
        scale = hd ** (-0.5)
        qkv = x @ W_attn
        q1 = qkv[..., 0 * C:1 * C].reshape(B, T, H, hd)
        k1 = qkv[..., 1 * C:2 * C].reshape(B, T, H, hd)
        q2 = qkv[..., 2 * C:3 * C].reshape(B, T, H, hd)
        k2 = qkv[..., 3 * C:4 * C].reshape(B, T, H, hd)
        v = qkv[..., 4 * C:6 * C].reshape(B, T, H, 2 * hd)
        lam = jnp.exp(jnp.dot(lambda_q1, lambda_k1)) - jnp.exp(jnp.dot(lambda_q2, lambda_k2)) + LAMBDA_INIT
        attn1 = jnp.einsum('bthd,bshd->bhts', q1, k1) * scale
        attn2 = jnp.einsum('bthd,bshd->bhts', q2, k2) * scale
        score = jax.nn.softmax(attn1 - lam * attn2, axis=-1)
        out = jnp.einsum('bhts,bshd->bthd', score, v)
        out = (1.0 - LAMBDA_INIT) * out.reshape(B, T, E)
        return out @ W_proj

    def _L0_xattn_ref(ref_feat, sup_feat, W_fc, b_fc, W_q, b_q, W_k, b_k, W_v, b_v):
        import jax, jax.numpy as jnp
        import numpy as np
        FEAT = 256
        G = 16
        DG = FEAT // G
        bs, N1, _ = ref_feat.shape
        sup = jax.nn.relu(sup_feat @ W_fc.T + b_fc)
        ref = jax.nn.relu(ref_feat @ W_fc.T + b_fc)
        q = (ref @ W_q.T + b_q).reshape(bs, N1, G, DG)
        k = (sup @ W_k.T + b_k).reshape(bs, -1, G, DG)
        aff = jnp.einsum('bqhd,bkhd->bhqk', q, k) * (1.0 / np.sqrt(DG))
        p = jax.nn.softmax(aff, axis=-1)
        out_h = jnp.einsum('bhqk,bkf->bhqf', p, sup)
        Wv = W_v.reshape(G, DG, FEAT)
        attn = jnp.einsum('bhqf,hjf->bqhj', out_h, Wv).reshape(bs, N1, FEAT) + b_v
        return ref + attn

    def _L0_ffn_ref(x, ln1_w, ln2_w, kv_d_w, q_d_w, k_u_w, v_u_w, q_u_w, rope_k_w, rope_q_w, o_w, sh_gate, sh_up, sh_down, r_gate, r_up, r_down, router_w, router_b):
        import jax, jax.numpy as jnp
        import numpy as np
        B, S, H = (4, 128, 256)
        NH = 16
        HD = H // NH
        RD = HD // 2
        LAT = H // 4
        I = 128
        NE = 8
        NSH = 1
        NR = NE - NSH
        TOPK = 2
        EPS = 1e-05
        SCALING = 8.0

        def _w(key, shape, fan_in):
            return jax.random.normal(key, shape, dtype=jnp.float32) / np.sqrt(fan_in)

        def rmsnorm(x, w):
            rms = jax.lax.rsqrt(jnp.mean(x * x, axis=-1, keepdims=True) + EPS)
            return w * rms * x

        def rope_cos_sin(seq_len):
            inv_freq = 1.0 / 10000.0 ** (jnp.arange(0, RD, 2, dtype=jnp.float32) / RD)
            t = jnp.arange(seq_len, dtype=jnp.float32)
            ang = jnp.outer(t, inv_freq)
            emb = jnp.concatenate([ang, ang], axis=-1)
            return (jnp.cos(emb), jnp.sin(emb))

        def apply_rope(x, cos, sin):
            c = cos[None, :, None, :]
            s = sin[None, :, None, :]
            x1, x2 = jnp.split(x, 2, axis=-1)
            rot = jnp.concatenate([-x2, x1], axis=-1)
            return x * c + rot * s

        def expert_ffn(x, wg, wu, wd):
            h = jax.nn.silu(x @ wg) * (x @ wu) / SCALING
            return h @ wd

        def attention(x, kv_d_w, q_d_w, k_u_w, v_u_w, q_u_w, rope_k_w, rope_q_w, o_w):
            b, s, _ = x.shape
            kv_d = x @ kv_d_w
            q_d = x @ q_d_w
            k_p = (kv_d @ k_u_w).reshape(b, s, NH, RD)
            q_p = (q_d @ q_u_w).reshape(b, s, NH, RD)
            v = (kv_d @ v_u_w).reshape(b, s, NH, HD)
            k_r = (x @ rope_k_w).reshape(b, s, NH, RD)
            q_r = (q_d @ rope_q_w).reshape(b, s, NH, RD)
            cos, sin = rope_cos_sin(s)
            k_r = apply_rope(k_r, cos, sin)
            q_r = apply_rope(q_r, cos, sin)
            k = jnp.concatenate([k_p, k_r], axis=-1)
            q = jnp.concatenate([q_p, q_r], axis=-1)
            scale = 1.0 / np.sqrt(HD)
            scores = jnp.einsum('bqhd,bkhd->bhqk', q, k) * scale
            causal = jnp.tril(jnp.ones((s, s), dtype=bool))
            scores = jnp.where(causal[None, None], scores, jnp.finfo(scores.dtype).min)
            probs = jax.nn.softmax(scores, axis=-1)
            out = jnp.einsum('bhqk,bkhd->bqhd', probs, v).reshape(b, s, H)
            return out @ o_w

        def moe(x, sh_gate, sh_up, sh_down, r_gate, r_up, r_down, router_w, router_b):
            shared = expert_ffn(x, sh_gate, sh_up, sh_down)
            logits = x @ router_w + router_b
            probs = jax.nn.sigmoid(logits)
            scores, idx = jax.lax.top_k(probs, TOPK)
            scores = scores / jnp.sum(scores, axis=-1, keepdims=True)
            w = jnp.sum(jax.nn.one_hot(idx, NR, dtype=x.dtype) * scores[..., None], axis=-2)
            combined = jnp.zeros_like(x)
            for e in range(NR):
                combined = combined + w[..., e:e + 1] * expert_ffn(x, r_gate[e], r_up[e], r_down[e])
            return shared + combined
        h = x + attention(rmsnorm(x, ln1_w), kv_d_w, q_d_w, k_u_w, v_u_w, q_u_w, rope_k_w, rope_q_w, o_w)
        out = h + moe(rmsnorm(h, ln2_w), sh_gate, sh_up, sh_down, r_gate, r_up, r_down, router_w, router_b)
        return out

    def _L1_attn_ref(hidden_states, Wq, Wk, Wv, Wo, gamma, beta):
        import jax, jax.numpy as jnp
        import numpy as np
        B, T, HID = (1, 256, 256)
        H = 16
        D = HID // H
        EPS = 1e-05

        def _layer_norm(x, eps=1e-05):
            mu = jnp.mean(x, axis=-1, keepdims=True)
            var = jnp.mean((x - mu) ** 2, axis=-1, keepdims=True)
            return (x - mu) * jax.lax.rsqrt(var + eps)

        def _feature_map(x, gamma, beta):
            return _layer_norm(x * gamma + beta)
        b, t, _ = hidden_states.shape
        q = (hidden_states @ Wq.T).reshape(b, t, H, D)
        k = (hidden_states @ Wk.T).reshape(b, t, H, D)
        v = (hidden_states @ Wv.T).reshape(b, t, H, D)
        q = _feature_map(q, gamma, beta)
        k = _feature_map(k, gamma, beta)
        q = q * D ** (-0.5)
        attn = jnp.einsum('bqhd,bkhd->bhqk', q, k) ** 2
        mask = jnp.tril(jnp.ones((t, t), dtype=bool))
        attn = jnp.where(mask, attn, 0.0)
        o = jnp.einsum('bhqk,bkhd->bqhd', attn, v)
        z = jnp.sum(attn, axis=-1)
        o = o / (jnp.swapaxes(z, 1, 2)[..., None] + EPS)
        o = o.reshape(b, t, H * D)
        return o @ Wo.T

    def _L1_xattn_ref(hidden_states, memory_tokens, memory_mask):
        import jax, jax.numpy as jnp
        import numpy as np
        B, S, D = hidden_states.shape
        scale = 1.0 / jnp.sqrt(jnp.asarray(D, hidden_states.dtype))
        scores = jnp.einsum('bsd,bmd->bsm', hidden_states, memory_tokens) * scale
        neg_inf = jnp.asarray(-1e+30, scores.dtype)
        scores = jnp.where(memory_mask[:, None, :], scores, neg_inf)
        attn = jax.nn.softmax(scores, axis=-1)
        readout = jnp.einsum('bsm,bmd->bsd', attn, memory_tokens)
        valid_b = jnp.any(memory_mask, axis=-1)
        out = jnp.where(valid_b[:, None, None], readout, jnp.zeros_like(readout))
        return out

    def _L1_ffn_ref(hidden_states, router_w, gate_up_proj, down_proj, shared_gate_w, shared_up_w, shared_down_w, shared_expert_gate_w):
        import jax, jax.numpy as jnp
        import numpy as np
        from jax import lax
        B, S, H = (1, 256, 256)
        E, I, TOP_K = (64, 64, 8)
        SHARED_I = 64
        b, s, h_dim = hidden_states.shape
        h = hidden_states.reshape(-1, h_dim)
        T = h.shape[0]
        shared = jnp.dot(jax.nn.silu(jnp.dot(h, shared_gate_w.T)) * jnp.dot(h, shared_up_w.T), shared_down_w.T)
        shared = jax.nn.sigmoid(jnp.dot(h, shared_expert_gate_w.T)) * shared
        logits = jnp.dot(h, router_w.T)
        probs = jax.nn.softmax(logits.astype(jnp.float32), axis=-1)
        top_vals, top_idx = lax.top_k(probs, TOP_K)
        top_vals = top_vals / jnp.sum(top_vals, axis=-1, keepdims=True)
        top_vals = top_vals.astype(h.dtype)
        comb = jnp.zeros((T, E), h.dtype).at[jnp.arange(T)[:, None], top_idx].add(top_vals)

        def body(acc, xs):
            wgu, wd, w_e = xs
            g, u = jnp.split(jnp.dot(h, wgu.T), 2, axis=-1)
            eo = jnp.dot(jax.nn.silu(g) * u, wd.T)
            return (acc + eo * w_e[:, None], None)
        expert_out, _ = lax.scan(body, jnp.zeros_like(h), (gate_up_proj, down_proj, comb.T))
        return (expert_out + shared).reshape(b, s, h_dim)
    x = _layernorm(x + _L0_attn_ref(x, L0_attn_W_attn, L0_attn_W_proj, L0_attn_lambda_q1, L0_attn_lambda_k1, L0_attn_lambda_q2, L0_attn_lambda_k2), axis=-1)
    x = _layernorm(x + _L0_xattn_ref(x, ctx_2048, L0_xattn_W_fc, L0_xattn_b_fc, L0_xattn_W_q, L0_xattn_b_q, L0_xattn_W_k, L0_xattn_b_k, L0_xattn_W_v, L0_xattn_b_v), axis=-1)
    x = _layernorm(x + _L0_ffn_ref(x, L0_ffn_ln1_w, L0_ffn_ln2_w, L0_ffn_kv_d_w, L0_ffn_q_d_w, L0_ffn_k_u_w, L0_ffn_v_u_w, L0_ffn_q_u_w, L0_ffn_rope_k_w, L0_ffn_rope_q_w, L0_ffn_o_w, L0_ffn_sh_gate, L0_ffn_sh_up, L0_ffn_sh_down, L0_ffn_r_gate, L0_ffn_r_up, L0_ffn_r_down, L0_ffn_router_w, L0_ffn_router_b), axis=-1)
    x = _layernorm(x + _L1_attn_ref(x, L1_attn_Wq, L1_attn_Wk, L1_attn_Wv, L1_attn_Wo, L1_attn_gamma, L1_attn_beta), axis=-1)
    x = _layernorm(x + _L1_xattn_ref(x, ctx_2048, mask_BxS2_bk0), axis=-1)
    x = _layernorm(x + _L1_ffn_ref(x, L1_ffn_router_w, L1_ffn_gate_up_proj, L1_ffn_down_proj, L1_ffn_shared_gate_w, L1_ffn_shared_up_w, L1_ffn_shared_down_w, L1_ffn_shared_expert_gate_w), axis=-1)
    return x

_drawn_inputs = setup_inputs


def setup_inputs(seed=0):
    import zlib

    import numpy as np

    out = dict(_drawn_inputs(seed))
    spreads = {'L0_xattn_b_fc': (0.0, 0.1),
     'L0_xattn_b_q': (0.0, 0.8),
     'L0_xattn_b_k': (0.0, 2.0),
     'L0_xattn_b_v': (0.0, 0.1),
     'L0_ffn_ln1_w': (1.0, 0.2),
     'L0_ffn_ln2_w': (1.0, 0.6),
     'L0_ffn_router_b': (0.0, 0.8)}
    factors = {'L0_attn_W_attn': 4.875,
     'L0_attn_W_proj': 5.066,
     'L0_attn_lambda_q1': 8.0,
     'L0_attn_lambda_k1': 8.0,
     'L0_attn_lambda_q2': 64.0,
     'L0_attn_lambda_k2': 64.0,
     'L0_xattn_W_q': 6.918,
     'L0_xattn_W_k': 6.966,
     'L1_ffn_router_w': 8.0,
     'L1_ffn_gate_up_proj': 8.0,
     'L1_ffn_down_proj': 8.0,
     'L1_ffn_shared_gate_w': 8.0,
     'L1_ffn_shared_up_w': 8.0,
     'L1_ffn_shared_down_w': 8.0,
     'L1_ffn_shared_expert_gate_w': 8.0}
    for name, (base, spread) in spreads.items():
        noise = np.random.default_rng([zlib.crc32(name.encode()), seed]).standard_normal(out[name].shape)
        drawn = base * np.exp(spread * noise) if base else spread * noise
        out[name] = jnp.asarray(drawn.astype(out[name].dtype))
    for name, factor in factors.items():
        out[name] = (out[name] * factor).astype(out[name].dtype)
    return out
```

```python
from contextlib import ExitStack

import numpy as np

import concourse.bass as bass
from concourse import mybir

F32 = mybir.dt.float32
BF16 = mybir.dt.bfloat16
U8 = mybir.dt.uint8
ALU = mybir.AluOpType
ACT = mybir.ActivationFunctionType
AX_X = mybir.AxisListType.X

P = 128
NB = 8
D = 256
KC = D // P
NH = 16
HD = D // NH
EPS = 1e-5
NEG = -1e30
LAT = 64
RD = 8
E0, E1 = 8, 65
BLK = 768
OUT0 = 0.8

C_ID, C_TRI, C_NEG, C_COS, C_SIN, C_MASK, C_SEL, C_R = 0, 128, 256, 384, 512, 640, 644, 646
C_END = 646 + 16

WEIGHTS = {
    "w0_qk": KC * 512, "w0_v": KC * D, "w0_o": KC * D,
    "wx_fc": KC * D, "wx_q": KC * D, "wx_k": KC * D, "wx_v": KC * D,
    "wm_lat": KC * P, "wm_kx": KC * D, "wm_kr": KC * D, "wm_up": 3 * D, "wm_qr": D, "wm_o": KC * D,
    "w_rt0": KC * E0,
    "w1_qk": KC * 512, "w1_v": KC * D, "w1_o": KC * D, "w_rt1": KC * E1,
    "cols": 16,
}
ROWS = {"lam": 4 * D, "bv": D, "rb": E0, "gb": 2 * HD}


class Phase:
    total = {}

    def __init__(self, name, fires, turns=NB):
        self.name, self.fires = name, fires
        self.base = dict(Phase.total)
        for s, n in fires.items():
            Phase.total[s] = Phase.total.get(s, 0) + n * turns


def build(nc, t_in, out):
    Phase.total = {}
    common = {"xcur": 1, "xt_ps": 1, "xt_sb": 1}
    attn = dict(common, qk_ps=1, v_ps=1, va_sb=1, mv_sb=1, s_ps=2, o_ps=1, rec=1, o_sb=1,
                z_sb=1)
    norm = dict(bst=1, bag=1, bve=1, bpw=1, x_out=1)
    soft = dict(attn, mx=2, sub=2, exp=2, pt_ps=4, pt_a=2, pt_d=2)
    proj = dict(ot_ps=1, ot_sb=1, pr_ps=1)
    ATTN0 = Phase("attn0", dict(soft, **norm, qk_a=1, **proj))
    XATTN0 = Phase("xattn0", dict(soft, **norm, qk_a=1, rf_ps=1, rf_sb=1, rn_ps=1, xbv=1, x_ref=1))
    MLA0 = Phase("mla0", dict(soft, rms_v=1, rms_e=1, rms_p=1, xc0=1, lat_ps=1, lat_sb=1, rope_a=1, rope_b=1, raw_p=1,
                              xh=1, **proj))
    ROUTE0 = Phase("route0", dict(common, rms_v=1, rms_e=1, rms_p=1, xc0=1, ht=1, lg_ps=1, lg_sb=1, lg_e=1, r1=1, r2=1, r3=1,
                                  r4=1, r5=1, r6=1, cb=1, cbt_ps=1, cbt_sb=1))
    MOE0 = Phase("moe0", dict(z_sb=1, bst=1, bag=1, bve=1, bpw=1, x_out=1))
    ATTN1 = Phase("attn1", dict(attn, **norm, fm_g=1, fm_b=1, fm_s=1, fm_c=1, fm_q=1, fm_v=1, fm_e=1, fm_p=1, fm_y=1, yt_ps=1,
                                qk_a=1, sub=2, exp=2, ze=1, **proj))
    XATTN1 = Phase("xattn1", dict(common, s_ps=1, mk_a=1, mk_b=1, mxr=1, mx=1, exp=1, pt_ps=1, pt_a=1, pr_ps=1, rec=1, rv=1,
                                  z_sb=1, bst=1, bag=1, bve=1, bpw=1, x_out=1))
    ROUTE1 = Phase("route1", dict(common, ht=1, lg_ps=1, lg_sb=1, lg_e=1, r1=1, r2=1, r3=1, r4=1, r5=1, r6=1, r7=1,
                                  cb=1, cbt_ps=1, cbt_sb=1))
    MOE1 = Phase("moe1", dict(z_sb=1, bst=1, bag=1, bve=1, bpw=1, x_out=1))

    ctx = ExitStack()
    with ctx:
        def sb(name, shape, dt=F32):
            return ctx.enter_context(nc.sbuf_tensor(name, shape, dt))

        def sem(name):
            return ctx.enter_context(nc.semaphore(name))

        X = sb("X", [P, NB, D])
        H = sb("H", [P, NB, D])
        CTX = sb("CTX", [P, NB, D])
        CTXT = sb("CTXT", [P, KC, NB, P])
        HT = sb("HT", [P, KC, NB, P])
        VA = sb("VA", [P, NB, NH, HD + 1])
        W = {n: sb(n, [P, c]) for n, c in WEIGHTS.items()}
        R = {n: sb("row_" + n, [P, c]) for n, c in ROWS.items()}
        CONST = sb("CONST", [P, C_END])
        MKU = sb("MKU", [P, NB * P // 4], mybir.dt.int32)
        MK = sb("MK", [P, NB, P])
        MKN = sb("MKN", [P, NB, P])
        VALID = sb("VALID", [P, NB])
        identb = sb("identb", [P, P], BF16)
        negb = sb("negb", [P, P], BF16)
        zerob = sb("zerob", [P, 512], BF16)
        neghalf = sb("neghalf", [P, 32])
        lam = sb("lam", [P, 8])
        qscale = sb("qscale", [P, 1])
        junk = sb("junk", [P, D])
        xcur = sb("xcur", [P, D])
        xraw = sb("xraw", [P, D])
        xT = sb("xT", [P, KC, P])
        rT = sb("rT", [P, 2 * KC, P])
        latT = sb("latT", [P, P])
        stat = sb("stat", [P, KC, P])
        raw = sb("raw", [P, KC, P])
        rope1 = sb("rope1", [P, 2 * KC, P])
        rope2 = sb("rope2", [P, 2 * KC, P])
        mv = sb("mv", [P, KC, 4, P])
        SM = sb("SM", [P, NH, P])
        PR = sb("PR", [P, NH, P])
        PT = sb("PT", [P, NH, P])
        mx = sb("mx", [P, NH])
        rec = sb("rec", [P, NH])
        O = sb("O", [P, D])
        OT = sb("OT", [P, KC, P])
        z = sb("z", [P, D])
        bst = sb("bst", [P, 6])
        bag = sb("bag", [P, 2])
        bve = sb("bve", [P, 1])
        rstd = sb("rstd", [P, 1])
        rms = sb("rms", [P, 4])
        fm1 = sb("fm1", [P, 2 * NH, HD])
        fm2 = sb("fm2", [P, 2 * NH, HD])
        fms = sb("fms", [P, 4, 2 * NH])
        lg = sb("lg", [P, E1])
        p16 = sb("p16", [P, 16])
        mr8 = sb("mr8", [P, 8])
        m8 = sb("m8", [P, 8])
        rep = sb("rep", [P, 64])
        sel = sb("sel", [P, 64])
        ex = sb("ex", [P, E1])
        es = sb("es", [P, 64])
        rsm = sb("rsm", [P, 8])
        cbs = sb("cbs", [P, E1])
        cbT = sb("cbT", [E1, NB, P])
        blk = [sb(f"blk{k}", [P, BLK]) for k in range(2)]
        wb = [sb(f"wb{k}", [P, NB * P]) for k in range(2)]
        sil = [sb(f"sil{k}", [P, 512]) for k in range(2)]
        hid0 = [sb(f"hid0{k}", [P, 512]) for k in range(2)]
        hid = [sb(f"hid{k}", [P, 512]) for k in range(2)]

        S = ctx.enter_context(nc.psum_tensor("S", [P, 2048], F32))
        T = [ctx.enter_context(nc.psum_tensor(f"T{k}", [P, 512], F32)) for k in range(2)]
        M = ctx.enter_context(nc.psum_tensor("M", [P, 512], F32))
        OB = ctx.enter_context(nc.psum_tensor("OB", [P, 512], F32))

        N_INIT = 19
        ident = CONST[:, C_ID:C_ID + P]
        tri = CONST[:, C_TRI:C_TRI + P]
        names = sorted(Phase.total)
        sems = {n: sem("s_" + n) for n in names}
        s_x0, s_x1, s_ctxt, s_ctx, s_cst, s_row = sem("s_x0"), sem("s_x1"), sem("s_ctxt"), sem("s_ctx"), sem("s_cst"), sem("s_row")
        s_w = {n: sem("s_w_" + n) for n in ("a", "b", "c", "d", "e")}
        s_mk, s_mk2 = sem("s_mk"), sem("s_mk2")
        s_init, s_pinit, s_lam, s_lame = sem("s_init"), sem("s_pinit"), sem("s_lam"), sem("s_lame")
        s_cbd, s_out = [sem("s_cbd0"), sem("s_cbd1")], sem("s_out")
        s_blk = [sem("s_blk0"), sem("s_blk1")]
        s_gu, s_sil, s_h0, s_hid, s_dn = sem("s_gu"), sem("s_sil"), sem("s_h0"), sem("s_hid"), sem("s_dn")

        WGROUP = {"w0_qk": "a", "w0_v": "a", "w0_o": "a", "wx_fc": "b", "wx_q": "b", "wx_k": "b", "wx_v": "b",
                  "cols": "b", "wm_lat": "c", "wm_kx": "c", "wm_kr": "c", "wm_up": "c", "wm_qr": "c", "wm_o": "c",
                  "w_rt0": "d", "w1_qk": "e", "w1_v": "e", "w1_o": "e", "w_rt1": "e"}
        NW = {g: 16 * sum(1 for v in WGROUP.values() if v == g) for g in "abcde"}

        def wait(eng, ph, s, i, k=0):
            per = ph.fires.get(s, 0)
            if per == 0 and (k or not isinstance(i, int)):
                return
            v = ph.base.get(s, 0) + per * i + k
            if isinstance(v, int) and v <= 0:
                return
            eng.wait_ge(sems[s], v)

        s_apart = {"dve": sem("s_apart_dve"), "pool": sem("s_apart_pool")}

        def apart(eng, who):
            eng.sem_inc(s_apart[who], 1)

        def at(buf, i):
            return buf[:, i, :] if isinstance(i, int) else buf[:, bass.ds(i, 1), :]

        def wv(n, k=KC):
            return W[n][:, :].rearrange("p (k n) -> p k n", k=k)

        def col(c):
            return W["cols"][:, c:c + 1]

        XT_SCALE = {"mla0": 0, "route0": 2}
        QB, KB, FB = 4, 6, 8

        D0 = nc.dram_tensor("route0_w", (E0, NB * P), F32, kind="Internal").ap()
        D1 = nc.dram_tensor("route1_w", (E1, NB * P), F32, kind="Internal").ap()

        block = ctx.enter_context(nc.Block())

        MOES = {
            "moe0": dict(ph=MOE0, prev=ROUTE0, w=t_in["blocks0"], dram=D0, cols=E0, n=8, scale=0.125, u0=0, dmas=2),
            "moe1": dict(ph=MOE1, prev=ROUTE1, w=t_in["blocks1"], dram=D1, cols=E1, n=33, scale=1.0, u0=16, dmas=3),
        }
        BEFORE = {"moe0": 0, "moe1": MOES["moe0"]["n"] // 2 * MOES["moe0"]["dmas"]}

        def landed(eng, name, k):
            m = MOES[name]
            return (BEFORE[name] + m["dmas"] * k) * 16 if isinstance(k, int) else k * (16 * m["dmas"]) + 16 * BEFORE[name]

        @block.sync
        def _(sp):
            sp.dma_start(CONST[:, :], t_in["consts"]).then_inc(s_cst, 16)
            sp.dma_start(X[:, 0:2, :], t_in["x"].rearrange("b t d -> t b d")[:, 0:2, :]).then_inc(s_x0, 16)

            def weights(g):
                for n, gg in WGROUP.items():
                    if gg == g:
                        sp.dma_start(W[n][:, :], t_in[n]).then_inc(s_w[g], 16)
            weights("a")
            for n in ROWS:
                sp.dma_start(R[n][:, :], t_in["row_" + n].to_broadcast([P, ROWS[n]])).then_inc(s_row, 16)
            sp.dma_start(X[:, 2:NB, :], t_in["x"].rearrange("b t d -> t b d")[:, 2:NB, :]).then_inc(s_x1, 16)
            weights("b")
            sp.dma_start(CTXT[:, :, :, :].rearrange("p k b t -> p k (b t)"),
                         t_in["ctxT"].rearrange("(k p) n -> p k n", p=P)).then_inc(s_ctxt, 16)
            weights("c")
            weights("d")
            weights("e")
            sp.dma_start(CTX[:, :, :], t_in["ctx"].rearrange("b t d -> t b d")).then_inc(s_ctx, 16)
            sp.dma_start(MKU[:, :], t_in["mask"].to_broadcast([P, NB * P // 4])).then_inc(s_mk, 16)

            def moe(name, which):
                m = MOES[name]
                dr, u0, n_blocks = m["dram"], m["u0"], m["n"]

                def load_w(n, slot):
                    src = m["w"][n] if isinstance(n, int) else m["w"][bass.ds(n, 1), :, :]
                    sp.dma_start(blk[slot][:, :], src).then_inc(s_blk[slot], 16)

                def load_b(n, slot):
                    def spread(e, p0, np_):
                        row = dr[e:e + 1, :] if isinstance(e, int) else dr[bass.ds(e, 1), :]
                        sp.dma_start(wb[slot][p0:p0 + np_, :], row.to_broadcast([np_, NB * P])).then_inc(s_blk[slot], 16)
                    first = isinstance(n, int) and n == 0
                    if which == 0:
                        spread(E0 - 1 if first else n - 1, 0, P)
                    else:
                        spread(E1 - 1 if first else n * 2 - 2, 0, 64)
                        spread(E1 - 1 if first else n * 2 - 1, 64, 64)

                if which == 1:
                    sp.wait_ge(s_dn, u0)
                load_w(0, 0)
                load_w(1, 1)
                with sp.Fori(0, NB) as i:
                    wait(sp, m["prev"], "cbt_sb", i, 1)
                    sp.dma_start(dr[:, bass.ds(i * P, P)], cbT[0:m["cols"], bass.ds(i, 1), :]).then_inc(s_cbd[which], 16)
                sp.wait_ge(s_cbd[which], 16 * NB)
                load_b(0, 0)
                load_b(1, 1)
                with sp.Fori(0, (n_blocks - 2) // 2) as j:
                    for k in range(2):
                        sp.wait_ge(s_dn, j * 4 + (u0 + 2 + 2 * k))
                        load_w(j * 2 + (2 + k), k)
                        load_b(j * 2 + (2 + k), k)
                if n_blocks % 2:
                    sp.wait_ge(s_dn, u0 + 2 * (n_blocks - 2))
                    load_w(n_blocks - 1, 0)
                    load_b(n_blocks - 1, 0)

            moe("moe0", 0)
            moe("moe1", 1)
            with sp.Fori(0, NB) as i:
                wait(sp, MOE1, "x_out", i, 1)
                sp.dma_start(out.rearrange("b t d -> t b d")[:, bass.ds(i, 1), :], X[:, bass.ds(i, 1), :]).then_inc(s_out, 16)
            sp.wait_ge(s_out, 16 * NB)

        def walk(eng, a, b, c, d, experts=None, last=None):
            for name, chain in (("moe0", [ATTN0, XATTN0, MLA0, ROUTE0]), ("moe1", [ATTN1, XATTN1, ROUTE1])):
                prev = None
                for ph in chain:
                    a(ph, 0)
                    if prev is not None:
                        c(prev, NB - 1)
                        d(prev, NB - 1)
                    b(ph, 0)
                    first = 2 if ph in (ATTN0, ROUTE0) else 1
                    if first == 2:
                        a(ph, 1)
                        c(ph, 0)
                        d(ph, 0)
                        b(ph, 1)
                    with eng.Fori(first, NB) as i:
                        a(ph, i)
                        c(ph, i - 1)
                        d(ph, i - 1)
                        b(ph, i)
                    prev = ph
                c(prev, NB - 1)
                d(prev, NB - 1)
                m = MOES[name]
                if experts is not None:
                    experts(m, name)
                if last is not None:
                    with eng.Fori(0, NB) as i:
                        last(m["ph"], i)

        @block.gpsimd
        def _(pool):
            pool.memset(neghalf[:, :], -0.5).then_inc(s_pinit, 1)
            pool.memset(VA[:, :, :, HD:HD + 1], 1.0).then_inc(s_pinit, 1)
            for j in range(9):
                pool.memset(p16[:, 7 + j:8 + j], -1.0 - j).then_inc(s_pinit, 1)
            for j in range(6):
                pool.memset(mr8[:, 2 + j:3 + j], -2.0 - j).then_inc(s_pinit, 1)
            pool.memset(cbs[:, E0 - 1:E0], 1.0).then_inc(s_pinit, 1)
            pool.memset(zerob[:, :], 0.0).then_inc(s_pinit, 1)
            pool.wait_ge(s_cst, 16)
            pool.wait_ge(s_pinit, N_INIT)

            def power(ph, i, s_in, s_out_, out_, in_, n=1):
                wait(pool, ph, s_in, i, 1)
                pool.tensor_tensor(out_, in_, neghalf[:, 0:n], ALU.pow).then_inc(sems[s_out_], 1)

            def a(ph, i):
                src = H if ph is ROUTE0 else X
                if ph is ATTN0:
                    pool.wait_ge(s_x0, 16)
                    if not isinstance(i, int):
                        pool.wait_ge(s_x1, 16)
                wait_src(ph, i)
                wait(pool, ph, "xt_ps", i)
                if "rms_v" in ph.fires:
                    wait(pool, ph, "rms_v", i)
                    wait(pool, ph, "xcur", i)
                    pool.tensor_copy(xraw[:, :], at(src, i)).then_inc(sems["xc0"], 1)
                    power(ph, i, "rms_e", "rms_p", rms[:, 2:3], rms[:, 1:2])
                    wait(pool, ph, "rms_p", i, 1)
                    apart(pool, "pool")
                    pool.tensor_scalar(xcur[:, :], xraw[:, :], rms[:, 2:3], None, ALU.mult).then_inc(sems["xcur"], 1)
                else:
                    pool.tensor_copy(xcur[:, :], at(src, i)).then_inc(sems["xcur"], 1)
                if ph in (ROUTE0, ROUTE1):
                    wait(pool, ph, "xt_sb", i, 1)
                    if isinstance(i, int):
                        pool.tensor_copy(HT[:, :, i, :], xT[:, :, :]).then_inc(sems["ht"], 1)
                    else:
                        pool.tensor_copy(HT[:, :, bass.ds(i, 1), :], xT[:, :, :]).then_inc(sems["ht"], 1)
                    return
                if ph is XATTN1:
                    return
                if ph is XATTN0:
                    if isinstance(i, int) and i == 0:
                        pool.wait_ge(s_row, 16 * len(ROWS))
                    wait(pool, ph, "xcur", i, 1)
                    apart(pool, "pool")
                    pool.tensor_tensor(at(X, i), at(X, i), R["bv"][:, :], ALU.add).then_inc(sems["xbv"], 1)
                if ph is MLA0:
                    wait(pool, ph, "rope_b", i, 1)
                    wait(pool, ph, "s_ps", i)
                    wait(pool, ph, "mv_sb", i)
                    pool.tensor_tensor(stat[:, :, :], rope1[:, 0:KC, :], rope2[:, 0:KC, :], ALU.add)
                    pool.tensor_tensor(raw[:, :, :], rope1[:, KC:2 * KC, :], rope2[:, KC:2 * KC, :], ALU.add).then_inc(sems["raw_p"], 1)
                    wait(pool, ph, "raw_p", i, 1)
                elif ph is ATTN1:
                    power(ph, i, "fm_e", "fm_p", fms[:, 3, :], fms[:, 2, :], 2 * NH)
                    return
                else:
                    wait(pool, ph, "qk_a", i, 1)
                masked(ph, i)

            def wait_src(ph, i):
                before = {"xattn0": ATTN0, "mla0": XATTN0, "attn1": MOE0, "xattn1": ATTN1, "route1": XATTN1}
                if ph.name in before:
                    wait(pool, before[ph.name], "x_out", i, 1)
                if ph is ROUTE0:
                    wait(pool, MLA0, "xh", i, 1)

            def d(ph, i):
                if "bve" in ph.fires:
                    power(ph, i, "bve", "bpw", rstd[:, :], bve[:, :])

            def masked(ph, i):
                wait(pool, ph, "s_ps", i)
                pool.tensor_tensor(
                    mv[:, :, :, :],
                    raw[:, :, :].unsqueeze(2).to_broadcast([P, KC, 4, P]),
                    CONST[:, C_MASK:C_MASK + 4].unsqueeze(1).unsqueeze(3).to_broadcast([P, KC, 4, P]),
                    ALU.mult).then_inc(sems["mv_sb"], 1)

            def b(ph, i):
                if ph is ATTN1:
                    wait(pool, ph, "qk_a", i, 1)
                    masked(ph, i)

            def c(ph, i):
                pass

            walk(pool, a, b, c, d, last=d)

        @block.scalar
        def _(act):
            act.wait_ge(s_lam, 2)
            act.activation(lam[:, 2:4], lam[:, 0:2], ACT.Exp).then_inc(s_lame, 1)
            act.wait_ge(s_cst, 16)

            def a(ph, i):
                first = isinstance(i, int) and i == 0
                if first and ph is XATTN0:
                    act.wait_ge(s_w["b"], NW["b"])
                wait(act, ph, "xt_ps", i, 1)
                src = M[:, 0:D].rearrange("p (k t) -> p k t", k=KC)
                if ph.name in XT_SCALE:
                    if ph is ROUTE0:
                        wait(act, ph, "ht", i)
                    for k in range(KC):
                        c_ = XT_SCALE[ph.name] + k
                        ins = act.activation(xT[:, k, :], src[:, k, :], ACT.Copy, scale=col(c_))
                    ins.then_inc(sems["xt_sb"], 1)
                else:
                    wait(act, ph, "ht", i)
                    act.activation(xT[:, :, :], src, ACT.Copy).then_inc(sems["xt_sb"], 1)
                t0 = T[0][:, :].rearrange("p (k t) -> p k t", t=P)
                t1 = T[1][:, :].rearrange("p (k t) -> p k t", t=P)
                if ph in (ROUTE0, ROUTE1):
                    wait(act, ph, "lg_sb", i, 1)
                    if ph is ROUTE0:
                        act.activation(ex[:, 0:E0], lg[:, 0:E0], ACT.Exp, scale=-1.0).then_inc(sems["lg_e"], 1)
                    else:
                        wait(act, ph, "r2", i, 1)
                        act.activation(ex[:, 0:64], lg[:, 0:64], ACT.Exp, bias=rsm[:, 0:1])
                        act.activation(ex[:, 64:65], lg[:, 64:65], ACT.Exp, scale=-1.0).then_inc(sems["lg_e"], 1)
                    return
                if ph is XATTN1:
                    return
                if ph is XATTN0:
                    wait(act, ph, "rf_ps", i, 1)
                    for k in range(2 * KC):
                        ins = act.activation(rT[:, k, :], t1[:, k, :], ACT.Relu, bias=col(FB + k % KC))
                    ins.then_inc(sems["rf_sb"], 1)
                if ph is MLA0:
                    wait(act, ph, "lat_ps", i, 1)
                    act.activation(latT[:, :], M[:, 256:256 + P], ACT.Copy).then_inc(sems["lat_sb"], 1)
                if ph in (ATTN0, XATTN0):
                    wait(act, ph, "qk_ps", i, 1)
                    wait(act, ph, "mv_sb", i)
                    wait(act, ph, "s_ps", i)
                    if ph is ATTN0:
                        if first:
                            act.wait_ge(s_lam, 4)
                        act.activation(raw[:, :, :], t0[:, KC:2 * KC, :], ACT.Copy)
                        act.activation(stat[:, :, :], t0[:, 0:KC, :], ACT.Copy, scale=qscale[:, 0:1]).then_inc(sems["qk_a"], 1)
                    else:
                        for k in range(KC):
                            act.activation(raw[:, k, :], t0[:, KC + k, :], ACT.Identity, bias=col(KB + k))
                        for k in range(KC):
                            ins = act.activation(stat[:, k, :], t0[:, k, :], ACT.Identity, bias=col(QB + k))
                        ins.then_inc(sems["qk_a"], 1)
                if ph is ATTN1:
                    wait(act, ph, "fm_c", i, 1)
                    act.activation(fm2[:, :, :], fm1[:, :, :], ACT.Square).then_inc(sems["fm_q"], 1)
                wait(act, ph, "v_ps", i, 1)
                dst = VA[:, i, :, 0:HD] if isinstance(i, int) else VA[:, bass.ds(i, 1), :, 0:HD]
                if first:
                    act.wait_ge(s_pinit, N_INIT)
                act.activation(dst, M[:, 256:512].rearrange("p (h d) -> p h d", h=NH), ACT.Copy).then_inc(sems["va_sb"], 1)

            def b(ph, i):
                if ph in (ROUTE0, ROUTE1):
                    return
                if ph is XATTN1:
                    wait(act, ph, "mx", i, 1)
                    wait(act, ph, "pt_ps", i)
                    act.activation(PR[:, 0, :], SM[:, 1, :], ACT.Exp, scale=1.0 / 16, accum_out=rec[:, 0:1]).then_inc(sems["exp"], 1)
                    return
                if ph is ATTN1:
                    t1 = T[1][:, :].rearrange("p (k t) -> p k t", t=P)
                    wait(act, ph, "yt_ps", i, 1)
                    wait(act, ph, "mv_sb", i)
                    wait(act, ph, "s_ps", i)
                    act.activation(raw[:, :, :], t1[:, 0:KC, :], ACT.Copy)
                    act.activation(stat[:, :, :], t1[:, KC:2 * KC, :], ACT.Copy).then_inc(sems["qk_a"], 1)
                for h in range(2):
                    wait(act, ph, "sub", i, h + 1)
                    hs = slice(8 * h, 8 * h + 8)
                    if ph is ATTN1:
                        wait(act, ph, "o_ps", i)
                        act.activation(PT[:, hs, :], SM[:, hs, :], ACT.Square, scale=0.25).then_inc(sems["exp"], 1)
                    else:
                        wait(act, ph, "pt_ps", i)
                        act.activation(PR[:, hs, :], SM[:, hs, :], ACT.Exp,
                                       scale=1.0 if ph is ATTN0 else 0.25).then_inc(sems["exp"], 1)

            def c(ph, i):
                if ph in (ROUTE0, ROUTE1):
                    n = E0 if ph is ROUTE0 else E1
                    wait(act, ph, "cbt_ps", i, 1)
                    dst = cbT[0:n, i, :] if isinstance(i, int) else cbT[0:n, bass.ds(i, 1), :]
                    act.activation(dst, OB[0:n, 0:P], ACT.Copy).then_inc(sems["cbt_sb"], 1)
                    return
                if ph is XATTN1:
                    wait(act, ph, "pt_ps", i, 1)
                    act.activation(PT[:, 0, :], T[0][:, 0:P], ACT.Copy).then_inc(sems["pt_a"], 1)
                    return
                if ph is ATTN1:
                    return
                for q in (0, 2):
                    wait(act, ph, "pt_ps", i, q + 1)
                    act.activation(PT[:, 4 * q:4 * q + 4, :], T[0][:, :], ACT.Copy).then_inc(sems["pt_a"], 1)

            def d(ph, i):
                if "ot_ps" in ph.fires:
                    wait(act, ph, "ot_ps", i, 1)
                    act.activation(OT[:, :, :], M[:, 0:D], ACT.Copy).then_inc(sems["ot_sb"], 1)

            def experts(m, name):
                u0 = m["u0"]

                def unit(half, u):
                    act.wait_ge(s_gu, u + 1)
                    if not isinstance(u, int) or u >= 2:
                        act.wait_ge(s_h0, u - 1)
                    act.activation(sil[half][:, :], T[half][:, :], ACT.Silu).then_inc(s_sil, 1)

                unit(0, u0)
                unit(1, u0 + 1)
                with act.Fori(0, (m["n"] - 1) // 2) as j:
                    for k in range(4):
                        unit(k % 2, j * 4 + (u0 + 2 + k))
                if m["n"] % 2 == 0:
                    u = u0 + 2 * (m["n"] - 1)
                    unit(0, u)
                    unit(1, u + 1)

            walk(act, a, b, c, d, experts)

        @block.vector
        def _(dve):
            dve.wait_ge(s_cst, 16)
            dve.tensor_copy(identb[:, :], ident).then_inc(s_init, 1)
            dve.tensor_copy(negb[:, :], CONST[:, C_NEG:C_NEG + P]).then_inc(s_init, 1)
            dve.wait_ge(s_row, 16 * len(ROWS))
            lr = R["lam"][:, :].rearrange("p (a n) -> p a n", a=4)
            for j in range(2):
                if j:
                    dve.wait_ge(s_lam, 1)
                dve.tensor_tensor_reduce(out=junk[:, :], in0=lr[:, 2 * j, :], in1=lr[:, 2 * j + 1, :], scale=1.0,
                                         scalar=0.0, op0=ALU.mult, op1=ALU.add,
                                         accum_out=lam[:, j:j + 1]).then_inc(s_lam, 1)
            dve.wait_ge(s_lame, 1)
            dve.tensor_tensor(lam[:, 4:5], lam[:, 2:3], lam[:, 3:4], ALU.subtract).then_inc(s_lam, 1)
            dve.wait_ge(s_lam, 3)
            c8 = float(8 ** -0.5)
            dve.tensor_scalar(lam[:, 5:6], lam[:, 4:5], 0.2, -c8, ALU.add, ALU.mult).then_inc(s_init, 1)
            dve.wait_ge(s_init, 3)
            dve.scalar_tensor_tensor(qscale[:, :], in0=CONST[:, C_SEL + 1:C_SEL + 2], scalar=lam[:, 5:6],
                                     in1=CONST[:, C_SEL:C_SEL + 1], op0=ALU.mult, op1=ALU.add).then_inc(s_lam, 1)

            def a(ph, i):
                first = isinstance(i, int) and i == 0
                if "rms_v" in ph.fires:
                    wait(dve, ph, "xc0", i, 1)
                    dve.tensor_tensor_reduce(out=junk[:, :], in0=xraw[:, :], in1=xraw[:, :], scale=1.0, scalar=0.0,
                                             op0=ALU.mult, op1=ALU.add, accum_out=rms[:, 0:1]).then_inc(sems["rms_v"], 1)
                    wait(dve, ph, "rms_v", i, 1)
                    dve.tensor_scalar(rms[:, 1:2], rms[:, 0:1], 1.0 / D, EPS, ALU.mult, ALU.add).then_inc(sems["rms_e"], 1)
                if ph is XATTN0:
                    wait(dve, ph, "rn_ps", i, 1)
                    wait(dve, ph, "xbv", i, 1)
                    dve.tensor_tensor(at(X, i), M[:, 0:D], at(X, i), ALU.add).then_inc(sems["x_ref"], 1)
                if ph is MLA0:
                    wait(dve, ph, "qk_ps", i, 1)
                    wait(dve, ph, "raw_p", i)
                    for s, tb, cc, dst in ((0, T[0], C_COS, rope1), (1, T[1], C_SIN, rope2)):
                        dve.tensor_tensor(dst[:, :, :], tb[:, :].rearrange("p (k t) -> p k t", t=P),
                                          CONST[:, cc:cc + P].unsqueeze(1).to_broadcast([P, 2 * KC, P]),
                                          ALU.mult).then_inc(sems["rope_a" if s == 0 else "rope_b"], 1)
                if ph is ATTN1:
                    feature_map(ph, i)
                if ph is ROUTE0:
                    route0(ph, i)
                if ph is ROUTE1:
                    route1(ph, i)

            def feature_map(ph, i):
                src = T[0][:, :].rearrange("p (h d) -> p h d", d=HD)

                def g(c_):
                    return R["gb"][:, c_ * HD:c_ * HD + HD].unsqueeze(1).to_broadcast([P, 2 * NH, HD])

                def per_head(k):
                    return fms[:, k, :].unsqueeze(2).to_broadcast([P, 2 * NH, HD])
                wait(dve, ph, "qk_ps", i, 1)
                wait(dve, ph, "fm_q", i)
                wait(dve, ph, "yt_ps", i)
                dve.tensor_tensor(fm1[:, :, :], src, g(0), ALU.mult).then_inc(sems["fm_g"], 1)
                wait(dve, ph, "fm_g", i, 1)
                dve.tensor_tensor(fm2[:, :, :], fm1[:, :, :], g(1), ALU.add).then_inc(sems["fm_b"], 1)
                wait(dve, ph, "fm_b", i, 1)
                dve.tensor_reduce(fms[:, 0, :], fm2[:, :, :], AX_X, ALU.add).then_inc(sems["fm_s"], 1)
                wait(dve, ph, "fm_s", i, 1)
                dve.scalar_tensor_tensor(fm1[:, :, :], in0=per_head(0), scalar=-1.0 / HD, in1=fm2[:, :, :],
                                         op0=ALU.mult, op1=ALU.add).then_inc(sems["fm_c"], 1)
                wait(dve, ph, "fm_q", i, 1)
                dve.tensor_reduce(fms[:, 1, :], fm2[:, :, :], AX_X, ALU.add).then_inc(sems["fm_v"], 1)
                wait(dve, ph, "fm_v", i, 1)
                dve.tensor_scalar(fms[:, 2, :], fms[:, 1, :], 1.0 / HD, EPS, ALU.mult, ALU.add).then_inc(sems["fm_e"], 1)
                wait(dve, ph, "fm_p", i, 1)
                dve.tensor_tensor(fm1[:, :, :], fm1[:, :, :], per_head(3), ALU.mult).then_inc(sems["fm_y"], 1)

            def route0(ph, i):
                if isinstance(i, int):
                    dve.wait_ge(s_pinit, N_INIT)
                wait(dve, ph, "lg_ps", i, 1)
                dve.tensor_tensor(lg[:, 0:E0], M[:, 256:256 + E0], R["rb"][:, :], ALU.add).then_inc(sems["lg_sb"], 1)
                wait(dve, ph, "lg_e", i, 1)
                dve.tensor_scalar(es[:, 0:7], ex[:, 0:7], 1.0, None, ALU.add).then_inc(sems["r1"], 1)
                wait(dve, ph, "r1", i, 1)
                dve.reciprocal(p16[:, 0:7], es[:, 0:7]).then_inc(sems["r2"], 1)
                wait(dve, ph, "r2", i, 1)
                apart(dve, "dve")
                dve.max(m8[:, :], p16[:, :]).then_inc(sems["r3"], 1)
                wait(dve, ph, "r3", i, 1)
                dve.tensor_copy(mr8[:, 0:2], m8[:, 0:2])
                dve.tensor_tensor(rsm[:, 1:2], m8[:, 0:1], m8[:, 1:2], ALU.add).then_inc(sems["r4"], 1)
                wait(dve, ph, "r4", i, 1)
                apart(dve, "dve")
                dve.match_replace(rep[:, 0:16], mr8[:, :], p16[:, :], 0.0)
                dve.reciprocal(rsm[:, 2:3], rsm[:, 1:2]).then_inc(sems["r5"], 1)
                wait(dve, ph, "r5", i, 1)
                dve.tensor_tensor(sel[:, 0:E0], p16[:, 0:E0], rep[:, 0:E0], ALU.subtract).then_inc(sems["r6"], 1)
                wait(dve, ph, "r6", i, 1)
                wait(dve, ph, "cbt_ps", i)
                dve.tensor_scalar(cbs[:, 0:E0 - 1], sel[:, 0:E0 - 1], rsm[:, 2:3], None, ALU.mult).then_inc(sems["cb"], 1)

            def route1(ph, i):
                wait(dve, ph, "lg_ps", i, 1)
                dve.tensor_copy(lg[:, :], M[:, 256:256 + E1]).then_inc(sems["lg_sb"], 1)
                wait(dve, ph, "lg_sb", i, 1)
                apart(dve, "dve")
                dve.max(m8[:, :], lg[:, 0:64]).then_inc(sems["r1"], 1)
                wait(dve, ph, "r1", i, 1)
                dve.tensor_scalar(rsm[:, 0:1], m8[:, 0:1], -1.0, None, ALU.mult).then_inc(sems["r2"], 1)
                dve.match_replace(rep[:, :], m8[:, :], lg[:, 0:64], -3e38).then_inc(sems["r3"], 1)
                wait(dve, ph, "r3", i, 1)
                dve.tensor_tensor(sel[:, :], lg[:, 0:64], rep[:, :], ALU.not_equal).then_inc(sems["r4"], 1)
                wait(dve, ph, "r4", i, 1)
                wait(dve, ph, "lg_e", i, 1)
                dve.tensor_tensor_reduce(out=es[:, :], in0=ex[:, 0:64], in1=sel[:, :], scale=1.0, scalar=0.0,
                                         op0=ALU.mult, op1=ALU.add, accum_out=rsm[:, 1:2])
                dve.tensor_scalar(rsm[:, 3:4], ex[:, 64:65], 1.0, None, ALU.add).then_inc(sems["r5"], 1)
                wait(dve, ph, "r5", i, 1)
                dve.reciprocal(rsm[:, 2:3], rsm[:, 1:2]).then_inc(sems["r6"], 1)
                wait(dve, ph, "r6", i, 1)
                wait(dve, ph, "cbt_ps", i)
                dve.reciprocal(cbs[:, 64:65], rsm[:, 3:4]).then_inc(sems["r7"], 1)
                dve.tensor_scalar(cbs[:, 0:64], es[:, :], rsm[:, 2:3], None, ALU.mult).then_inc(sems["cb"], 1)

            def b(ph, i):
                if ph in (ROUTE0, ROUTE1):
                    return
                if ph is XATTN1:
                    def row(m_):
                        return at(m_, i)
                    if isinstance(i, int) and i == 0:
                        dve.wait_ge(s_mk2, 1)
                    wait(dve, ph, "s_ps", i, 1)
                    wait(dve, ph, "exp", i)
                    dve.tensor_tensor(SM[:, 2, :], S[:, 0:P], row(MK), ALU.mult).then_inc(sems["mk_a"], 1)
                    wait(dve, ph, "mk_a", i, 1)
                    dve.tensor_tensor(SM[:, 3, :], SM[:, 2, :], row(MKN), ALU.add).then_inc(sems["mk_b"], 1)
                    wait(dve, ph, "mk_b", i, 1)
                    dve.tensor_reduce(mx[:, 0:1], SM[:, 3, :], AX_X, ALU.max).then_inc(sems["mxr"], 1)
                    wait(dve, ph, "mxr", i, 1)
                    dve.tensor_scalar(SM[:, 1, :], SM[:, 3, :], mx[:, 0:1], None, ALU.subtract).then_inc(sems["mx"], 1)
                    return
                for h in range(2):
                    hs = slice(8 * h, 8 * h + 8)
                    s_in = S[:, 1024 * h:1024 * h + 1024].rearrange("p (h t) -> p h t", h=8)
                    wait(dve, ph, "s_ps", i, h + 1)
                    if ph is ATTN1:
                        wait(dve, ph, "exp", i)
                        dve.tensor_tensor(SM[:, hs, :], s_in, tri.unsqueeze(1).to_broadcast([P, 8, P]),
                                          ALU.mult).then_inc(sems["sub"], 1)
                        continue
                    dve.tensor_reduce(mx[:, hs], s_in, AX_X, ALU.max).then_inc(sems["mx"], 1)
                    wait(dve, ph, "mx", i, h + 1)
                    wait(dve, ph, "exp", i)
                    dve.tensor_tensor(SM[:, hs, :], s_in, mx[:, hs].unsqueeze(2).to_broadcast([P, 8, P]),
                                      ALU.subtract).then_inc(sems["sub"], 1)

            def c(ph, i):
                if ph in (ROUTE0, ROUTE1, XATTN1):
                    return
                if ph is not ATTN1:
                    for q in (1, 3):
                        wait(dve, ph, "pt_ps", i, q + 1)
                        dve.tensor_copy(PT[:, 4 * q:4 * q + 4, :], T[1][:, :]).then_inc(sems["pt_d"], 1)
                ob = OB[:, 0:NH * (HD + 1)].rearrange("p (h d) -> p h d", h=NH)
                wait(dve, ph, "o_ps", i, 1)
                den = ob[:, :, HD:HD + 1]
                if ph is ATTN1:
                    dve.tensor_scalar(mx[:, :], den, EPS, None, ALU.add).then_inc(sems["ze"], 1)
                    wait(dve, ph, "ze", i, 1)
                    den = mx[:, :]
                dve.reciprocal(rec[:, :], den).then_inc(sems["rec"], 1)
                wait(dve, ph, "rec", i, 1)
                wait(dve, ph, "z_sb", i)
                dve.tensor_tensor(O[:, :].rearrange("p (h d) -> p h d", h=NH), ob[:, :, 0:HD],
                                  rec[:, :].unsqueeze(2).to_broadcast([P, NH, HD]), ALU.mult).then_inc(sems["o_sb"], 1)

            def layernorm(ph, i):
                wait(dve, ph, "z_sb", i, 1)
                dve.bn_stats(bst[:, :], z[:, :]).then_inc(sems["bst"], 1)
                wait(dve, ph, "bst", i, 1)
                apart(dve, "dve")
                dve.bn_aggr(bag[:, :], bst[:, :]).then_inc(sems["bag"], 1)
                wait(dve, ph, "bag", i, 1)
                dve.tensor_scalar(bve[:, :], bag[:, 1:2], EPS, None, ALU.add).then_inc(sems["bve"], 1)
                wait(dve, ph, "bpw", i, 1)
                dve.tensor_scalar(at(X, i), z[:, :], bag[:, 0:1], rstd[:, 0:1], ALU.subtract, ALU.mult).then_inc(sems["x_out"], 1)

            def d(ph, i):
                if ph in (ROUTE0, ROUTE1):
                    return
                wait(dve, ph, "x_out", i)
                if ph is XATTN0:
                    wait(dve, ph, "o_sb", i, 1)
                    dve.tensor_tensor(z[:, :], O[:, :], at(X, i), ALU.add).then_inc(sems["z_sb"], 1)
                elif ph is XATTN1:
                    wait(dve, ph, "pr_ps", i, 1)
                    dve.reciprocal(rec[:, 1:2], rec[:, 0:1]).then_inc(sems["rec"], 1)
                    wait(dve, ph, "rec", i, 1)
                    v = VALID[:, i:i + 1] if isinstance(i, int) else VALID[:, bass.ds(i, 1)]
                    dve.tensor_tensor(rec[:, 2:3], rec[:, 1:2], v, ALU.mult).then_inc(sems["rv"], 1)
                    wait(dve, ph, "rv", i, 1)
                    dve.scalar_tensor_tensor(z[:, :], in0=OB[:, 0:D], scalar=rec[:, 2:3], in1=at(X, i),
                                             op0=ALU.mult, op1=ALU.add).then_inc(sems["z_sb"], 1)
                elif ph is ATTN0:
                    wait(dve, ph, "pr_ps", i, 1)
                    dve.scalar_tensor_tensor(z[:, :], in0=OB[:, 0:D], scalar=OUT0, in1=at(X, i),
                                             op0=ALU.mult, op1=ALU.add).then_inc(sems["z_sb"], 1)
                elif ph is MLA0:
                    wait(dve, ph, "pr_ps", i, 1)
                    dve.tensor_tensor(at(H, i), OB[:, 0:D], at(X, i), ALU.add).then_inc(sems["z_sb"], 1)
                    wait(dve, ph, "z_sb", i, 1)
                    dve.tensor_tensor(at(X, i), at(H, i), at(X, i), ALU.add).then_inc(sems["xh"], 1)
                    return
                elif ph in (MOE0, MOE1):
                    dve.tensor_tensor(z[:, :], S[:, bass.ds(i * D, D)], at(X, i), ALU.add).then_inc(sems["z_sb"], 1)
                else:
                    wait(dve, ph, "pr_ps", i, 1)
                    dve.tensor_tensor(z[:, :], OB[:, 0:D], at(X, i), ALU.add).then_inc(sems["z_sb"], 1)
                layernorm(ph, i)

            def experts(m, name):
                u0 = m["u0"]
                ub = [M, OB]

                def unit(half, u, slot, k):
                    dve.wait_ge(s_sil, u + 1)
                    if not isinstance(u, int) or u >= 2:
                        dve.wait_ge(s_hid, u - 1)
                        dve.wait_ge(s_dn, u - 1)
                    dve.scalar_tensor_tensor(hid0[half][:, :], in0=ub[half][:, :], scalar=m["scale"],
                                             in1=sil[half][:, :], op0=ALU.mult, op1=ALU.mult).then_inc(s_h0, 1)
                    dve.wait_ge(s_blk[slot], landed(dve, name, k))
                    dve.wait_ge(s_h0, u + 1)
                    dve.tensor_tensor(hid[half][:, :], hid0[half][:, :], wb[slot][:, 512 * half:512 * half + 512],
                                      ALU.mult).then_inc(s_hid, 1)

                unit(0, u0, 0, 1)
                unit(1, u0 + 1, 0, 1)
                with dve.Fori(0, (m["n"] - 1) // 2) as j:
                    for k in range(4):
                        slot = 1 - k // 2
                        unit(k % 2, j * 4 + (u0 + 2 + k), slot, j + (1 if slot else 2))
                if m["n"] % 2 == 0:
                    u = u0 + 2 * (m["n"] - 1)
                    unit(0, u, 1, m["n"] // 2)
                    unit(1, u + 1, 1, m["n"] // 2)
                dve.wait_ge(s_dn, u0 + 2 * m["n"])
                if name == "moe0":
                    dve.wait_ge(s_mk, 16)
                    dve.tensor_copy(MK[:, :, :].rearrange("p b t -> p (b t)"), MKU[:, :].bitcast(U8)).then_inc(s_init, 1)
                    dve.wait_ge(s_init, 4)
                    dve.tensor_reduce(VALID[:, :], MK[:, :, :], AX_X, ALU.max)
                    dve.tensor_scalar(MKN[:, :, :], MK[:, :, :], -NEG, NEG, ALU.mult, ALU.add).then_inc(s_mk2, 1)

            walk(dve, a, b, c, d, experts, d)

        @block.tensor
        def _(pe):
            pe.wait_ge(s_cst, 16)

            def mm(out_, lhsT, rhs, start=True, stop=True, **kw):
                return pe.matmul(out_, lhsT, rhs, start=start, stop=stop, **kw)

            def over_k(out_, lhsT, rhs):
                for k in range(KC):
                    ins = mm(out_, lhsT(k), rhs(k), start=(k == 0), stop=(k == KC - 1))
                return ins

            def a(ph, i):
                first = isinstance(i, int) and i == 0
                wait(pe, ph, "xcur", i, 1)
                wait(pe, ph, "va_sb", i)
                if ph is XATTN1 or ph in (ROUTE0, ROUTE1):
                    wait(pe, ph, "lg_sb", i)
                wait(pe, ph, "xt_sb", i)
                for k in range(KC):
                    ins = pe.transpose(M[:, k * P:k * P + P], xcur[:, k * P:k * P + P], ident)
                ins.then_inc(sems["xt_ps"], 1)
                t0 = T[0][:, :].rearrange("p (k t) -> p k t", t=P)
                t1 = T[1][:, :].rearrange("p (k t) -> p k t", t=P)
                wait(pe, ph, "xt_sb", i, 1)
                if ph in (ROUTE0, ROUTE1):
                    n = E0 if ph is ROUTE0 else E1
                    w = wv("w_rt0" if ph is ROUTE0 else "w_rt1")
                    if first:
                        pe.wait_ge(s_w["d" if ph is ROUTE0 else "e"], NW["d" if ph is ROUTE0 else "e"])
                    over_k(M[:, 256:256 + n], lambda k: xT[:, k, :], lambda k: w[:, k, :]).then_inc(sems["lg_ps"], 1)
                    return
                if ph is XATTN1:
                    return
                if ph is ATTN0:
                    if first:
                        pe.wait_ge(s_w["a"], NW["a"])
                    w, v = wv("w0_qk"), wv("w0_v")
                    for c in range(4):
                        ins = over_k(t0[:, c, :], lambda k: w[:, k, c * P:c * P + P], lambda k: xT[:, k, :])
                    ins.then_inc(sems["qk_ps"], 1)
                if ph is XATTN0:
                    if first:
                        pe.wait_ge(s_w["b"], NW["b"])
                        pe.wait_ge(s_ctxt, 16)
                    w = wv("wx_fc")
                    cx = CTXT[:, :, i, :] if isinstance(i, int) else CTXT[:, :, bass.ds(i, 1), :]
                    if not first:
                        wait(pe, ph, "qk_a", i)
                    for c in range(KC):
                        over_k(t1[:, c, :], lambda k: w[:, k, c * P:c * P + P], lambda k: xT[:, k, :])
                    for c in range(KC):
                        ins = over_k(t1[:, KC + c, :], lambda k: w[:, k, c * P:c * P + P], lambda k: cx[:, k])
                    ins.then_inc(sems["rf_ps"], 1)
                    wait(pe, ph, "rf_sb", i, 1)
                    for k in range(KC):
                        ins = pe.transpose(M[:, k * P:k * P + P], rT[:, k, :], ident)
                    ins.then_inc(sems["rn_ps"], 1)
                    for n, wn in enumerate(("wx_q", "wx_k")):
                        w = wv(wn)
                        for c in range(KC):
                            ins = over_k(t0[:, KC * n + c, :], lambda k: w[:, k, c * P:c * P + P], lambda k: rT[:, KC * n + k, :])
                    ins.then_inc(sems["qk_ps"], 1)
                    v = wv("wx_v")
                    wait(pe, ph, "x_ref", i, 1)
                if ph is MLA0:
                    if first:
                        pe.wait_ge(s_w["c"], NW["c"])
                    lt, kx, kr, up = wv("wm_lat"), wv("wm_kx"), wv("wm_kr"), wv("wm_up", 3)
                    over_k(M[:, 256:256 + P], lambda k: lt[:, k, :], lambda k: xT[:, k, :]).then_inc(sems["lat_ps"], 1)
                    for c in range(KC):
                        over_k(t1[:, KC + c, :], lambda k: kr[:, k, c * P:c * P + P], lambda k: xT[:, k, :])
                    wait(pe, ph, "lat_sb", i, 1)
                    for c in range(KC):
                        cs = slice(c * P, c * P + P)
                        for k in range(KC):
                            mm(t0[:, KC + c, :], kx[:, k, cs], xT[:, k, :], start=(k == 0), stop=False)
                        mm(t0[:, KC + c, :], up[:, 0, cs], latT[:, :], start=False)
                        mm(t0[:, c, :], up[:, 1, cs], latT[:, :])
                        ins = mm(t1[:, c, :], W["wm_qr"][:, cs], latT[:, :])
                    ins.then_inc(sems["qk_ps"], 1)
                    mm(M[:, 256:512], latT[:, :], up[:, 2, :]).then_inc(sems["v_ps"], 1)
                    return
                if ph is ATTN1:
                    if first:
                        pe.wait_ge(s_w["e"], NW["e"])
                    w, v = wv("w1_qk"), wv("w1_v")
                    over_k(T[0][:, :], lambda k: xT[:, k, :], lambda k: w[:, k, :]).then_inc(sems["qk_ps"], 1)
                src = rT[:, KC:2 * KC, :] if ph is XATTN0 else xT[:, :, :]
                over_k(M[:, 256:512], lambda k: src[:, k, :], lambda k: v[:, k, :]).then_inc(sems["v_ps"], 1)

            def b(ph, i):
                if ph in (ROUTE0, ROUTE1):
                    return
                if ph is XATTN1:
                    cx = CTXT[:, :, i, :] if isinstance(i, int) else CTXT[:, :, bass.ds(i, 1), :]
                    wait(pe, ph, "mk_a", i)
                    wait(pe, ph, "sub", i)
                    over_k(S[:, 0:P], lambda k: xT[:, k, :], lambda k: cx[:, k]).then_inc(sems["s_ps"], 1)
                    return
                if ph is ATTN1:
                    wait(pe, ph, "fm_y", i, 1)
                    y = fm1[:, :, :].rearrange("p h d -> p (h d)")
                    for c in range(4):
                        ins = pe.transpose(T[1][:, c * P:c * P + P], y[:, c * P:c * P + P], ident)
                    ins.then_inc(sems["yt_ps"], 1)
                wait(pe, ph, "mv_sb", i, 1)
                if ph is MLA0:
                    if isinstance(i, int) and i == 0:
                        pe.wait_ge(s_init, 2)
                else:
                    wait(pe, ph, "qk_a", i, 1)
                wait(pe, ph, "sub", i)
                if ph is ATTN1 and isinstance(i, int):
                    wait(pe, MOE0, "z_sb", NB)
                for j in range(4):
                    c, r = j // 2, 64 * (j % 2)
                    bank = S[:, 512 * j:512 * j + 512]
                    if ph is MLA0:
                        mm(bank, identb[:, :], negb[:, :].unsqueeze(1).to_broadcast([P, 4, P]), stop=False)
                    ins = mm(bank, stat[r:r + 64, c, :], mv[r:r + 64, c, :, :], start=ph is not MLA0)
                    if j % 2:
                        ins.then_inc(sems["s_ps"], 1)

            def c(ph, i):
                if ph in (ROUTE0, ROUTE1):
                    n = E0 if ph is ROUTE0 else E1
                    wait(pe, ph, "cb", i, 1)
                    wait(pe, ph, "cbt_sb", i)
                    pe.transpose(OB[0:n, 0:P], cbs[:, 0:n], ident).then_inc(sems["cbt_ps"], 1)
                    return
                if ph is XATTN1:
                    wait(pe, ph, "exp", i, 1)
                    pe.transpose(T[0][:, 0:P], PR[:, 0, :], ident).then_inc(sems["pt_ps"], 1)
                    cx = CTX[:, i, :] if isinstance(i, int) else CTX[:, bass.ds(i, 1), :]
                    if isinstance(i, int):
                        pe.wait_ge(s_ctx, 16)
                    wait(pe, ph, "pt_a", i, 1)
                    wait(pe, ph, "z_sb", i)
                    if 1:
                        mm(OB[:, 0:D], PT[:, 0, :], cx).then_inc(sems["pr_ps"], 1)
                    return

                def pv(q):
                    if ph is ATTN1:
                        wait(pe, ph, "exp", i, q // 2 + 1)
                    else:
                        wait(pe, ph, "pt_d" if q % 2 else "pt_a", i, q // 2 + 1)
                    for h in range(4 * q, 4 * q + 4):
                        vv = VA[:, i, h, :] if isinstance(i, int) else VA[:, bass.ds(i, 1), h, :]
                        ins = mm(OB[:, 17 * h:17 * h + 17], PT[:, h, :], vv)
                    if q == 3:
                        ins.then_inc(sems["o_ps"], 1)
                wait(pe, ph, "z_sb", i)
                if ph is ATTN1:
                    wait(pe, ph, "va_sb", i, 1)
                    for q in range(4):
                        pv(q)
                    return
                for q in range(4):
                    if q % 2 == 0:
                        wait(pe, ph, "exp", i, q // 2 + 1)
                    if q == 0:
                        c_free(ph, i)
                    if q >= 2:
                        wait(pe, ph, "pt_d" if q % 2 else "pt_a", i, 1)
                    for h in range(4):
                        ins = pe.transpose(T[q % 2][:, h * P:h * P + P], PR[:, 4 * q + h, :], ident)
                    ins.then_inc(sems["pt_ps"], 1)
                    if q >= 1:
                        if q == 1:
                            wait(pe, ph, "va_sb", i, 1)
                        pv(q - 1)
                pv(3)

            def c_free(ph, i):
                if isinstance(i, int) and i == NB - 1:
                    nxt = {"attn0": XATTN0, "xattn0": MLA0}.get(ph.name)
                    if nxt is XATTN0:
                        wait(pe, nxt, "qk_a", 0, 1)
                    if nxt is MLA0:
                        wait(pe, nxt, "rope_b", 0, 1)
                    return
                wait(pe, ph, "qk_a", i + 1, 1)
                wait(pe, ph, "rope_b", i + 1, 1)

            def d(ph, i):
                if "ot_ps" not in ph.fires:
                    return
                last = isinstance(i, int) and i == NB - 1
                if not last:
                    wait(pe, ph, "va_sb", i + 1, 1)
                elif ph is ATTN0:
                    wait(pe, XATTN0, "va_sb", 0, 1)
                elif ph is MLA0:
                    wait(pe, ROUTE0, "lg_sb", 0, 1)
                elif ph is ATTN1:
                    wait(pe, XATTN1, "xt_sb", 0, 1)
                wait(pe, ph, "o_sb", i, 1)
                for k in range(KC):
                    ins = pe.transpose(M[:, k * P:k * P + P], O[:, k * P:k * P + P], ident)
                ins.then_inc(sems["ot_ps"], 1)
                w = wv({"attn0": "w0_o", "mla0": "wm_o", "attn1": "w1_o"}[ph.name])
                wait(pe, ph, "ot_sb", i, 1)
                over_k(OB[:, 0:D], lambda k: OT[:, k, :], lambda k: w[:, k, :]).then_inc(sems["pr_ps"], 1)

            def experts(m, name):
                u0, n_blocks, prev = m["u0"], m["n"], m["prev"]
                ub = [M, OB]
                wait(pe, prev, "ht", NB)
                wait(pe, prev, "lg_sb", NB)
                wait(pe, prev, "cbt_sb", NB)
                wait(pe, m["ph"], "z_sb", 0)
                wait(pe, m["ph"], "sub", 0)
                wait(pe, m["ph"], "mk_a", 0)

                def gate_up(half, u, slot, k):
                    if half == 0:
                        pe.wait_ge(s_blk[slot], landed(pe, name, k))
                    if not isinstance(u, int) or u >= 2:
                        pe.wait_ge(s_h0, u - 1)
                    w = blk[slot][:, 0:512].rearrange("p (g k n) -> p g k n", g=2, k=KC)
                    for g, bank in ((0, T[half]), (1, ub[half])):
                        ins = over_k(bank[:, :], lambda k_: w[:, g, k_, :], lambda k_: HT[:, k_, 4 * half:4 * half + 4, :])
                    ins.then_inc(s_gu, 1)

                def down(half, u, slot):
                    pe.wait_ge(s_hid, u + 1)
                    for t in range(4):
                        tok = 4 * half + t
                        ins = mm(S[:, D * tok:D * tok + D], hid[half][:, t * P:t * P + P], blk[slot][:, 512:768],
                                 start=False, stop=False, skip_group_check=True)
                    ins.then_inc(s_dn, 1)

                for j in range(4):
                    mm(S[:, 512 * j:512 * j + 512], identb[:, :], zerob[:, :], stop=False, skip_group_check=True)
                gate_up(0, u0, 0, 1)
                gate_up(1, u0 + 1, 0, 1)
                down(0, u0, 0)
                with pe.Fori(0, (n_blocks - 1) // 2) as j:
                    for k in range(4):
                        slot, half = 1 - k // 2, k % 2
                        u = j * 4 + (u0 + 2 + k)
                        gate_up(half, u, slot, j + (1 if slot else 2))
                        down(1 - half, j * 4 + (u0 + 1 + k), (0, 1, 1, 0)[k])
                if n_blocks % 2 == 0:
                    u = u0 + 2 * (n_blocks - 1)
                    gate_up(0, u, 1, n_blocks // 2)
                    down(1, u - 1, 0)
                    gate_up(1, u + 1, 1, n_blocks // 2)
                    down(0, u, 1)
                    down(1, u + 1, 1)
                else:
                    down(1, u0 + 2 * n_blocks - 1, 0)

            walk(pe, a, b, c, d, experts)


def constants():
    c = np.zeros((P, C_END), np.float32)
    p, t = np.arange(P)[:, None], np.arange(P)[None, :]
    c[:, C_ID:C_ID + P] = p == t
    c[:, C_TRI:C_TRI + P] = p <= t
    c[:, C_NEG:C_NEG + P] = np.where(t > p, np.float32(NEG), np.float32(0))
    inv = np.float32(1) / np.power(np.float32(10000), np.arange(0, RD, 2, dtype=np.float32) / np.float32(RD))
    ang = np.outer(np.arange(P, dtype=np.float32), inv.astype(np.float32)).astype(np.float32)
    emb = np.concatenate([ang, ang], axis=-1).T
    for row in range(P):
        d = row % HD
        if d < RD:
            c[row, C_COS:C_COS + P] = 1
        else:
            c[row, C_COS:C_COS + P] = np.cos(emb[d - RD])
            c[row, C_SIN:C_SIN + P] = np.sin(emb[d - RD]) * (-1 if d - RD < RD // 2 else 1)
        c[row, C_MASK + row % 64 // HD] = 1
        c[row, C_SEL + (0 if d < RD else 1)] = np.float32(8 ** -0.5) if d < RD else 1
    return c


def kernel(**inputs):
    import concourse.bacc as bacc
    from concourse.bass_utils import run_bass_kernel_spmd as run

    a = {n: np.asarray(v) for n, v in inputs.items()}

    def chunks(w):
        return np.ascontiguousarray(w.reshape(-1, P, w.shape[1]).transpose(1, 0, 2).reshape(P, -1))

    def row(*vs):
        return np.ascontiguousarray(np.concatenate([v.reshape(-1) for v in vs])[None, :])

    h, d = np.arange(NH)[:, None], np.arange(HD)[None, :]
    half = HD // 2
    q_cols = np.where(d < half, h * half + d, 256 + h * half + d - half).reshape(-1)
    wa = a["L0_attn_W_attn"]
    rope = (h * RD + d - RD)[:, RD:]
    swap = np.concatenate([rope[:, RD // 2:], rope[:, :RD // 2]], axis=1)

    def spread(plain, roped, order):
        src = plain if plain is not None else roped
        w = np.zeros((src.shape[0], NH, HD), np.float32)
        if plain is not None:
            w[:, :, :RD] = plain.reshape(-1, NH, RD)
        if roped is not None:
            w[:, :, RD:] = roped[:, order]
        return w.reshape(-1, D)

    kr, qr = a["L0_ffn_rope_k_w"], a["L0_ffn_rope_q_w"]
    up = np.zeros((P, 3, D), np.float32)
    up[:LAT, 0] = spread(a["L0_ffn_k_u_w"], None, None)
    up[LAT:, 1] = spread(a["L0_ffn_q_u_w"], qr, rope)
    up[:LAT, 2] = a["L0_ffn_v_u_w"]
    qrot = np.zeros((P, D), np.float32)
    qrot[LAT:] = spread(None, qr, swap)
    cols = np.zeros((P, 16), np.float32)
    for n, name in enumerate(["L0_ffn_ln1_w", "L0_ffn_ln2_w", "L0_xattn_b_q", "L0_xattn_b_k", "L0_xattn_b_fc"]):
        cols[:, 2 * n:2 * n + 2] = a[name].reshape(KC, P).T
    rt0 = np.zeros((D, E0), np.float32)
    rt0[:, :7] = a["L0_ffn_router_w"]
    rb = np.zeros((E0,), np.float32)
    rb[:7] = a["L0_ffn_router_b"]

    def block(gate, upw, down):
        return np.concatenate([chunks(gate), chunks(upw), down], axis=1)

    blocks0 = np.stack([block(a["L0_ffn_sh_gate"], a["L0_ffn_sh_up"], a["L0_ffn_sh_down"])] +
                       [block(a["L0_ffn_r_gate"][e], a["L0_ffn_r_up"][e], a["L0_ffn_r_down"][e]) for e in range(7)])
    gu, dn = a["L1_ffn_gate_up_proj"], a["L1_ffn_down_proj"]
    none = np.zeros((D, 64), np.float32)
    shared = block(np.concatenate([a["L1_ffn_shared_gate_w"].T, none], axis=1),
                   np.concatenate([a["L1_ffn_shared_up_w"].T, none], axis=1),
                   np.concatenate([a["L1_ffn_shared_down_w"].T, none.T], axis=0))
    blocks1 = np.stack([shared] + [
        block(np.concatenate([gu[e, :64].T, gu[e + 1, :64].T], axis=1),
              np.concatenate([gu[e, 64:].T, gu[e + 1, 64:].T], axis=1),
              np.concatenate([dn[e].T, dn[e + 1].T], axis=0)) for e in range(0, 64, 2)])

    arrays = {
        "x": a["x"], "ctx": a["ctx_2048"], "ctxT": a["ctx_2048"].reshape(-1, D).T,
        "mask": a["mask_BxS2_bk0"].reshape(1, -1).view(np.int32), "consts": constants(),
        "row_lam": row(a["L0_attn_lambda_q1"], a["L0_attn_lambda_k1"], a["L0_attn_lambda_q2"], a["L0_attn_lambda_k2"]),
        "row_bv": row(a["L0_xattn_b_v"]), "row_rb": row(rb), "row_gb": row(a["L1_attn_gamma"], a["L1_attn_beta"]),
        "w0_qk": chunks(np.concatenate([wa[:, q_cols], wa[:, q_cols + 128]], axis=1)),
        "w0_v": chunks(wa[:, 512:]), "w0_o": chunks(a["L0_attn_W_proj"]),
        "wx_fc": chunks(a["L0_xattn_W_fc"].T), "wx_q": chunks(a["L0_xattn_W_q"].T), "wx_k": chunks(a["L0_xattn_W_k"].T),
        "wx_v": chunks(a["L0_xattn_W_v"].reshape(D, D).T),
        "wm_lat": chunks(np.concatenate([a["L0_ffn_kv_d_w"], a["L0_ffn_q_d_w"]], axis=1)),
        "wm_kx": chunks(spread(None, kr, rope)), "wm_kr": chunks(spread(None, kr, swap)),
        "wm_up": up.reshape(P, -1), "wm_qr": qrot, "wm_o": chunks(a["L0_ffn_o_w"]), "w_rt0": chunks(rt0), "cols": cols,
        "w1_qk": chunks(np.concatenate([a["L1_attn_Wq"].T, a["L1_attn_Wk"].T], axis=1)),
        "w1_v": chunks(a["L1_attn_Wv"].T), "w1_o": chunks(a["L1_attn_Wo"].T),
        "w_rt1": chunks(np.concatenate([a["L1_ffn_router_w"].T, a["L1_ffn_shared_expert_gate_w"].T], axis=1)),
        "blocks0": blocks0, "blocks1": blocks1,
    }
    nc = bacc.Bacc("TRN2", target_bir_lowering=False, num_devices=1)
    arrays = {n: np.ascontiguousarray(v) for n, v in arrays.items()}
    t_in = {n: nc.dram_tensor("in_" + n, v.shape, mybir.dt.from_np(v.dtype), kind="ExternalInput").ap()
            for n, v in arrays.items()}
    out = nc.dram_tensor("out_0", (NB, P, D), F32, kind="ExternalOutput").ap()
    build(nc, t_in, out)
    r = run(nc, [{"in_" + n: v for n, v in arrays.items()}], core_ids=[0])
    return r.results[0]["out_0"]
```

```python
from contextlib import ExitStack

import numpy as np

import concourse.bass as bass
from concourse import mybir

F32 = mybir.dt.float32
BF16 = mybir.dt.bfloat16
F32R = mybir.dt.float32r
I32 = mybir.dt.int32
U8 = mybir.dt.uint8
ALU = mybir.AluOpType
ACT = mybir.ActivationFunctionType
AX_X = mybir.AxisListType.X

P = 128
NB = 8
D = 256
KC = D // P
NH = 16
HD = D // NH
EPS = 1e-5
NEG = -1e30
LAT = 64
RD = 8
E0, E1 = 8, 65
BLK = 768
HIGH = -4096
OUT0 = 0.8

C_ID, C_TRI, C_NEG, C_COS, C_SIN, C_MASK, C_SEL, C_R = 0, 128, 256, 384, 512, 640, 644, 646
C_END = 646 + 16

WEIGHTS = {
    "w0_qk": KC * 512, "w0_v": KC * D, "w0_o": KC * D,
    "wx_fc": KC * D, "wx_q": KC * D, "wx_k": KC * D, "wx_v": KC * D,
    "wm_lat": KC * P, "wm_kx": KC * D, "wm_kr": KC * D, "wm_up": 3 * D, "wm_qr": D, "wm_o": KC * D,
    "w_rt0": KC * E0,
    "w1_qk": KC * 512, "w1_v": KC * D, "w1_o": KC * D, "w_rt1": KC * E1,
    "cols": 16,
}
ROWS = {"lam": 4 * D, "bv": D, "rb": E0, "gb": 2 * HD}


class Phase:
    total = {}

    def __init__(self, name, fires, turns=NB):
        self.name, self.fires = name, fires
        self.base = dict(Phase.total)
        for s, n in fires.items():
            Phase.total[s] = Phase.total.get(s, 0) + n * turns


def build(nc, t_in, out):
    Phase.total = {}
    common = {"xcur": 1, "xt_ps": 1, "xt_sb": 1}
    attn = dict(common, qk_ps=1, v_ps=1, va_sb=1, mv_sb=2, s_ps=2, o_ps=1, rec=1, o_sb=1,
                z_sb=1)
    norm = dict(bst=1, bag=1, bve=1, bpw=1, x_out=1)
    soft = dict(attn, mx=2, sub=2, exp=2, pt_ps=4, pt_a=3, pt_d=1)
    proj = dict(ot_ps=1, ot_sb=1, pr_ps=1)
    ATTN0 = Phase("attn0", dict(soft, **norm, k_a=1, qk_a=1, **proj))
    XATTN0 = Phase("xattn0", dict(soft, **norm, k_a=1, qk_a=1, rf_ps=1, rf_sb=1, rn_ps=1, xbv=1, x_ref=1))
    MLA0 = Phase("mla0", dict(soft, rms_e=1, rms_p=1, xc0=1, lat_ps=1, lat_sb=1, rot_ps=1, rope_a=1, rope_b=1, k_sb=1, q_sb=1,
                              hsq=1, hms=1, hpw=1, hn=1, xh=1, **proj))
    ROUTE0 = Phase("route0", dict(common, ht_m=1, ht_h=1, ht=1, lg_ps=1, lg_sb=1))
    RULE0 = Phase("rule0", dict(lg_e=1, r1=1, r2=1, r3=8, r4=1, r5=1, r6=1, cb=1, cbt_ps=2, cbt_sb=2), turns=1)
    MOE0 = Phase("moe0", dict(z_sb=8, bst=8, bag=8, bve=2, bpw=2, x_out=8), turns=1)
    ATTN1 = Phase("attn1", dict(attn, **norm, fm_g=1, fm_b=1, fm_s=1, fm_c=1, fm_q=1, fm_v=1, fm_e=1, fm_p=1, fm_r=1, fm_y=1, yt_ps=1,
                                k_a=1, qk_a=1, sub=2, exp=2, ze=1, **proj))
    XATTN1 = Phase("xattn1", dict(common, s_ps=1, mxr=1, mx=1, exp=1, pt_ps=1, pt_a=1, pr_ps=1, rec=1, rv=1,
                                  z_sb=1, bst=1, bag=1, bve=1, bpw=1, x_out=1))
    ROUTE1 = Phase("route1", dict(common, ht_m=1, ht_h=1, ht=1, lg_ps=1, lg_sb=1))
    RULE1 = Phase("rule1", dict(lg_e=1, r1=8, r2=1, r3=1, r4=1, r5=1, r6=1, r7=1, cb=1, cbt_ps=2, cbt_sb=2), turns=1)
    MOE1 = Phase("moe1", dict(z_sb=8, bst=8, bag=8, bve=2, bpw=2, x_out=8), turns=1)

    ctx = ExitStack()
    with ctx:
        def sb(name, shape, dt=F32):
            return ctx.enter_context(nc.sbuf_tensor(name, shape, dt))

        def sem(name):
            return ctx.enter_context(nc.semaphore(name))

        X = sb("X", [P, NB, D])
        H = sb("H", [P, NB, D])
        CTX = sb("CTX", [P, NB, D])
        CTXT = sb("CTXT", [P, KC, NB, P])
        HTh, HTl = sb("HTh", [P, KC, NB, P], F32R), sb("HTl", [P, KC, NB, P], F32R)
        xm = sb("xm", [P, KC, P])
        VA = sb("VA", [P, NB, NH, HD + 1])
        W = {n: sb(n, [P, c]) for n, c in WEIGHTS.items()}
        R = {n: sb("row_" + n, [P, c]) for n, c in ROWS.items()}
        CONST = sb("CONST", [P, C_END])
        MKU = sb("MKU", [P, NB * P // 4], mybir.dt.int32)
        MK = sb("MK", [P, NB, P])
        MKN = sb("MKN", [P, NB, P], BF16)
        VALID = sb("VALID", [P, NB])
        identb = sb("identb", [P, P], BF16)
        negb = sb("negb", [P, P], BF16)
        zerob = sb("zerob", [P, 512], BF16)
        neghalf = sb("neghalf", [P, 32])
        lam = sb("lam", [P, 8])
        qscale = sb("qscale", [P, 1])
        junk = sb("junk", [P, D])
        xcur = sb("xcur", [P, D])
        junk_a = sb("junk_a", [P, D])
        xT = sb("xT", [P, KC, P])
        rT = sb("rT", [P, 2 * KC, P])
        latT = sb("latT", [P, P])
        stat = sb("stat", [P, KC, 2, P])
        raw = sb("raw", [P, KC, P])
        rope1 = sb("rope1", [P, 2 * KC, P])
        rope2 = sb("rope2", [P, 2 * KC, P])
        mv = sb("mv", [P, KC, 4, P])
        SM = sb("SM", [P, NH, P])
        PR = sb("PR", [P, NH, P])
        PT = sb("PT", [P, NH, P])
        mx = sb("mx", [P, NH])
        rec = sb("rec", [P, NH])
        mxm = sb("mxm", [P, 2])
        recm = sb("recm", [P, 4])
        O = sb("O", [P, D])
        OT = sb("OT", [P, KC, P])
        z = sb("z", [P, D])
        bst = sb("bst", [P, 6])
        bag = sb("bag", [P, 2])
        bve = sb("bve", [P, 1])
        rstd = sb("rstd", [P, 1])
        Z = H
        bst8 = sb("bst8", [P, NB, 6])
        bag8 = sb("bag8", [P, NB, 2])
        bve8 = sb("bve8", [P, NB])
        rstd8 = sb("rstd8", [P, NB])
        rms = sb("rms", [P, 4])
        hrm = sb("hrm", [P, 4])
        fm1 = sb("fm1", [P, 2 * NH, HD])
        fm2 = sb("fm2", [P, 2 * NH, HD])
        fms = sb("fms", [P, 4, 2 * NH])
        lg0, lg1 = sb("lg0", [P, NB, E0]), sb("lg1", [P, NB, E1])
        p16 = sb("p16", [P, NB, 16])
        mr8 = sb("mr8", [P, NB, 8])
        m8 = sb("m8", [P, NB, 8])
        rep0, rep1 = sb("rep0", [P, NB, 16]), sb("rep1", [P, NB, 64])
        sel = sb("sel", [P, NB, 64])
        ex = sb("ex", [P, NB, E1])
        es = sb("es", [P, NB, 64])
        rsm = sb("rsm", [P, 4, NB])
        cbs0, cbs1 = sb("cbs0", [P, NB, E0]), sb("cbs1", [P, NB, E1])
        cbT = sb("cbT", [E1, NB, P])
        blk = [sb(f"blk{k}", [P, BLK]) for k in range(2)]
        def lent(buf, k, n):
            return buf[:, :, :].rearrange("p h t -> p (h t)")[:, k * n:k * n + n]
        wb = [lent(PR, k, NB * P) for k in range(2)]
        sil, hid0 = [lent(SM, k, 512) for k in (0, 1)], [lent(SM, k, 512) for k in (2, 3)]
        hid, hidm = [lent(PT, k, 512) for k in (0, 1)], [lent(PT, k, 512) for k in (2, 3)]
        hidh = [sb(f"hidh{k}", [P, 512], F32R) for k in range(2)]
        hidl = [sb(f"hidl{k}", [P, 512], F32R) for k in range(2)]
        blkm = mv[:, :, :, :].rearrange("p k h t -> p (k h t)")[:, 0:BLK]
        blkh = [sb(f"blkh{k}", [P, BLK], F32R) for k in range(2)]
        blkl = [sb(f"blkl{k}", [P, BLK], F32R) for k in range(2)]

        S = ctx.enter_context(nc.psum_tensor("S", [P, 2048], F32))
        T = [ctx.enter_context(nc.psum_tensor(f"T{k}", [P, 512], F32)) for k in range(2)]
        M = ctx.enter_context(nc.psum_tensor("M", [P, 512], F32))
        OB = ctx.enter_context(nc.psum_tensor("OB", [P, 512], F32))

        N_INIT = 20
        HALVES = (slice(0, 64), slice(64, P))
        ident = CONST[:, C_ID:C_ID + P]
        tri = CONST[:, C_TRI:C_TRI + P]
        names = sorted(Phase.total)
        sems = {n: sem("s_" + n) for n in names}
        s_x0, s_x1, s_ctxt, s_ctx, s_cst, s_row = sem("s_x0"), sem("s_x1"), sem("s_ctxt"), sem("s_ctx"), sem("s_cst"), sem("s_row")
        s_w = {n: sem("s_w_" + n) for n in ("a", "b", "c", "d", "e")}
        s_mk, s_mk2 = sem("s_mk"), sem("s_mk2")
        s_init, s_pinit, s_lam, s_lame = sem("s_init"), sem("s_pinit"), sem("s_lam"), sem("s_lame")
        s_cbd, s_out = [sem("s_cbd0"), sem("s_cbd1")], sem("s_out")
        s_blk = [sem("s_blk0"), sem("s_blk1")]
        s_wb = [sem("s_wb0"), sem("s_wb1")]
        s_bm, s_bh, s_bl = sem("s_bm"), sem("s_bh"), sem("s_bl")
        s_hm, s_hh, s_hl = sem("s_hm"), sem("s_hh"), sem("s_hl")
        s_gu, s_sil, s_h0, s_hid, s_dn = sem("s_gu"), sem("s_sil"), sem("s_h0"), sem("s_hid"), sem("s_dn")

        WGROUP = {"w0_qk": "a", "w0_v": "a", "w0_o": "a", "wx_fc": "b", "wx_q": "b", "wx_k": "b", "wx_v": "b",
                  "cols": "b", "wm_lat": "c", "wm_kx": "c", "wm_kr": "c", "wm_up": "c", "wm_qr": "c", "wm_o": "c",
                  "w_rt0": "d", "w1_qk": "e", "w1_v": "e", "w1_o": "e", "w_rt1": "e"}
        NW = {g: 16 * sum(1 for v in WGROUP.values() if v == g) for g in "abcde"}

        def wait(eng, ph, s, i, k=0, past=False):
            per = ph.fires.get(s, 0)
            if per == 0 and (k or not (isinstance(i, int) or past)):
                return
            if per == 0:
                i = 0
            v = ph.base.get(s, 0) + per * i + k
            if isinstance(v, int) and v <= 0:
                return
            eng.wait_ge(sems[s], v)

        s_apart = {"dve": sem("s_apart_dve"), "pool": sem("s_apart_pool"), "act": sem("s_apart_act")}

        def apart(eng, who):
            eng.sem_inc(s_apart[who], 1)

        def at(buf, i):
            return buf[:, i, :] if isinstance(i, int) else buf[:, bass.ds(i, 1), :]

        def logits(i):
            return M[:, 256:512] if isinstance(i, int) and i == 0 else OB

        def wv(n, k=KC):
            return W[n][:, :].rearrange("p (k n) -> p k n", k=k)

        def col(c):
            return W["cols"][:, c:c + 1]

        XT_SCALE = {"mla0": 0, "route0": 2}
        QB, KB, FB = 4, 6, 8

        D0 = nc.dram_tensor("route0_w", (E0, NB * P), F32, kind="Internal").ap()
        D1 = nc.dram_tensor("route1_w", (E1, NB * P), F32, kind="Internal").ap()

        block = ctx.enter_context(nc.Block())

        MOES = {
            "moe0": dict(ph=MOE0, prev=ROUTE0, rule=RULE0, w=t_in["blocks0"], dram=D0, cols=E0, n=8, scale=0.125, u0=0, dmas=1),
            "moe1": dict(ph=MOE1, prev=ROUTE1, rule=RULE1, w=t_in["blocks1"], dram=D1, cols=E1, n=33, scale=1.0, u0=16, dmas=2),
        }
        BEFORE = {"moe0": 0, "moe1": MOES["moe0"]["n"] // 2 * MOES["moe0"]["dmas"]}

        def spread_in(name, k):
            m = MOES[name]
            return (BEFORE[name] + m["dmas"] * k) * 16 if isinstance(k, int) else k * (16 * m["dmas"]) + 16 * BEFORE[name]

        def landed(name, k):
            k0 = MOES[name]["u0"] // 4
            return (k0 + k) * 16 if isinstance(k, int) else k * 16 + 16 * k0

        @block.sync
        def _(sp):
            sp.dma_start(CONST[:, :], t_in["consts"]).then_inc(s_cst, 16)
            sp.dma_start(X[:, 0:2, :], t_in["x"].rearrange("b t d -> t b d")[:, 0:2, :]).then_inc(s_x0, 16)

            def weights(g):
                for n, gg in WGROUP.items():
                    if gg == g:
                        sp.dma_start(W[n][:, :], t_in[n]).then_inc(s_w[g], 16)
            weights("a")
            for n in ROWS:
                sp.dma_start(R[n][:, :], t_in["row_" + n].to_broadcast([P, ROWS[n]])).then_inc(s_row, 16)
            sp.dma_start(X[:, 2:NB, :], t_in["x"].rearrange("b t d -> t b d")[:, 2:NB, :]).then_inc(s_x1, 16)
            weights("b")
            sp.dma_start(CTXT[:, :, :, :].rearrange("p k b t -> p k (b t)"),
                         t_in["ctxT"].rearrange("(k p) n -> p k n", p=P)).then_inc(s_ctxt, 16)
            weights("c")
            weights("d")
            weights("e")
            sp.dma_start(CTX[:, :, :], t_in["ctx"].rearrange("b t d -> t b d")).then_inc(s_ctx, 16)
            sp.dma_start(MKU[:, :], t_in["mask"].to_broadcast([P, NB * P // 4])).then_inc(s_mk, 16)

            def moe(name, which):
                m = MOES[name]
                dr, u0, n_blocks = m["dram"], m["u0"], m["n"]

                def load_w(n, slot):
                    src = m["w"][n] if isinstance(n, int) else m["w"][bass.ds(n, 1), :, :]
                    sp.dma_start(blk[slot][:, :], src).then_inc(s_blk[slot], 16)

                def load_b(n, slot):
                    def spread(e, p0, np_):
                        row = dr[e:e + 1, :] if isinstance(e, int) else dr[bass.ds(e, 1), :]
                        sp.dma_start(wb[slot][p0:p0 + np_, :], row.to_broadcast([np_, NB * P])).then_inc(s_wb[slot], 16)
                    first = isinstance(n, int) and n == 0
                    if which == 0:
                        spread(E0 - 1 if first else n - 1, 0, P)
                    else:
                        spread(E1 - 1 if first else n * 2 - 2, 0, 64)
                        spread(E1 - 1 if first else n * 2 - 1, 64, 64)

                if which == 1:
                    sp.wait_ge(s_bh, u0 // 2)
                    sp.wait_ge(s_bl, u0 // 2)
                    sp.wait_ge(s_hid, u0)
                load_w(0, 0)
                load_w(1, 1)
                wait(sp, m["rule"], "cbt_sb", 0, 2)
                sp.dma_start(dr.rearrange("e (b t) -> e b t", b=NB), cbT[0:m["cols"], :, :]).then_inc(s_cbd[which], 16)
                sp.wait_ge(s_cbd[which], 16)
                load_b(0, 0)
                load_b(1, 1)
                def reload(n, slot, split, used):
                    sp.wait_ge(s_bm, split)
                    sp.wait_ge(s_bl, split)
                    load_w(n, slot)
                    sp.wait_ge(s_hid, used)
                    load_b(n, slot)

                with sp.Fori(0, (n_blocks - 2) // 2) as j:
                    for k in range(2):
                        reload(j * 2 + (2 + k), k, j * 2 + (u0 // 2 + 1 + k), j * 4 + (u0 + 2 + 2 * k))
                if n_blocks % 2:
                    reload(n_blocks - 1, 0, u0 // 2 + n_blocks - 2, u0 + 2 * (n_blocks - 2))

            moe("moe0", 0)
            moe("moe1", 1)
            with sp.Fori(0, NB) as i:
                sp.wait_ge(sems["x_out"], i + (MOE1.base["x_out"] + 1))
                sp.dma_start(out.rearrange("b t d -> t b d")[:, bass.ds(i, 1), :], X[:, bass.ds(i, 1), :]).then_inc(s_out, 16)
            sp.wait_ge(s_out, 16 * NB)

        def blocks(eng, m, split, unit, early=False):
            u0, n_blocks = m["u0"], m["n"]

            def block(n, u, slot, k, nxt):
                if nxt and early:
                    split(*nxt)
                unit(0, u, slot, k)
                if nxt and not early:
                    split(*nxt)
                unit(1, u + 1, slot, k)

            split(0, 0, 1)
            block(0, u0, 0, 1, (1, 1, 1))
            with eng.Fori(0, (n_blocks - 2) // 2) as j:
                block(j * 2 + 1, j * 4 + (u0 + 2), 1, j + 1, (j * 2 + 2, 0, j + 2))
                block(j * 2 + 2, j * 4 + (u0 + 4), 0, j + 2, (j * 2 + 3, 1, j + 2))
            for n in range(2 * ((n_blocks - 2) // 2) + 1, n_blocks):
                nxt = (n + 1, (n + 1) % 2, (n + 1) // 2 + 1) if n + 1 < n_blocks else None
                block(n, u0 + 2 * n, n % 2, n // 2 + 1, nxt)

        def walk(turn, eng, rule=None, experts=None, last=None):
            for name, chain in (("moe0", [ATTN0, XATTN0, MLA0, ROUTE0]), ("moe1", [ATTN1, XATTN1, ROUTE1])):
                turn(None, None, (chain[0], 0), None)
                for n, ph in enumerate(chain):
                    prev, nxt = (chain[n - 1] if n else None), (chain[n + 1] if n + 1 < len(chain) else None)
                    turn((ph, 0), (prev, NB - 1) if prev else None, (ph, 1), (prev, NB - 2) if prev else None)
                    turn((ph, 1), (ph, 0), (ph, 2), (prev, NB - 1) if prev else None)
                    with eng.Fori(2, NB - 1) as i:
                        turn((ph, i), (ph, i - 1), (ph, i + 1), (ph, i - 2))
                    turn((ph, NB - 1), (ph, NB - 2), (nxt, 0) if nxt else None, (ph, NB - 3))
                m = MOES[name]
                if rule is not None:
                    rule(m["rule"])
                if experts is not None:
                    experts(m, name)
                if last is not None:
                    last(m["ph"])

        @block.gpsimd
        def _(pool):
            pool.memset(neghalf[:, :], -0.5).then_inc(s_pinit, 1)
            pool.memset(VA[:, :, :, HD:HD + 1], 1.0).then_inc(s_pinit, 1)
            for j in range(9):
                pool.memset(p16[:, :, 7 + j:8 + j], -1.0 - j).then_inc(s_pinit, 1)
            for j in range(6):
                pool.memset(mr8[:, :, 2 + j:3 + j], -2.0 - j).then_inc(s_pinit, 1)
            pool.memset(cbs0[:, :, E0 - 1:E0], 1.0).then_inc(s_pinit, 1)
            pool.memset(stat[:, :, :, :], 0.0).then_inc(s_pinit, 1)
            pool.memset(zerob[:, :], 0.0).then_inc(s_pinit, 1)
            pool.wait_ge(s_cst, 16)
            pool.wait_ge(s_pinit, N_INIT)

            def power(ph, i, s_in, s_out_, out_, in_, n=1):
                wait(pool, ph, s_in, i, 1)
                pool.tensor_tensor(out_, in_, neghalf[:, 0:n], ALU.pow).then_inc(sems[s_out_], 1)

            def a0(ph, i):
                if "rms_p" in ph.fires:
                    power(ph, i, "rms_e", "rms_p", rms[:, 2:3], rms[:, 1:2])

            def a1(ph, i, old):
                if ph in (ROUTE0, ROUTE1):
                    wait(pool, ph, "ht_m", i, 1)
                    wait(pool, ph, "xt_sb", i, 1)
                    dst = HTl[:, :, i, :] if isinstance(i, int) else HTl[:, :, bass.ds(i, 1), :]
                    apart(pool, "pool")
                    pool.tensor_tensor(dst, xT[:, :, :], xm[:, :, :], ALU.subtract).then_inc(sems["ht"], 1)
                    return
                if ph in (ATTN1, XATTN1):
                    return
                wait(pool, ph, "k_sb" if ph is MLA0 else "k_a", i, 1)
                masked(ph, i, 0)
                if old and ph in (ATTN0, XATTN0):
                    d2(*old)
                masked(ph, i, 1)

            def e(ph, i):
                if ph is XATTN0:
                    if isinstance(i, int) and i == 0:
                        pool.wait_ge(s_row, 16 * len(ROWS))
                    wait(pool, ph, "xcur", i, 1)
                    wait(pool, ATTN0, "x_out", i, 1)
                    apart(pool, "pool")
                    pool.tensor_tensor(at(X, i), at(X, i), R["bv"][:, :], ALU.add).then_inc(sems["xbv"], 1)

            def d2(ph, i):
                if "bve" in ph.fires:
                    power(ph, i, "bve", "bpw", rstd[:, :], bve[:, :])
                if ph is MLA0:
                    power(ph, i, "hms", "hpw", hrm[:, 2:3], hrm[:, 1:2])
                    wait(pool, ph, "hpw", i, 1)
                    apart(pool, "pool")
                    pool.tensor_tensor(at(H, i), z[:, :], hrm[:, 2:3].to_broadcast([P, D]), ALU.mult).then_inc(sems["hn"], 1)

            def masked(ph, i, c):
                if c == 0:
                    wait(pool, ph, "s_ps", i)
                pool.tensor_tensor(
                    mv[:, c, :, :], raw[:, c, :].unsqueeze(1).to_broadcast([P, 4, P]),
                    CONST[:, C_MASK:C_MASK + 4].unsqueeze(2).to_broadcast([P, 4, P]),
                    ALU.mult).then_inc(sems["mv_sb"], 1)

            def y(ph, i):
                if ph is ATTN1:
                    wait(pool, ph, "k_a", i, 1)
                    masked(ph, i, 0)
                    masked(ph, i, 1)

            def experts(m, name):
                b0 = m["u0"] // 2

                def split(n, slot, k):
                    pool.wait_ge(s_bm, n + (b0 + 1))
                    if not isinstance(n, int) or n + b0 >= 2:
                        pool.wait_ge(s_dn, n * 2 + (2 * b0 - 2))
                    pool.tensor_tensor(blkl[slot][:, :], blk[slot][:, :], blkm[:, :], ALU.subtract).then_inc(s_bl, 1)

                blocks(pool, m, split, lambda *a: None)

            def last(ph):
                for h in range(2):
                    wait(pool, ph, "bve", 0, h + 1)
                    pool.tensor_tensor(rstd8[:, 4 * h:4 * h + 4], bve8[:, 4 * h:4 * h + 4], neghalf[:, 0:4],
                                       ALU.pow).then_inc(sems["bpw"], 1)

            def turn(now, before, after, old):
                if old and not (now and now[0] in (ATTN0, XATTN0)):
                    d2(*old)
                if now:
                    a1(*now, old)
                    y(*now)
                if after:
                    a0(*after)
                    e(*after)

            walk(turn, pool, experts=experts, last=last)

        @block.scalar
        def _(act):
            act.wait_ge(s_lam, 2)
            act.activation(lam[:, 2:4], lam[:, 0:2], ACT.Exp).then_inc(s_lame, 1)
            act.wait_ge(s_cst, 16)

            def wait_src(ph, i):
                before = {"xattn0": ATTN0, "mla0": XATTN0, "attn1": MOE0, "xattn1": ATTN1, "route1": XATTN1}
                if ph is ATTN0:
                    act.wait_ge(s_x0, 16)
                    if not isinstance(i, int) or i >= 2:
                        act.wait_ge(s_x1, 16)
                if ph.name in before:
                    if ph is ATTN1:
                        act.wait_ge(sems["x_out"], MOE0.base["x_out"] + 1 + i)
                    else:
                        wait(act, before[ph.name], "x_out", i, 1)
                if ph is ROUTE0:
                    wait(act, MLA0, "hn", i, 1)

            def tokens(ph, i):
                wait_src(ph, i)
                wait(act, ph, "xt_ps", i)
                if "rms_e" in ph.fires:
                    wait(act, ph, "rms_e", i)
                    apart(act, "act")
                    act.activation(junk_a[:, :], at(X, i), ACT.Square,
                                   accum_out=rms[:, 0:1]).then_inc(sems["xc0"], 1)
                else:
                    apart(act, "act")
                    act.activation(xcur[:, :], at(H if ph is ROUTE0 else X, i), ACT.Copy).then_inc(sems["xcur"], 1)

            def scaled(ph, i):
                if "rms_e" in ph.fires:
                    wait(act, ph, "rms_p", i, 1)
                    apart(act, "act")
                    act.activation(xcur[:, :], at(X, i), ACT.Copy,
                                   scale=rms[:, 2:3]).then_inc(sems["xcur"], 1)

            def a0(ph, i):
                if isinstance(i, int) and ph is XATTN0:
                    act.wait_ge(s_w["b"], NW["b"])
                wait(act, ph, "xt_ps", i, 1)
                wait(act, ph, "lg_ps", i)
                src = M[:, 0:D].rearrange("p (k t) -> p k t", k=KC)
                if ph.name in XT_SCALE:
                    if ph is ROUTE0:
                        wait(act, ph, "ht", i)
                    wait(act, ph, "ht_m", i)
                    for k in range(KC):
                        c_ = XT_SCALE[ph.name] + k
                        ins = act.activation(xT[:, k, :], src[:, k, :], ACT.Copy, scale=col(c_))
                    ins.then_inc(sems["xt_sb"], 1)
                else:
                    wait(act, ph, "ht", i)
                    wait(act, ph, "ht_m", i)
                    act.activation(xT[:, :, :], src, ACT.Copy).then_inc(sems["xt_sb"], 1)

            def a1(ph, i):
                first = isinstance(i, int) and i == 0
                if first:
                    act.wait_ge(s_pinit, N_INIT)
                t0 = T[0][:, :].rearrange("p (k t) -> p k t", t=P)
                t1 = T[1][:, :].rearrange("p (k t) -> p k t", t=P)
                if ph in (ROUTE0, ROUTE1):
                    return
                if ph is XATTN1:
                    return
                if ph is ATTN1:
                    return
                if ph in (ATTN0, XATTN0):
                    wait(act, ph, "qk_ps", i, 1)
                    wait(act, ph, "mv_sb", i)
                    wait(act, ph, "s_ps", i)
                    if ph is ATTN0:
                        if first:
                            act.wait_ge(s_lam, 4)
                        act.activation(raw[:, :, :], t0[:, KC:2 * KC, :], ACT.Copy).then_inc(sems["k_a"], 1)
                        for r_, rows in enumerate(HALVES):
                            ins = act.activation(stat[rows, :, r_, :], t0[rows, 0:KC, :], ACT.Copy, scale=qscale[rows, 0:1])
                        ins.then_inc(sems["qk_a"], 1)
                    else:
                        for k in range(KC):
                            ins = act.activation(raw[:, k, :], t0[:, KC + k, :], ACT.Identity, bias=col(KB + k))
                        ins.then_inc(sems["k_a"], 1)
                        for k in range(KC):
                            for r_, rows in enumerate(HALVES):
                                ins = act.activation(stat[rows, k, r_, :], t0[rows, k, :], ACT.Identity,
                                                     bias=W["cols"][rows, QB + k:QB + k + 1])
                        ins.then_inc(sems["qk_a"], 1)

            def e(ph, i):
                if ph is XATTN0:
                    wait(act, ph, "rf_ps", i, 1)
                    t1 = T[1][:, :].rearrange("p (k t) -> p k t", t=P)
                    for k in range(2 * KC):
                        ins = act.activation(rT[:, k, :], t1[:, k, :], ACT.Relu, bias=col(FB + k % KC))
                    ins.then_inc(sems["rf_sb"], 1)
                if ph is MLA0:
                    wait(act, ph, "lat_ps", i, 1)
                    wait(act, ph, "v_ps", i)
                    act.activation(latT[:, :], M[:, 256:256 + P], ACT.Copy).then_inc(sems["lat_sb"], 1)
                if ph is ATTN1:
                    values(ph, i)
                    wait(act, ph, "fm_c", i, 1)
                    act.activation(fm2[:, :, :], fm1[:, :, :], ACT.Square).then_inc(sems["fm_q"], 1)

            def values(ph, i):
                if ph in (ROUTE0, ROUTE1):
                    wait(act, ph, "ht_m", i, 1)
                    dst = HTh[:, :, i, :] if isinstance(i, int) else HTh[:, :, bass.ds(i, 1), :]
                    apart(act, "act")
                    act.activation(dst, xm[:, :, :], ACT.Copy).then_inc(sems["ht_h"], 1)
                    return
                if "v_ps" not in ph.fires:
                    return
                wait(act, ph, "v_ps", i, 1)
                dst = VA[:, i, :, 0:HD] if isinstance(i, int) else VA[:, bass.ds(i, 1), :, 0:HD]
                act.activation(dst, M[:, 256:512].rearrange("p (h d) -> p h d", h=NH), ACT.Copy).then_inc(sems["va_sb"], 1)

            def y(ph, i):
                if ph is ATTN1:
                    t1 = T[1][:, :].rearrange("p (k t) -> p k t", t=P)
                    wait(act, ph, "yt_ps", i, 1)
                    wait(act, ph, "mv_sb", i)
                    wait(act, ph, "s_ps", i)
                    act.activation(raw[:, :, :], t1[:, 0:KC, :], ACT.Copy).then_inc(sems["k_a"], 1)
                    for r_, rows in enumerate(HALVES):
                        ins = act.activation(stat[rows, :, r_, :], t1[rows, KC:2 * KC, :], ACT.Copy)
                    ins.then_inc(sems["qk_a"], 1)

            def b(ph, i, h):
                if ph in (ROUTE0, ROUTE1) or ph is XATTN1 and h:
                    return
                if ph is XATTN1:
                    wait(act, ph, "mx", i, 1)
                    wait(act, ph, "pt_ps", i)
                    act.activation(PR[:, 0, :], S[:, 0:P], ACT.Exp, scale=1.0 / 16, bias=mxm[:, 1:2], accum_out=recm[:, 0:1]).then_inc(sems["exp"], 1)
                    return
                wait(act, ph, "sub", i, h + 1)
                hs = slice(8 * h, 8 * h + 8)
                if ph is ATTN1:
                    wait(act, ph, "o_ps", i)
                    act.activation(PT[:, hs, :], SM[:, hs, :], ACT.Square, scale=0.25).then_inc(sems["exp"], 1)
                else:
                    wait(act, ph, "pt_ps", i)
                    act.activation(PR[:, hs, :], SM[:, hs, :], ACT.Exp,
                                   scale=1.0 if ph is ATTN0 else 0.25).then_inc(sems["exp"], 1)

            def root(ph, i):
                if ph is ATTN1:
                    wait(act, ph, "fm_e", i, 1)
                    act.activation(fms[:, 3, :], fms[:, 2, :], ACT.Sqrt).then_inc(sems["fm_p"], 1)

            def c(ph, i, part):
                if ph in (ROUTE0, ROUTE1):
                    return
                if ph is XATTN1:
                    if part:
                        return
                    wait(act, ph, "pt_ps", i, 1)
                    act.activation(PT[:, 0, :], T[0][:, 0:P], ACT.Copy).then_inc(sems["pt_a"], 1)
                    return
                if ph is ATTN1:
                    return
                for q in ((0,), (2, 3))[part]:
                    wait(act, ph, "pt_ps", i, q + 1)
                    act.activation(PT[:, 4 * q:4 * q + 4, :], T[1 - q % 2][:, :], ACT.Copy).then_inc(sems["pt_a"], 1)

            def d1(ph, i):
                if "ot_ps" in ph.fires:
                    wait(act, ph, "ot_ps", i, 1)
                    act.activation(OT[:, :, :], M[:, 0:D], ACT.Copy).then_inc(sems["ot_sb"], 1)

            def rule(ph):
                if ph is RULE0:
                    n = E0
                    wait(act, ROUTE0, "lg_sb", NB)
                    act.activation(ex[:, :, 0:E0], lg0[:, :, :], ACT.Exp, scale=-1.0).then_inc(sems["lg_e"], 1)
                else:
                    n = E1
                    wait(act, ph, "r3", 0, 1)
                    act.activation(ex[:, :, 0:64], sel[:, :, :], ACT.Exp)
                    act.activation(ex[:, :, 64:65], lg1[:, :, 64:65], ACT.Exp, scale=-1.0).then_inc(sems["lg_e"], 1)
                for h, bank in enumerate((OB, T[0])):
                    wait(act, ph, "cbt_ps", 0, h + 1)
                    act.activation(cbT[0:n, 4 * h:4 * h + 4, :], bank[0:n, :].rearrange("e (b t) -> e b t", b=4),
                                   ACT.Copy).then_inc(sems["cbt_sb"], 1)

            def experts(m, name):
                u0, b0 = m["u0"], m["u0"] // 2

                def split(n, slot, k):
                    act.wait_ge(s_bm, n + (b0 + 1))
                    if not isinstance(n, int) or n + b0 >= 2:
                        act.wait_ge(s_dn, n * 2 + (2 * b0 - 2))
                    act.activation(blkh[slot][:, :], blkm[:, :], ACT.Copy).then_inc(s_bh, 1)

                def high(half, u):
                    act.wait_ge(s_hm, u + 1)
                    if not isinstance(u, int) or u >= 2:
                        act.wait_ge(s_dn, u - 1)
                    act.activation(hidh[half][:, :], hidm[half][:, :], ACT.Copy).then_inc(s_hh, 1)

                def unit(half, u, slot, k):
                    act.wait_ge(s_gu, u + 1)
                    if not isinstance(u, int) or u >= 2:
                        act.wait_ge(s_hid, u - 1)
                    act.activation(sil[half][:, :], T[half][:, :], ACT.Silu).then_inc(s_sil, 1)
                    high(half, u)

                blocks(act, m, split, unit)

            def turn(now, before, after, old):
                if after and after[0] is ATTN1:
                    tokens(*after)
                if now:
                    a1(*now)
                    y(*now)
                if before:
                    c(*before, 0)
                    b(*before, 1)
                if after and after[0] is not ATTN1:
                    tokens(*after)
                if now and now[0] is not ATTN1:
                    values(*now)
                if before:
                    c(*before, 1)
                if after:
                    scaled(*after)
                    a0(*after)
                if now and now[0] is not ATTN1:
                    b(*now, 0)
                if after:
                    e(*after)
                if now and now[0] is ATTN1:
                    b(*now, 0)
                if after:
                    root(*after)
                if before:
                    d1(*before)

            walk(turn, act, rule, experts)

        @block.vector
        def _(dve):
            dve.wait_ge(s_cst, 16)
            dve.tensor_copy(identb[:, :], ident).then_inc(s_init, 1)
            dve.tensor_copy(negb[:, :], CONST[:, C_NEG:C_NEG + P]).then_inc(s_init, 1)
            dve.wait_ge(s_row, 16 * len(ROWS))
            lr = R["lam"][:, :].rearrange("p (a n) -> p a n", a=4)
            for j in range(2):
                if j:
                    dve.wait_ge(s_lam, 1)
                dve.tensor_tensor_reduce(out=junk[:, :], in0=lr[:, 2 * j, :], in1=lr[:, 2 * j + 1, :], scale=1.0,
                                         scalar=0.0, op0=ALU.mult, op1=ALU.add,
                                         accum_out=lam[:, j:j + 1]).then_inc(s_lam, 1)
            dve.wait_ge(s_lame, 1)
            dve.tensor_tensor(lam[:, 4:5], lam[:, 2:3], lam[:, 3:4], ALU.subtract).then_inc(s_lam, 1)
            dve.wait_ge(s_lam, 3)
            c8 = float(8 ** -0.5)
            dve.tensor_scalar(lam[:, 5:6], lam[:, 4:5], 0.2, -c8, ALU.add, ALU.mult).then_inc(s_init, 1)
            dve.wait_ge(s_init, 3)
            dve.scalar_tensor_tensor(qscale[:, :], in0=CONST[:, C_SEL + 1:C_SEL + 2], scalar=lam[:, 5:6],
                                     in1=CONST[:, C_SEL:C_SEL + 1], op0=ALU.mult, op1=ALU.add).then_inc(s_lam, 1)

            def a0(ph, i):
                if "rms_e" in ph.fires:
                    wait(dve, ph, "xc0", i, 1)
                    wait(dve, ph, "rms_p", i)
                    dve.tensor_scalar(rms[:, 1:2], rms[:, 0:1], 1.0 / D, EPS, ALU.mult, ALU.add).then_inc(sems["rms_e"], 1)

            def reference_features(ph, i):
                if ph is XATTN0:
                    wait(dve, ph, "rn_ps", i, 1)
                    wait(dve, ph, "xbv", i, 1)
                    dve.tensor_tensor(at(X, i), M[:, 0:D], at(X, i), ALU.add).then_inc(sems["x_ref"], 1)

            def a1(ph, i):
                if ph is MLA0:
                    for s, tb, cc, dst in ((1, T[1], C_SIN, rope2), (0, T[0], C_COS, rope1)):
                        wait(dve, ph, "qk_ps" if s == 0 else "rot_ps", i, 1)
                        dve.tensor_tensor(dst[:, :, :], tb[:, :].rearrange("p (k t) -> p k t", t=P),
                                          CONST[:, cc:cc + P].unsqueeze(1).to_broadcast([P, 2 * KC, P]),
                                          ALU.mult).then_inc(sems["rope_a" if s == 0 else "rope_b"], 1)
                    wait(dve, ph, "rope_a", i, 1)
                    wait(dve, ph, "rope_b", i, 1)
                    wait(dve, ph, "mv_sb", i)
                    wait(dve, ph, "s_ps", i)
                    dve.tensor_tensor(raw[:, :, :], rope1[:, KC:2 * KC, :], rope2[:, KC:2 * KC, :],
                                      ALU.add).then_inc(sems["k_sb"], 1)
                    for r_, rows in enumerate(HALVES):
                        ins = dve.tensor_tensor(stat[rows, :, r_, :], rope1[rows, 0:KC, :], rope2[rows, 0:KC, :], ALU.add)
                    ins.then_inc(sems["q_sb"], 1)
                if ph in (ROUTE0, ROUTE1):
                    wait(dve, ph, "xt_sb", i, 1)
                    wait(dve, ph, "ht_h", i)
                    wait(dve, ph, "ht", i)
                    dve.tensor_scalar(xm[:, :, :].bitcast(I32), xT[:, :, :].bitcast(I32), HIGH, None,
                                      ALU.bitwise_and).then_inc(sems["ht_m"], 1)
                    wait(dve, ph, "lg_ps", i, 1)
                    if ph is ROUTE0:
                        dve.tensor_tensor(at(lg0, i), logits(i)[:, 0:E0], R["rb"][:, :], ALU.add).then_inc(sems["lg_sb"], 1)
                    else:
                        dve.tensor_copy(at(lg1, i), logits(i)[:, 0:E1]).then_inc(sems["lg_sb"], 1)

            def feature_map(ph, i, part):
                if ph is not ATTN1:
                    return
                src = T[0][:, :].rearrange("p (h d) -> p h d", d=HD)

                def g(c_):
                    return R["gb"][:, c_ * HD:c_ * HD + HD].unsqueeze(1).to_broadcast([P, 2 * NH, HD])

                def per_head(k):
                    return fms[:, k, :].unsqueeze(2).to_broadcast([P, 2 * NH, HD])
                if part == 0:
                    wait(dve, ph, "qk_ps", i, 1)
                    wait(dve, ph, "fm_q", i)
                    wait(dve, ph, "yt_ps", i)
                    dve.tensor_tensor(fm1[:, :, :], src, g(0), ALU.mult).then_inc(sems["fm_g"], 1)
                    wait(dve, ph, "fm_g", i, 1)
                    dve.tensor_tensor(fm2[:, :, :], fm1[:, :, :], g(1), ALU.add).then_inc(sems["fm_b"], 1)
                    wait(dve, ph, "fm_b", i, 1)
                    dve.tensor_reduce(fms[:, 0, :], fm2[:, :, :], AX_X, ALU.add).then_inc(sems["fm_s"], 1)
                    wait(dve, ph, "fm_s", i, 1)
                    dve.scalar_tensor_tensor(fm1[:, :, :], in0=per_head(0), scalar=-1.0 / HD, in1=fm2[:, :, :],
                                             op0=ALU.mult, op1=ALU.add).then_inc(sems["fm_c"], 1)
                if part == 1:
                    wait(dve, ph, "fm_q", i, 1)
                    dve.tensor_reduce(fms[:, 1, :], fm2[:, :, :], AX_X, ALU.add).then_inc(sems["fm_v"], 1)
                    wait(dve, ph, "fm_v", i, 1)
                    dve.tensor_scalar(fms[:, 2, :], fms[:, 1, :], 1.0 / HD, EPS, ALU.mult, ALU.add).then_inc(sems["fm_e"], 1)
                if part == 2:
                    wait(dve, ph, "fm_p", i, 1)
                    dve.reciprocal(fms[:, 0, :], fms[:, 3, :]).then_inc(sems["fm_r"], 1)
                    wait(dve, ph, "fm_r", i, 1)
                    dve.tensor_tensor(fm1[:, :, :], fm1[:, :, :], per_head(0), ALU.mult).then_inc(sems["fm_y"], 1)

            def rule(ph):
                if ph is RULE0:
                    rule0(ph)
                else:
                    rule1(ph)

            def rule0(ph):
                dve.wait_ge(s_pinit, N_INIT)
                wait(dve, ph, "lg_e", 0, 1)
                dve.tensor_scalar(es[:, :, 0:7], ex[:, :, 0:7], 1.0, None, ALU.add).then_inc(sems["r1"], 1)
                wait(dve, ph, "r1", 0, 1)
                dve.reciprocal(p16[:, :, 0:7], es[:, :, 0:7]).then_inc(sems["r2"], 1)
                wait(dve, ph, "r2", 0, 1)
                for i in range(NB):
                    dve.max(m8[:, i, :], p16[:, i, :]).then_inc(sems["r3"], 1)
                wait(dve, ph, "r3", 0, NB)
                dve.tensor_copy(mr8[:, :, 0:2], m8[:, :, 0:2])
                dve.tensor_tensor(rsm[:, 0, :], m8[:, :, 0], m8[:, :, 1], ALU.add).then_inc(sems["r4"], 1)
                wait(dve, ph, "r4", 0, 1)
                for i in range(NB):
                    dve.match_replace(rep0[:, i, :], mr8[:, i, :], p16[:, i, :], 0.0)
                dve.reciprocal(rsm[:, 1, :], rsm[:, 0, :]).then_inc(sems["r5"], 1)
                wait(dve, ph, "r5", 0, 1)
                dve.tensor_tensor(sel[:, :, 0:E0], p16[:, :, 0:E0], rep0[:, :, 0:E0], ALU.subtract).then_inc(sems["r6"], 1)
                wait(dve, ph, "r6", 0, 1)
                dve.tensor_tensor(cbs0[:, :, 0:E0 - 1], sel[:, :, 0:E0 - 1],
                                  rsm[:, 1, :].unsqueeze(2).to_broadcast([P, NB, E0 - 1]), ALU.mult).then_inc(sems["cb"], 1)

            def rule1(ph):
                wait(dve, ROUTE1, "lg_sb", NB)
                for i in range(NB):
                    dve.max(m8[:, i, :], lg1[:, i, 0:64]).then_inc(sems["r1"], 1)
                wait(dve, ph, "r1", 0, NB)
                for i in range(NB):
                    ins = dve.match_replace(rep1[:, i, :], m8[:, i, :], lg1[:, i, 0:64], -3e38)
                ins.then_inc(sems["r2"], 1)
                dve.tensor_tensor(sel[:, :, :], lg1[:, :, 0:64], m8[:, :, 0:1].to_broadcast([P, NB, 64]),
                                  ALU.subtract).then_inc(sems["r3"], 1)
                wait(dve, ph, "r2", 0, 1)
                wait(dve, ph, "lg_e", 0, 1)
                dve.tensor_tensor(sel[:, :, :], lg1[:, :, 0:64], rep1[:, :, :], ALU.not_equal).then_inc(sems["r4"], 1)
                dve.tensor_scalar(rsm[:, 2, :], ex[:, :, 64], 1.0, None, ALU.add)
                wait(dve, ph, "r4", 0, 1)
                dve.tensor_tensor(es[:, :, :], ex[:, :, 0:64], sel[:, :, :], ALU.mult).then_inc(sems["r5"], 1)
                wait(dve, ph, "r5", 0, 1)
                dve.reciprocal(cbs1[:, :, 64], rsm[:, 2, :])
                dve.tensor_reduce(rsm[:, 0, :], es[:, :, :], AX_X, ALU.add).then_inc(sems["r6"], 1)
                wait(dve, ph, "r6", 0, 1)
                dve.reciprocal(rsm[:, 1, :], rsm[:, 0, :]).then_inc(sems["r7"], 1)
                wait(dve, ph, "r7", 0, 1)
                dve.tensor_tensor(cbs1[:, :, 0:64], es[:, :, :], rsm[:, 1, :].unsqueeze(2).to_broadcast([P, NB, 64]),
                                  ALU.mult).then_inc(sems["cb"], 1)

            def b(ph, i, h, after):
                if ph in (ROUTE0, ROUTE1):
                    return
                if ph is XATTN1:
                    if h:
                        return

                    if isinstance(i, int) and i == 0:
                        wait(dve, ph, "sub", i)
                    wait(dve, ph, "s_ps", i, 1)
                    wait(dve, ph, "exp", i)
                    dve.tensor_reduce(mxm[:, 0:1], S[:, 0:P], AX_X, ALU.max).then_inc(sems["mxr"], 1)
                    wait(dve, ph, "mxr", i, 1)
                    dve.tensor_scalar(mxm[:, 1:2], mxm[:, 0:1], -1.0 / 16, None, ALU.mult).then_inc(sems["mx"], 1)
                    return
                hs = slice(8 * h, 8 * h + 8)
                s_in = S[:, 1024 * h:1024 * h + 1024].rearrange("p (h t) -> p h t", h=8)
                wait(dve, ph, "s_ps", i, h + 1)
                if ph is ATTN1:
                    wait(dve, ph, "exp", i)
                    dve.tensor_tensor(SM[:, hs, :], s_in, tri.unsqueeze(1).to_broadcast([P, 8, P]),
                                      ALU.mult).then_inc(sems["sub"], 1)
                    return
                dve.tensor_reduce(mx[:, hs], s_in, AX_X, ALU.max).then_inc(sems["mx"], 1)
                if h and after:
                    reference_features(*after)
                wait(dve, ph, "mx", i, h + 1)
                wait(dve, ph, "exp", i)
                dve.tensor_tensor(SM[:, hs, :], s_in, mx[:, hs].unsqueeze(2).to_broadcast([P, 8, P]),
                                  ALU.subtract).then_inc(sems["sub"], 1)

            def c(ph, i, part):
                if ph in (ROUTE0, ROUTE1):
                    return
                if ph is XATTN1:
                    if part:
                        return
                    wait(dve, ph, "exp", i, 1)
                    wait(dve, ph, "z_sb", i)
                    dve.reciprocal(recm[:, 1:2], recm[:, 0:1]).then_inc(sems["rec"], 1)
                    wait(dve, ph, "rec", i, 1)
                    v = VALID[:, i:i + 1] if isinstance(i, int) else VALID[:, bass.ds(i, 1)]
                    dve.tensor_tensor(recm[:, 2:3], recm[:, 1:2], v, ALU.mult).then_inc(sems["rv"], 1)
                    return
                if part == 0:
                    if ph is not ATTN1:
                        wait(dve, ph, "pt_ps", i, 2)
                        dve.tensor_copy(PT[:, 4:8, :], T[0][:, :]).then_inc(sems["pt_d"], 1)
                    return
                ob = OB[:, 0:NH * (HD + 1)].rearrange("p (h d) -> p h d", h=NH)
                wait(dve, ph, "o_ps", i, 1)
                den = ob[:, :, HD:HD + 1]
                if ph is ATTN1:
                    dve.tensor_scalar(mx[:, :], den, EPS, None, ALU.add).then_inc(sems["ze"], 1)
                    wait(dve, ph, "ze", i, 1)
                    den = mx[:, :]
                dve.reciprocal(rec[:, :], den).then_inc(sems["rec"], 1)
                wait(dve, ph, "rec", i, 1)
                wait(dve, ph, "z_sb", i)
                dve.tensor_tensor(O[:, :].rearrange("p (h d) -> p h d", h=NH), ob[:, :, 0:HD],
                                  rec[:, :].unsqueeze(2).to_broadcast([P, NH, HD]), ALU.mult).then_inc(sems["o_sb"], 1)

            def layernorm(ph, i):
                wait(dve, ph, "z_sb", i, 1)
                dve.bn_stats(bst[:, :], z[:, :]).then_inc(sems["bst"], 1)
                wait(dve, ph, "bst", i, 1)
                apart(dve, "dve")
                dve.bn_aggr(bag[:, :], bst[:, :]).then_inc(sems["bag"], 1)
                wait(dve, ph, "bag", i, 1)
                dve.tensor_scalar(bve[:, :], bag[:, 1:2], EPS, None, ALU.add).then_inc(sems["bve"], 1)
                wait(dve, ph, "bpw", i, 1)
                dve.tensor_scalar(at(X, i), z[:, :], bag[:, 0:1], rstd[:, 0:1], ALU.subtract, ALU.mult).then_inc(sems["x_out"], 1)

            def d2(ph, i):
                if ph in (ROUTE0, ROUTE1):
                    return
                wait(dve, ph, "x_out", i)
                if ph is XATTN0:
                    wait(dve, ph, "o_sb", i, 1)
                    dve.tensor_tensor(z[:, :], O[:, :], at(X, i), ALU.add).then_inc(sems["z_sb"], 1)
                elif ph is XATTN1:
                    wait(dve, ph, "pr_ps", i, 1)
                    wait(dve, ph, "rv", i, 1)
                    dve.scalar_tensor_tensor(z[:, :], in0=OB[:, 0:D], scalar=recm[:, 2:3], in1=at(X, i),
                                             op0=ALU.mult, op1=ALU.add).then_inc(sems["z_sb"], 1)
                elif ph is ATTN0:
                    wait(dve, ph, "pr_ps", i, 1)
                    dve.scalar_tensor_tensor(z[:, :], in0=OB[:, 0:D], scalar=OUT0, in1=at(X, i),
                                             op0=ALU.mult, op1=ALU.add).then_inc(sems["z_sb"], 1)
                elif ph is MLA0:
                    wait(dve, ph, "pr_ps", i, 1)
                    wait(dve, ph, "hn", i)
                    dve.tensor_tensor(z[:, :], OB[:, 0:D], at(X, i), ALU.add).then_inc(sems["z_sb"], 1)
                    wait(dve, ph, "z_sb", i, 1)
                    dve.tensor_tensor(at(X, i), z[:, :], at(X, i), ALU.add).then_inc(sems["xh"], 1)
                    dve.tensor_tensor_reduce(out=junk[:, :], in0=z[:, :], in1=z[:, :], scale=1.0, scalar=0.0,
                                             op0=ALU.mult, op1=ALU.add, accum_out=hrm[:, 0:1]).then_inc(sems["hsq"], 1)
                    wait(dve, ph, "hsq", i, 1)
                    dve.tensor_scalar(hrm[:, 1:2], hrm[:, 0:1], 1.0 / D, EPS, ALU.mult, ALU.add).then_inc(sems["hms"], 1)
                    return
                else:
                    wait(dve, ph, "pr_ps", i, 1)
                    dve.tensor_tensor(z[:, :], OB[:, 0:D], at(X, i), ALU.add).then_inc(sems["z_sb"], 1)
                layernorm(ph, i)

            def experts(m, name):
                u0, b0 = m["u0"], m["u0"] // 2
                ub = [M, OB]

                def split(n, slot, k):
                    dve.wait_ge(s_blk[slot], landed(name, k))
                    if not isinstance(n, int) or n + b0 >= 1:
                        dve.wait_ge(s_bh, n + b0)
                        dve.wait_ge(s_bl, n + b0)
                    dve.tensor_scalar(blkm[:, :].bitcast(I32), blk[slot][:, :].bitcast(I32), HIGH, None,
                                      ALU.bitwise_and).then_inc(s_bm, 1)

                def unit(half, u, slot, k):
                    later = not isinstance(u, int) or u >= 2
                    dve.wait_ge(s_gu, u + 1)
                    dve.wait_ge(s_wb[slot], spread_in(name, k))
                    if later:
                        dve.wait_ge(s_hid, u - 1)
                    dve.scalar_tensor_tensor(hid0[half][:, :], in0=ub[half][:, :], scalar=m["scale"],
                                             in1=wb[slot][:, 512 * half:512 * half + 512],
                                             op0=ALU.mult, op1=ALU.mult).then_inc(s_h0, 1)
                    dve.wait_ge(s_h0, u + 1)
                    dve.wait_ge(s_sil, u + 1)
                    if later:
                        dve.wait_ge(s_hl, u - 1)
                    dve.tensor_tensor(hid[half][:, :], hid0[half][:, :], sil[half][:, :], ALU.mult).then_inc(s_hid, 1)
                    dve.wait_ge(s_hid, u + 1)
                    if later:
                        dve.wait_ge(s_hh, u - 1)
                    dve.tensor_scalar(hidm[half][:, :].bitcast(I32), hid[half][:, :].bitcast(I32), HIGH, None,
                                      ALU.bitwise_and).then_inc(s_hm, 1)
                    dve.wait_ge(s_hm, u + 1)
                    if later:
                        dve.wait_ge(s_dn, u - 1)
                    dve.tensor_tensor(hidl[half][:, :], hid[half][:, :], hidm[half][:, :], ALU.subtract).then_inc(s_hl, 1)

                blocks(dve, m, split, unit, early=True)
                if name == "moe0":
                    dve.wait_ge(s_mk, 16)
                    dve.tensor_copy(MK[:, :, :].rearrange("p b t -> p (b t)"), MKU[:, :].bitcast(U8)).then_inc(s_init, 1)
                    dve.wait_ge(s_init, 4)
                    dve.tensor_reduce(VALID[:, :], MK[:, :, :], AX_X, ALU.max)
                    dve.tensor_scalar(MKN[:, :, :], MK[:, :, :], -NEG, NEG, ALU.mult, ALU.add).then_inc(s_mk2, 1)

            def last(ph):
                m = MOES[ph.name]
                for h in range(2):
                    dve.wait_ge(s_dn, m["u0"] + 2 * m["n"] - 1 + h)
                    for i in range(4 * h, 4 * h + 4):
                        dve.tensor_tensor(Z[:, i, :], S[:, i * D:i * D + D], X[:, i, :], ALU.add).then_inc(sems["z_sb"], 1)
                    wait(dve, ph, "z_sb", 0, 4 * h + 4)
                    for i in range(4 * h, 4 * h + 4):
                        dve.bn_stats(bst8[:, i, :], Z[:, i, :]).then_inc(sems["bst"], 1)
                    wait(dve, ph, "bst", 0, 4 * h + 4)
                    for i in range(4 * h, 4 * h + 4):
                        dve.bn_aggr(bag8[:, i, :], bst8[:, i, :]).then_inc(sems["bag"], 1)
                    wait(dve, ph, "bag", 0, 4 * h + 4)
                    dve.tensor_scalar(bve8[:, 4 * h:4 * h + 4], bag8[:, 4 * h:4 * h + 4, 1], EPS, None, ALU.add).then_inc(sems["bve"], 1)
                for h in range(2):
                    wait(dve, ph, "bpw", 0, h + 1)
                    for i in range(4 * h, 4 * h + 4):
                        dve.tensor_scalar(X[:, i, :], Z[:, i, :], bag8[:, i, 0:1], rstd8[:, i:i + 1],
                                          ALU.subtract, ALU.mult).then_inc(sems["x_out"], 1)

            def turn(now, before, after, old):
                if now:
                    a1(*now)
                if before:
                    c(*before, 0)
                if after:
                    a0(*after)
                if after:
                    feature_map(*after, 0)
                if before and before[0] is ATTN1:
                    c(*before, 1)
                if now:
                    b(*now, 0, after)
                if after:
                    feature_map(*after, 1)
                if before and before[0] is not ATTN1:
                    c(*before, 1)
                if after:
                    feature_map(*after, 2)
                if now:
                    b(*now, 1, after)
                if before:
                    d2(*before)

            walk(turn, dve, rule, experts, last)

        @block.tensor
        def _(pe):
            pe.wait_ge(s_cst, 16)

            def mm(out_, lhsT, rhs, start=True, stop=True, **kw):
                return pe.matmul(out_, lhsT, rhs, start=start, stop=stop, **kw)

            def over_k(out_, lhsT, rhs):
                for k in range(KC):
                    ins = mm(out_, lhsT(k), rhs(k), start=(k == 0), stop=(k == KC - 1))
                return ins

            def a0(ph, i):
                wait(pe, ph, "xcur", i, 1)
                wait(pe, ph, "va_sb", i)
                if isinstance(i, int) and i < 2:
                    wait(pe, ph, "lg_sb", i)
                wait(pe, ph, "xt_sb", i)
                for k in range(KC):
                    ins = pe.transpose(M[:, k * P:k * P + P], xcur[:, k * P:k * P + P], ident)
                ins.then_inc(sems["xt_ps"], 1)

            def a1(ph, i):
                first = isinstance(i, int) and i == 0
                t0 = T[0][:, :].rearrange("p (k t) -> p k t", t=P)
                t1 = T[1][:, :].rearrange("p (k t) -> p k t", t=P)
                if ph is ATTN1:
                    return
                wait(pe, ph, "xt_sb", i, 1)
                if ph in (ROUTE0, ROUTE1):
                    n = E0 if ph is ROUTE0 else E1
                    w = wv("w_rt0" if ph is ROUTE0 else "w_rt1")
                    if first:
                        pe.wait_ge(s_w["d" if ph is ROUTE0 else "e"], NW["d" if ph is ROUTE0 else "e"])
                    if not first:
                        wait(pe, ph, "lg_sb", i)
                        wait(pe, ph, "z_sb", i, past=True)
                    over_k(logits(i)[:, 0:n], lambda k: xT[:, k, :], lambda k: w[:, k, :]).then_inc(sems["lg_ps"], 1)
                    return
                if ph is XATTN1:
                    cx = CTXT[:, :, i, :] if isinstance(i, int) else CTXT[:, :, bass.ds(i, 1), :]
                    wait(pe, ph, "exp", i)
                    if first:
                        wait(pe, ph, "sub", i)
                        pe.wait_ge(s_mk2, 1)
                    mk = MKN[:, i, :] if isinstance(i, int) else MKN[:, bass.ds(i, 1), :]
                    mm(S[:, 0:P], identb[:, :], mk, stop=False)
                    for k in range(KC):
                        ins = mm(S[:, 0:P], xT[:, k, :], cx[:, k], start=False, stop=(k == KC - 1))
                    ins.then_inc(sems["s_ps"], 1)
                    return
                if ph is ATTN0:
                    if first:
                        pe.wait_ge(s_w["a"], NW["a"])
                    w, v = wv("w0_qk"), wv("w0_v")
                    for c in range(4):
                        ins = over_k(t0[:, c, :], lambda k: w[:, k, c * P:c * P + P], lambda k: xT[:, k, :])
                    ins.then_inc(sems["qk_ps"], 1)
                if ph is XATTN0:
                    wait(pe, ph, "rf_sb", i, 1)
                    for k in range(KC):
                        ins = pe.transpose(M[:, k * P:k * P + P], rT[:, k, :], ident)
                    ins.then_inc(sems["rn_ps"], 1)
                    for n, wn in enumerate(("wx_q", "wx_k")):
                        w = wv(wn)
                        for c in range(KC):
                            ins = over_k(t0[:, KC * n + c, :], lambda k: w[:, k, c * P:c * P + P], lambda k: rT[:, KC * n + k, :])
                    ins.then_inc(sems["qk_ps"], 1)
                    v = wv("wx_v")
                    wait(pe, ph, "x_ref", i, 1)
                if ph is MLA0:
                    kx, kr, up = wv("wm_kx"), wv("wm_kr"), wv("wm_up", 3)
                    for c in range(KC):
                        over_k(t1[:, KC + c, :], lambda k: kr[:, k, c * P:c * P + P], lambda k: xT[:, k, :])
                    wait(pe, ph, "lat_sb", i, 1)
                    for c in range(KC):
                        ins = mm(t1[:, c, :], W["wm_qr"][:, c * P:c * P + P], latT[:, :])
                    ins.then_inc(sems["rot_ps"], 1)
                    for c in range(KC):
                        cs = slice(c * P, c * P + P)
                        for k in range(KC):
                            mm(t0[:, KC + c, :], kx[:, k, cs], xT[:, k, :], start=(k == 0), stop=False)
                        mm(t0[:, KC + c, :], up[:, 0, cs], latT[:, :], start=False)
                        ins = mm(t0[:, c, :], up[:, 1, cs], latT[:, :])
                    ins.then_inc(sems["qk_ps"], 1)
                    mm(M[:, 256:512], latT[:, :], up[:, 2, :]).then_inc(sems["v_ps"], 1)
                    return
                src = rT[:, KC:2 * KC, :] if ph is XATTN0 else xT[:, :, :]
                over_k(M[:, 256:512], lambda k: src[:, k, :], lambda k: v[:, k, :]).then_inc(sems["v_ps"], 1)

            def e(ph, i):
                first = isinstance(i, int) and i == 0
                if ph is XATTN0:
                    if first:
                        pe.wait_ge(s_w["b"], NW["b"])
                        pe.wait_ge(s_ctxt, 16)
                    w, t1 = wv("wx_fc"), T[1][:, :].rearrange("p (k t) -> p k t", t=P)
                    cx = CTXT[:, :, i, :] if isinstance(i, int) else CTXT[:, :, bass.ds(i, 1), :]
                    for c in range(KC):
                        over_k(t1[:, KC + c, :], lambda k: w[:, k, c * P:c * P + P], lambda k: cx[:, k])
                    wait(pe, ph, "xt_sb", i, 1)
                    for c in range(KC):
                        ins = over_k(t1[:, c, :], lambda k: w[:, k, c * P:c * P + P], lambda k: xT[:, k, :])
                    ins.then_inc(sems["rf_ps"], 1)
                if ph is MLA0:
                    if first:
                        pe.wait_ge(s_w["c"], NW["c"])
                    lt = wv("wm_lat")
                    wait(pe, ph, "xt_sb", i, 1)
                    over_k(M[:, 256:256 + P], lambda k: lt[:, k, :], lambda k: xT[:, k, :]).then_inc(sems["lat_ps"], 1)
                if ph is ATTN1:
                    if first:
                        pe.wait_ge(s_w["e"], NW["e"])
                    w, v = wv("w1_qk"), wv("w1_v")
                    wait(pe, ph, "xt_sb", i, 1)
                    wait(pe, ph, "fm_g", i)
                    over_k(T[0][:, :], lambda k: xT[:, k, :], lambda k: w[:, k, :]).then_inc(sems["qk_ps"], 1)
                    over_k(M[:, 256:512], lambda k: xT[:, k, :], lambda k: v[:, k, :]).then_inc(sems["v_ps"], 1)

            def y(ph, i):
                if ph is ATTN1:
                    wait(pe, ph, "fm_y", i, 1)
                    y = fm1[:, :, :].rearrange("p h d -> p (h d)")
                    for c in range(4):
                        ins = pe.transpose(T[1][:, c * P:c * P + P], y[:, c * P:c * P + P], ident)
                    ins.then_inc(sems["yt_ps"], 1)

            def b(ph, i, js):
                if ph in (ROUTE0, ROUTE1, XATTN1):
                    return
                wait(pe, ph, "mv_sb", i, js[0] // 2 + 1)
                if ph is MLA0:
                    wait(pe, ph, "q_sb", i, 1)
                    if isinstance(i, int) and i == 0:
                        pe.wait_ge(s_init, 2)
                else:
                    wait(pe, ph, "qk_a", i, 1)
                wait(pe, ph, "sub", i)
                if ph is ATTN1 and isinstance(i, int):
                    wait(pe, MOE0, "z_sb", 1)
                for j in js:
                    c, r = j // 2, j % 2
                    bank = S[:, 512 * j:512 * j + 512]
                    if ph is MLA0:
                        mm(bank, identb[:, :], negb[:, :].unsqueeze(1).to_broadcast([P, 4, P]), stop=False)
                    ins = mm(bank, stat[:, c, r, :], mv[:, c, :, :], start=ph is not MLA0)
                    if j % 2:
                        ins.then_inc(sems["s_ps"], 1)

            def c(ph, i, now, part):
                if ph in (ROUTE0, ROUTE1):
                    return
                if ph is XATTN1:
                    if part:
                        return
                    wait(pe, ph, "exp", i, 1)
                    pe.transpose(T[0][:, 0:P], PR[:, 0, :], ident).then_inc(sems["pt_ps"], 1)
                    cx = CTX[:, i, :] if isinstance(i, int) else CTX[:, bass.ds(i, 1), :]
                    if isinstance(i, int):
                        pe.wait_ge(s_ctx, 16)
                    wait(pe, ph, "pt_a", i, 1)
                    wait(pe, ph, "z_sb", i)
                    mm(OB[:, 0:D], PT[:, 0, :], cx).then_inc(sems["pr_ps"], 1)
                    return

                def pv(q):
                    if q == 0:
                        wait(pe, ph, "z_sb", i)
                        wait(pe, ph, "va_sb", i, 1)
                    if ph is ATTN1:
                        wait(pe, ph, "exp", i, q // 2 + 1)
                    else:
                        copied(q)
                    for h in range(4 * q, 4 * q + 4):
                        vv = VA[:, i, h, :] if isinstance(i, int) else VA[:, bass.ds(i, 1), h, :]
                        ins = mm(OB[:, 17 * h:17 * h + 17], PT[:, h, :], vv)
                    if q == 3:
                        ins.then_inc(sems["o_ps"], 1)

                def copied(q):
                    wait(pe, ph, "pt_d" if q == 1 else "pt_a", i, (1, 1, 2, 3)[q])

                def pt(q):
                    if q % 2 == 0:
                        wait(pe, ph, "exp", i, q // 2 + 1)
                    if q < 2:
                        free(now, q)
                    else:
                        copied(q - 2)
                    for h in range(4):
                        ins = pe.transpose(T[1 - q % 2][:, h * P:h * P + P], PR[:, 4 * q + h, :], ident)
                    ins.then_inc(sems["pt_ps"], 1)

                if ph is ATTN1:
                    pv(2 * part)
                    pv(2 * part + 1)
                elif part == 0:
                    pt(0)
                    pt(1)
                    pv(0)
                    pt(2)
                elif part == 1:
                    pv(1)
                    pt(3)
                else:
                    pv(2)
                    pv(3)

            def free(now, q):
                if now:
                    ph, i = now
                    if q:
                        wait(pe, ph, "qk_a", i, 1)
                        wait(pe, ph, "rope_a", i, 1)
                    else:
                        wait(pe, ph, "rope_b", i, 1)

            def d1(ph, i, after):
                if "ot_ps" not in ph.fires:
                    return
                if after:
                    ph2, i2 = after
                    wait(pe, ph2, "xt_sb", i2, 1)
                    if ph2 is MLA0:
                        wait(pe, ph2, "lat_sb", i2, 1)
                    if ph2 is ATTN1:
                        wait(pe, ph2, "va_sb", i2, 1)
                wait(pe, ph, "o_sb", i, 1)
                for k in range(KC):
                    ins = pe.transpose(M[:, k * P:k * P + P], O[:, k * P:k * P + P], ident)
                ins.then_inc(sems["ot_ps"], 1)

            def d2(ph, i):
                if "ot_ps" not in ph.fires:
                    return
                w = wv({"attn0": "w0_o", "mla0": "wm_o", "attn1": "w1_o"}[ph.name])
                wait(pe, ph, "ot_sb", i, 1)
                over_k(OB[:, 0:D], lambda k: OT[:, k, :], lambda k: w[:, k, :]).then_inc(sems["pr_ps"], 1)

            def rule(ph):
                cbs = cbs0 if ph is RULE0 else cbs1
                wait(pe, ph, "cb", 0, 1)
                wait(pe, ph, "z_sb", 0, past=True)
                for i in range(NB):
                    bank = (OB, T[0])[i // 4]
                    ins = pe.transpose(bank[0:cbs.shape[2], i % 4 * P:i % 4 * P + P], cbs[:, i, :], ident)
                    if i % 4 == 3:
                        ins.then_inc(sems["cbt_ps"], 1)

            def experts(m, name):
                u0, n_blocks, prev = m["u0"], m["n"], m["prev"]
                ub = [M, OB]
                wait(pe, prev, "ht", NB)
                wait(pe, prev, "ht_h", NB)
                wait(pe, prev, "lg_sb", NB)
                wait(pe, m["rule"], "cbt_sb", 0, 2)
                wait(pe, m["ph"], "z_sb", 0)
                wait(pe, m["ph"], "sub", 0)

                def parts3(out_, left, right, start=True, stop=True, **kw):
                    (lh, ll), (rh, rl) = left, right
                    mm(out_, lh, rl, start=start, stop=False, **kw)
                    mm(out_, lh, rh, start=False, stop=False, **kw)
                    return mm(out_, ll, rh, start=False, stop=stop, **kw)

                def gate_up(half, u, slot, n):
                    if half == 0:
                        pe.wait_ge(s_bh, n + (u0 // 2 + 1))
                        pe.wait_ge(s_bl, n + (u0 // 2 + 1))
                    if not isinstance(u, int) or u >= 2:
                        pe.wait_ge(s_sil, u - 1)
                        pe.wait_ge(s_h0, u - 1)
                    w = [b[slot][:, 0:512].rearrange("p (g k n) -> p g k n", g=2, k=KC) for b in (blkh, blkl)]
                    for g, bank in ((1, ub[half]), (0, T[half])):
                        for k in range(KC):
                            ins = parts3(bank[:, :], [w_[:, g, k, :] for w_ in w],
                                         [h_[:, k, 4 * half:4 * half + 4, :] for h_ in (HTh, HTl)],
                                         start=(k == 0), stop=(k == KC - 1))
                    ins.then_inc(s_gu, 1)

                def down(half, u, slot):
                    pe.wait_ge(s_hh, u + 1)
                    pe.wait_ge(s_hl, u + 1)
                    for t in range(4):
                        tok = 4 * half + t
                        ins = parts3(S[:, D * tok:D * tok + D], [h_[half][:, t * P:t * P + P] for h_ in (hidh, hidl)],
                                     [b[slot][:, 512:768] for b in (blkh, blkl)],
                                     start=False, stop=False, skip_group_check=True)
                    ins.then_inc(s_dn, 1)

                for j in range(4):
                    mm(S[:, 512 * j:512 * j + 512], identb[:, :], zerob[:, :], stop=False, skip_group_check=True)
                gate_up(0, u0, 0, 0)
                gate_up(1, u0 + 1, 0, 0)
                down(0, u0, 0)
                with pe.Fori(0, (n_blocks - 1) // 2) as j:
                    for k in range(4):
                        slot, half = 1 - k // 2, k % 2
                        u = j * 4 + (u0 + 2 + k)
                        gate_up(half, u, slot, j * 2 + (1 + k // 2))
                        down(1 - half, j * 4 + (u0 + 1 + k), (0, 1, 1, 0)[k])
                if n_blocks % 2 == 0:
                    u = u0 + 2 * (n_blocks - 1)
                    gate_up(0, u, 1, n_blocks - 1)
                    down(1, u - 1, 0)
                    gate_up(1, u + 1, 1, n_blocks - 1)
                    down(0, u, 1)
                    down(1, u + 1, 1)
                else:
                    down(1, u0 + 2 * n_blocks - 1, 0)

            def turn(now, before, after, old):
                early = after and after[0] is ATTN1
                router = after and now and now[0] in (ROUTE0, ROUTE1) and not (isinstance(now[1], int) and now[1] == 0)
                if router:
                    a0(*after)
                if now:
                    a1(*now)
                    y(*now)
                if early:
                    a0(*after)
                if before:
                    c(*before, now, 0)
                if early:
                    e(*after)
                elif now:
                    b(*now, (0,))
                if before:
                    c(*before, now, 1)
                if early:
                    if now:
                        b(*now, (0, 1))
                    if before:
                        d1(*before, after)
                    if now:
                        b(*now, (2, 3))
                else:
                    if now:
                        b(*now, (1,))
                    if before and before[0] is not ATTN1:
                        c(*before, now, 2)
                    if after and not router:
                        a0(*after)
                    if after and after[0] is XATTN0:
                        e(*after)
                    if now:
                        b(*now, (2,))
                    if after and after[0] is MLA0:
                        e(*after)
                    if now:
                        b(*now, (3,))
                if before:
                    if not early:
                        d1(*before, after)
                    d2(*before)

            walk(turn, pe, rule, experts)


def constants():
    c = np.zeros((P, C_END), np.float32)
    p, t = np.arange(P)[:, None], np.arange(P)[None, :]
    c[:, C_ID:C_ID + P] = p == t
    c[:, C_TRI:C_TRI + P] = p <= t
    c[:, C_NEG:C_NEG + P] = np.where(t > p, np.float32(NEG), np.float32(0))
    inv = np.float32(1) / np.power(np.float32(10000), np.arange(0, RD, 2, dtype=np.float32) / np.float32(RD))
    ang = np.outer(np.arange(P, dtype=np.float32), inv.astype(np.float32)).astype(np.float32)
    emb = np.concatenate([ang, ang], axis=-1).T
    for row in range(P):
        d = row % HD
        if d < RD:
            c[row, C_COS:C_COS + P] = 1
        else:
            c[row, C_COS:C_COS + P] = np.cos(emb[d - RD])
            c[row, C_SIN:C_SIN + P] = np.sin(emb[d - RD]) * (-1 if d - RD < RD // 2 else 1)
        c[row, C_MASK + row % 64 // HD] = 1
        c[row, C_SEL + (0 if d < RD else 1)] = np.float32(8 ** -0.5) if d < RD else 1
    return c


def kernel(**inputs):
    import concourse.bacc as bacc
    from concourse.bass_utils import run_bass_kernel_spmd as run

    a = {n: np.asarray(v) for n, v in inputs.items()}

    def chunks(w):
        return np.ascontiguousarray(w.reshape(-1, P, w.shape[1]).transpose(1, 0, 2).reshape(P, -1))

    def row(*vs):
        return np.ascontiguousarray(np.concatenate([v.reshape(-1) for v in vs])[None, :])

    h, d = np.arange(NH)[:, None], np.arange(HD)[None, :]
    half = HD // 2
    q_cols = np.where(d < half, h * half + d, 256 + h * half + d - half).reshape(-1)
    wa = a["L0_attn_W_attn"]
    rope = (h * RD + d - RD)[:, RD:]
    swap = np.concatenate([rope[:, RD // 2:], rope[:, :RD // 2]], axis=1)

    def spread(plain, roped, order):
        src = plain if plain is not None else roped
        w = np.zeros((src.shape[0], NH, HD), np.float32)
        if plain is not None:
            w[:, :, :RD] = plain.reshape(-1, NH, RD)
        if roped is not None:
            w[:, :, RD:] = roped[:, order]
        return w.reshape(-1, D)

    kr, qr = a["L0_ffn_rope_k_w"], a["L0_ffn_rope_q_w"]
    up = np.zeros((P, 3, D), np.float32)
    up[:LAT, 0] = spread(a["L0_ffn_k_u_w"], None, None)
    up[LAT:, 1] = spread(a["L0_ffn_q_u_w"], qr, rope)
    up[:LAT, 2] = a["L0_ffn_v_u_w"]
    qrot = np.zeros((P, D), np.float32)
    qrot[LAT:] = spread(None, qr, swap)
    cols = np.zeros((P, 16), np.float32)
    for n, name in enumerate(["L0_ffn_ln1_w", "L0_ffn_ln2_w", "L0_xattn_b_q", "L0_xattn_b_k", "L0_xattn_b_fc"]):
        cols[:, 2 * n:2 * n + 2] = a[name].reshape(KC, P).T
    rt0 = np.zeros((D, E0), np.float32)
    rt0[:, :7] = a["L0_ffn_router_w"]
    rb = np.zeros((E0,), np.float32)
    rb[:7] = a["L0_ffn_router_b"]

    def block(gate, upw, down):
        return np.concatenate([chunks(gate), chunks(upw), down], axis=1)

    blocks0 = np.stack([block(a["L0_ffn_sh_gate"], a["L0_ffn_sh_up"], a["L0_ffn_sh_down"])] +
                       [block(a["L0_ffn_r_gate"][e], a["L0_ffn_r_up"][e], a["L0_ffn_r_down"][e]) for e in range(7)])
    gu, dn = a["L1_ffn_gate_up_proj"], a["L1_ffn_down_proj"]
    none = np.zeros((D, 64), np.float32)
    shared = block(np.concatenate([a["L1_ffn_shared_gate_w"].T, none], axis=1),
                   np.concatenate([a["L1_ffn_shared_up_w"].T, none], axis=1),
                   np.concatenate([a["L1_ffn_shared_down_w"].T, none.T], axis=0))
    blocks1 = np.stack([shared] + [
        block(np.concatenate([gu[e, :64].T, gu[e + 1, :64].T], axis=1),
              np.concatenate([gu[e, 64:].T, gu[e + 1, 64:].T], axis=1),
              np.concatenate([dn[e].T, dn[e + 1].T], axis=0)) for e in range(0, 64, 2)])

    arrays = {
        "x": a["x"], "ctx": a["ctx_2048"], "ctxT": a["ctx_2048"].reshape(-1, D).T,
        "mask": a["mask_BxS2_bk0"].reshape(1, -1).view(np.int32), "consts": constants(),
        "row_lam": row(a["L0_attn_lambda_q1"], a["L0_attn_lambda_k1"], a["L0_attn_lambda_q2"], a["L0_attn_lambda_k2"]),
        "row_bv": row(a["L0_xattn_b_v"]), "row_rb": row(rb), "row_gb": row(a["L1_attn_gamma"], a["L1_attn_beta"]),
        "w0_qk": chunks(np.concatenate([wa[:, q_cols], wa[:, q_cols + 128]], axis=1)),
        "w0_v": chunks(wa[:, 512:]), "w0_o": chunks(a["L0_attn_W_proj"]),
        "wx_fc": chunks(a["L0_xattn_W_fc"].T), "wx_q": chunks(a["L0_xattn_W_q"].T), "wx_k": chunks(a["L0_xattn_W_k"].T),
        "wx_v": chunks(a["L0_xattn_W_v"].reshape(D, D).T),
        "wm_lat": chunks(np.concatenate([a["L0_ffn_kv_d_w"], a["L0_ffn_q_d_w"]], axis=1)),
        "wm_kx": chunks(spread(None, kr, rope)), "wm_kr": chunks(spread(None, kr, swap)),
        "wm_up": up.reshape(P, -1), "wm_qr": qrot, "wm_o": chunks(a["L0_ffn_o_w"]), "w_rt0": chunks(rt0), "cols": cols,
        "w1_qk": chunks(np.concatenate([a["L1_attn_Wq"].T, a["L1_attn_Wk"].T], axis=1)),
        "w1_v": chunks(a["L1_attn_Wv"].T), "w1_o": chunks(a["L1_attn_Wo"].T),
        "w_rt1": chunks(np.concatenate([a["L1_ffn_router_w"].T, a["L1_ffn_shared_expert_gate_w"].T], axis=1)),
        "blocks0": blocks0, "blocks1": blocks1,
    }
    nc = bacc.Bacc("TRN2", target_bir_lowering=False, num_devices=1)
    arrays = {n: np.ascontiguousarray(v) for n, v in arrays.items()}
    t_in = {n: nc.dram_tensor("in_" + n, v.shape, mybir.dt.from_np(v.dtype), kind="ExternalInput").ap()
            for n, v in arrays.items()}
    out = nc.dram_tensor("out_0", (NB, P, D), F32, kind="ExternalOutput").ap()
    build(nc, t_in, out)
    r = run(nc, [{"in_" + n: v for n, v in arrays.items()}], core_ids=[0])
    return r.results[0]["out_0"]
```

```python
from contextlib import ExitStack

import numpy as np

import concourse.bass as bass
from concourse import mybir

F32 = mybir.dt.float32
BF16 = mybir.dt.bfloat16
F32R = mybir.dt.float32r
I32 = mybir.dt.int32
U8 = mybir.dt.uint8
ALU = mybir.AluOpType
ACT = mybir.ActivationFunctionType
AX_X = mybir.AxisListType.X

P = 128
NB = 8
D = 256
KC = D // P
NH = 16
HD = D // NH
EPS = 1e-5
NEG = -1e30
LAT = 64
RD = 8
E0, E1 = 8, 65
BLK = 768
HIGH = -4096
OUT0 = 0.8

C_ID, C_TRI, C_NEG, C_COS, C_SIN, C_MASK, C_SEL, C_R = 0, 128, 256, 384, 512, 640, 644, 646
C_END = 646 + 16

WEIGHTS = {
    "w0_qk": KC * 512, "w0_v": KC * D, "w0_o": KC * D,
    "wx_fc": KC * D, "wx_q": KC * D, "wx_k": KC * D, "wx_v": KC * D,
    "wm_lat": KC * P, "wm_kx": KC * D, "wm_kr": KC * D, "wm_up": 3 * D, "wm_qr": D, "wm_o": KC * D,
    "w_rt0": KC * E0,
    "w1_qk": KC * 512, "w1_v": KC * D, "w1_o": KC * D, "w_rt1": KC * E1,
    "cols": 16,
}
ROWS = {"lam": 4 * D, "bv": D, "rb": E0, "gb": 2 * HD}


class Phase:
    total = {}

    def __init__(self, name, fires, turns=NB):
        self.name, self.fires = name, fires
        self.base = dict(Phase.total)
        for s, n in fires.items():
            Phase.total[s] = Phase.total.get(s, 0) + n * turns


def build(nc, t_in, out):
    Phase.total = {}
    common = {"xcur": 1, "xt_ps": 1, "xt_sb": 1}
    attn = dict(common, qk_ps=1, v_ps=1, va_sb=1, mv_sb=2, s_ps=2, o_ps=1, rec=1, o_sb=1,
                z_sb=1)
    norm = dict(bst=1, bag=1, bve=1, bpw=1, x_out=1)
    soft = dict(attn, mx=2, sub=2, exp=2, pt_ps=4, pt_a=3, pt_d=1)
    proj = dict(ot_ps=1, ot_sb=1, pr_ps=1)
    ATTN0 = Phase("attn0", dict(soft, **norm, k_a=1, qk_a=1, **proj))
    XATTN0 = Phase("xattn0", dict(soft, **norm, k_a=1, qk_a=1, rf_ps=1, rf_sb=1, rn_ps=1, xbv=1, x_ref=1))
    MLA0 = Phase("mla0", dict(soft, rms_e=1, rms_p=1, xc0=1, lat_ps=1, lat_sb=1, rot_ps=1, rope_a=1, rope_b=1, k_sb=1, q_sb=1,
                              hsq=1, hms=1, hpw=1, hn=1, xh=1, **proj))
    ROUTE0 = Phase("route0", dict(rc=1, rt_ps=1, rt_sb=1, ht_m=1, ht_h=1, ht=1, lg_ps=1, lg_sb=1))
    RULE0 = Phase("rule0", dict(lg_e=1, r1=1, r2=1, r3=8, r4=1, r5=1, r6=1, cb=1, cbt_ps=2, cbt_sb=2), turns=1)
    MOE0 = Phase("moe0", dict(bst=8, bag=8, bve=2, bpw=2, x_out=8), turns=1)
    ATTN1 = Phase("attn1", dict(attn, **norm, fm_g=1, fm_b=1, fm_s=1, fm_c=1, fm_q=1, fm_v=1, fm_e=1, fm_p=1, fm_r=1, fm_y=1, yt_ps=1,
                                k_a=1, qk_a=1, sub=2, exp=2, ze=1, **proj))
    XATTN1 = Phase("xattn1", dict(common, s_ps=1, mxr=1, mx=1, exp=1, pt_ps=1, pt_a=1, pr_ps=1, rec=1, rv=1,
                                  z_sb=1, bst=1, bag=1, bve=1, bpw=1, x_out=1))
    ROUTE1 = Phase("route1", dict(rc=1, rt_ps=1, rt_sb=1, ht_m=1, ht_h=1, ht=1, lg_ps=1, lg_sb=1))
    RULE1 = Phase("rule1", dict(lg_e=1, r1=8, r2=1, r3=1, r4=1, r5=1, r6=1, r7=1, cb=1, cbt_ps=2, cbt_sb=2), turns=1)
    MOE1 = Phase("moe1", dict(bst=8, bag=8, bve=2, bpw=2, x_out=8), turns=1)

    ctx = ExitStack()
    with ctx:
        def sb(name, shape, dt=F32):
            return ctx.enter_context(nc.sbuf_tensor(name, shape, dt))

        def sem(name):
            return ctx.enter_context(nc.semaphore(name))

        X = sb("X", [P, NB, D])
        H = sb("H", [P, NB, D])
        CTX = sb("CTX", [P, NB, D])
        CTXT = sb("CTXT", [P, KC, NB, P])
        HTh, HTl = sb("HTh", [P, KC, NB, P], F32R), sb("HTl", [P, KC, NB, P], F32R)
        xm = sb("xm", [P, KC, P])
        VA = sb("VA", [P, NB, NH, HD + 1])
        W = {n: sb(n, [P, c]) for n, c in WEIGHTS.items()}
        R = {n: sb("row_" + n, [P, c]) for n, c in ROWS.items()}
        CONST = sb("CONST", [P, C_END])
        MKU = sb("MKU", [P, NB * P // 4], mybir.dt.int32)
        MK = sb("MK", [P, NB, P])
        MKN = sb("MKN", [P, NB, P], BF16)
        VALID = sb("VALID", [P, NB])
        loaded = sb("loaded", [P, 3])
        identb = sb("identb", [P, P], BF16)
        negb = sb("negb", [P, P], BF16)
        neghalf = sb("neghalf", [P, 32])
        lam = sb("lam", [P, 8])
        qscale = sb("qscale", [P, 1])
        junk = sb("junk", [P, D])
        xcur = sb("xcur", [P, D])
        junk_a = sb("junk_a", [P, D])
        xT = sb("xT", [P, KC, P])
        rcur, rtT = sb("rcur", [P, D]), sb("rtT", [P, KC, P])
        rT = sb("rT", [P, 2 * KC, P])
        latT = sb("latT", [P, P])
        stat = sb("stat", [P, KC, 2, P])
        raw = sb("raw", [P, KC, P])
        rope1 = sb("rope1", [P, 2 * KC, P])
        rope2 = sb("rope2", [P, 2 * KC, P])
        mv = sb("mv", [P, KC, 4, P])
        SM = sb("SM", [P, NH, P])
        PR = sb("PR", [P, NH, P])
        PT = sb("PT", [P, NH, P])
        mx = sb("mx", [P, NH])
        rec = sb("rec", [P, NH])
        mxm = sb("mxm", [P, 2])
        recm = sb("recm", [P, 4])
        O = sb("O", [P, D])
        OT = sb("OT", [P, KC, P])
        z = sb("z", [P, D])
        bst = sb("bst", [P, 6])
        bag = sb("bag", [P, 2])
        bve = sb("bve", [P, 1])
        rstd = sb("rstd", [P, 1])
        bst8 = sb("bst8", [P, NB, 6])
        bag8 = sb("bag8", [P, NB, 2])
        bve8 = sb("bve8", [P, NB])
        rstd8 = sb("rstd8", [P, NB])
        rms = sb("rms", [P, 4])
        hrm = sb("hrm", [P, 4])
        fm1 = sb("fm1", [P, 2 * NH, HD])
        fm2 = sb("fm2", [P, 2 * NH, HD])
        fms = sb("fms", [P, 4, 2 * NH])
        lg0, lg1 = sb("lg0", [P, NB, E0]), sb("lg1", [P, NB, E1])
        p16 = sb("p16", [P, NB, 16])
        mr8 = sb("mr8", [P, NB, 8])
        m8 = sb("m8", [P, NB, 8])
        rep0, rep1 = sb("rep0", [P, NB, 16]), sb("rep1", [P, NB, 64])
        sel = sb("sel", [P, NB, 64])
        ex = sb("ex", [P, NB, E1])
        es = sb("es", [P, NB, 64])
        rsm = sb("rsm", [P, 4, NB])
        cbs0, cbs1 = sb("cbs0", [P, NB, E0]), sb("cbs1", [P, NB, E1])
        cbT = sb("cbT", [E1, NB, P])
        blk = [sb(f"blk{k}", [P, BLK]) for k in range(2)]
        def lent(buf, k, n):
            return buf[:, :, :].rearrange("p h t -> p (h t)")[:, k * n:k * n + n]
        wb = [lent(PR, k, NB * P) for k in range(2)]
        sil, hid0 = [lent(SM, k, 512) for k in (0, 1)], [lent(SM, k, 512) for k in (2, 3)]
        hid, hidm = [lent(PT, k, 512) for k in (0, 1)], [lent(PT, k, 512) for k in (2, 3)]
        hidh = [sb(f"hidh{k}", [P, 512], F32R) for k in range(2)]
        hidl = [sb(f"hidl{k}", [P, 512], F32R) for k in range(2)]
        blkm = mv[:, :, :, :].rearrange("p k h t -> p (k h t)")[:, 0:BLK]
        blkh = [sb(f"blkh{k}", [P, BLK], F32R) for k in range(2)]
        blkl = [sb(f"blkl{k}", [P, BLK], F32R) for k in range(2)]

        S = ctx.enter_context(nc.psum_tensor("S", [P, 2048], F32))
        T = [ctx.enter_context(nc.psum_tensor(f"T{k}", [P, 512], F32)) for k in range(2)]
        M = ctx.enter_context(nc.psum_tensor("M", [P, 512], F32))
        OB = ctx.enter_context(nc.psum_tensor("OB", [P, 512], F32))

        N_INIT = 19
        HALVES = (slice(0, 64), slice(64, P))
        ident = CONST[:, C_ID:C_ID + P]
        tri = CONST[:, C_TRI:C_TRI + P]
        names = sorted(Phase.total)
        sems = {n: sem("s_" + n) for n in names}
        s_x0, s_x1, s_ctxt, s_ctx, s_cst, s_row = sem("s_x0"), sem("s_x1"), sem("s_ctxt"), sem("s_ctx"), sem("s_cst"), sem("s_row")
        s_w = {n: sem("s_w_" + n) for n in ("a", "b", "c", "d", "e")}
        s_mk, s_mk2 = sem("s_mk"), sem("s_mk2")
        s_init, s_pinit, s_lam, s_lame = sem("s_init"), sem("s_pinit"), sem("s_lam"), sem("s_lame")
        s_cbd, s_out = [sem("s_cbd0"), sem("s_cbd1")], sem("s_out")
        s_blk = [sem("s_blk0"), sem("s_blk1")]
        s_wb = [sem("s_wb0"), sem("s_wb1")]
        s_bm, s_bh, s_bl = sem("s_bm"), sem("s_bh"), sem("s_bl")
        s_hm, s_hh, s_hl = sem("s_hm"), sem("s_hh"), sem("s_hl")
        s_gu, s_sil, s_h0, s_hid, s_dn = sem("s_gu"), sem("s_sil"), sem("s_h0"), sem("s_hid"), sem("s_dn")

        WGROUP = {"w0_qk": "a", "w0_v": "a", "w0_o": "a", "wx_fc": "b", "wx_q": "b", "wx_k": "b", "wx_v": "b",
                  "cols": "b", "wm_lat": "c", "wm_kx": "c", "wm_kr": "c", "wm_up": "c", "wm_qr": "c", "wm_o": "c",
                  "w_rt0": "d", "w1_qk": "e", "w1_v": "e", "w1_o": "e", "w_rt1": "e"}
        NW = {g: 16 * sum(1 for v in WGROUP.values() if v == g) for g in "abcde"}

        def wait(eng, ph, s, i, k=0, past=False):
            per = ph.fires.get(s, 0)
            if per == 0 and (k or not (isinstance(i, int) or past)):
                return
            if per == 0:
                i = 0
            v = ph.base.get(s, 0) + per * i + k
            if isinstance(v, int) and v <= 0:
                return
            eng.wait_ge(sems[s], v)

        s_apart = {"dve": sem("s_apart_dve"), "pool": sem("s_apart_pool"), "act": sem("s_apart_act")}

        def apart(eng, who):
            eng.sem_inc(s_apart[who], 1)

        def at(buf, i):
            return buf[:, i, :] if isinstance(i, int) else buf[:, bass.ds(i, 1), :]

        def router(old):
            if old and old[0] in (MLA0, XATTN1):
                return (ROUTE0 if old[0] is MLA0 else ROUTE1, old[1])

        def router_bank(ph):
            return M if ph is ROUTE0 else T[1]

        def readout(before, old):
            return bool(before and before[0] is XATTN1) or bool(old and old[0] is XATTN1)

        def wv(n, k=KC):
            return W[n][:, :].rearrange("p (k n) -> p k n", k=k)

        def col(c):
            return W["cols"][:, c:c + 1]

        XT_SCALE = {"mla0": 0, "route0": 2}
        QB, KB, FB = 4, 6, 8

        D0 = nc.dram_tensor("route0_w", (E0, NB * P), F32, kind="Internal").ap()
        D1 = nc.dram_tensor("route1_w", (E1, NB * P), F32, kind="Internal").ap()

        block = ctx.enter_context(nc.Block())

        MOES = {
            "moe0": dict(ph=MOE0, prev=ROUTE0, rule=RULE0, w=t_in["blocks0"], dram=D0, cols=E0, n=8, scale=0.125, u0=0, dmas=1),
            "moe1": dict(ph=MOE1, prev=ROUTE1, rule=RULE1, w=t_in["blocks1"], dram=D1, cols=E1, n=33, scale=1.0, u0=16, dmas=2),
        }
        BEFORE = {"moe0": 0, "moe1": MOES["moe0"]["n"] // 2 * MOES["moe0"]["dmas"]}

        def spread_in(name, k, slot):
            m = MOES[name]
            before = 16 * (BEFORE[name] - (slot == 0))
            return before + 16 * m["dmas"] * k if isinstance(k, int) else k * (16 * m["dmas"]) + before

        def landed(name, k):
            k0 = MOES[name]["u0"] // 4
            return (k0 + k) * 16 if isinstance(k, int) else k * 16 + 16 * k0

        @block.sync
        def _(sp):
            sp.dma_start(CONST[:, :], t_in["consts"]).then_inc(s_cst, 16)
            sp.dma_start(X[:, 0:2, :], t_in["x"].rearrange("b t d -> t b d")[:, 0:2, :]).then_inc(s_x0, 16)

            def weights(g):
                for n, gg in WGROUP.items():
                    if gg == g:
                        sp.dma_start(W[n][:, :], t_in[n]).then_inc(s_w[g], 16)
            weights("a")
            for n in ROWS:
                sp.dma_start(R[n][:, :], t_in["row_" + n].to_broadcast([P, ROWS[n]])).then_inc(s_row, 16)
            sp.dma_start(X[:, 2:NB, :], t_in["x"].rearrange("b t d -> t b d")[:, 2:NB, :]).then_inc(s_x1, 16)
            weights("b")
            sp.dma_start(CTXT[:, :, :, :].rearrange("p k b t -> p k (b t)"),
                         t_in["ctxT"].rearrange("(k p) n -> p k n", p=P)).then_inc(s_ctxt, 16)
            weights("c")
            weights("d")
            weights("e")
            sp.dma_start(CTX[:, :, :], t_in["ctx"].rearrange("b t d -> t b d")).then_inc(s_ctx, 16)
            sp.dma_start(MKU[:, :], t_in["mask"].to_broadcast([P, NB * P // 4])).then_inc(s_mk, 16)

            def moe(name, which):
                m = MOES[name]
                dr, u0, n_blocks = m["dram"], m["u0"], m["n"]

                def load_w(n, slot):
                    src = m["w"][n] if isinstance(n, int) else m["w"][bass.ds(n, 1), :, :]
                    sp.dma_start(blk[slot][:, :], src).then_inc(s_blk[slot], 16)

                def load_b(n, slot):
                    def spread(e, p0, np_):
                        row = dr[e:e + 1, :] if isinstance(e, int) else dr[bass.ds(e, 1), :]
                        sp.dma_start(wb[slot][p0:p0 + np_, :], row.to_broadcast([np_, NB * P])).then_inc(s_wb[slot], 16)
                    first = isinstance(n, int) and n == 0
                    if which == 0:
                        spread(n - 1, 0, P)
                    else:
                        spread(E1 - 1 if first else n * 2 - 2, 0, 64)
                        spread(E1 - 1 if first else n * 2 - 1, 64, 64)

                if which == 1:
                    sp.wait_ge(s_bh, u0 // 2)
                    sp.wait_ge(s_bl, u0 // 2)
                    sp.wait_ge(s_hid, u0)
                load_w(0, 0)
                load_w(1, 1)
                wait(sp, m["rule"], "cbt_sb", 0, 2)
                sp.dma_start(dr.rearrange("e (b t) -> e b t", b=NB), cbT[0:m["cols"], :, :]).then_inc(s_cbd[which], 16)
                sp.wait_ge(s_cbd[which], 16)
                if which == 1:
                    load_b(0, 0)
                load_b(1, 1)
                def reload(n, slot, split, used):
                    sp.wait_ge(s_bm, split)
                    sp.wait_ge(s_bl, split)
                    load_w(n, slot)
                    sp.wait_ge(s_hid, used)
                    load_b(n, slot)

                with sp.Fori(0, (n_blocks - 2) // 2) as j:
                    for k in range(2):
                        reload(j * 2 + (2 + k), k, j * 2 + (u0 // 2 + 1 + k), j * 4 + (u0 + 2 + 2 * k))
                if n_blocks % 2:
                    reload(n_blocks - 1, 0, u0 // 2 + n_blocks - 2, u0 + 2 * (n_blocks - 2))

            moe("moe0", 0)
            moe("moe1", 1)
            for i in range(0, NB, 2):
                wait(sp, MOE1, "x_out", 0, i + 2)
                sp.dma_start(out.rearrange("b t d -> t b d")[:, i:i + 2, :], X[:, i:i + 2, :]).then_inc(s_out, 16)
            sp.wait_ge(s_out, 16 * (NB // 2))

        def blocks(eng, m, split, unit, early=False):
            u0, n_blocks = m["u0"], m["n"]

            def block(n, u, slot, k, nxt):
                if nxt and early:
                    split(*nxt)
                unit(0, u, slot, k)
                if nxt and not early:
                    split(*nxt)
                unit(1, u + 1, slot, k)

            block(0, u0, 0, 1, (1, 1, 1))
            with eng.Fori(0, (n_blocks - 2) // 2) as j:
                block(j * 2 + 1, j * 4 + (u0 + 2), 1, j + 1, (j * 2 + 2, 0, j + 2))
                block(j * 2 + 2, j * 4 + (u0 + 4), 0, j + 2, (j * 2 + 3, 1, j + 2))
            for n in range(2 * ((n_blocks - 2) // 2) + 1, n_blocks):
                nxt = (n + 1, (n + 1) % 2, (n + 1) // 2 + 1) if n + 1 < n_blocks else None
                block(n, u0 + 2 * n, n % 2, n // 2 + 1, nxt)

        def walk(turn, eng, start=None, rule=None, experts=None, last=None):
            for name, chain in (("moe0", [ATTN0, XATTN0, MLA0]), ("moe1", [ATTN1, XATTN1])):
                turn(None, None, (chain[0], 0), None)
                for n, ph in enumerate(chain):
                    prev, nxt = (chain[n - 1] if n else None), (chain[n + 1] if n + 1 < len(chain) else None)
                    turn((ph, 0), (prev, NB - 1) if prev else None, (ph, 1), (prev, NB - 2) if prev else None)
                    turn((ph, 1), (ph, 0), (ph, 2), (prev, NB - 1) if prev else None)
                    first = 3 if ph is MLA0 else 2
                    if first == 3:
                        turn((ph, 2), (ph, 1), (ph, 3), (ph, 0))
                    with eng.Fori(first, NB - 1) as i:
                        turn((ph, i), (ph, i - 1), (ph, i + 1), (ph, i - 2))
                    turn((ph, NB - 1), (ph, NB - 2), (nxt, 0) if nxt else None, (ph, NB - 3))
                turn(None, (chain[-1], NB - 1), None, (chain[-1], NB - 2))
                turn(None, None, None, (chain[-1], NB - 1))
                m = MOES[name]
                if start is not None:
                    start(m)
                if rule is not None:
                    rule(m["rule"])
                if experts is not None:
                    experts(m, name)
                if last is not None:
                    last(m["ph"])

        @block.gpsimd
        def _(pool):
            pool.memset(neghalf[:, :], -0.5).then_inc(s_pinit, 1)
            pool.memset(VA[:, :, :, HD:HD + 1], 1.0).then_inc(s_pinit, 1)
            for j in range(9):
                pool.memset(p16[:, :, 7 + j:8 + j], -1.0 - j).then_inc(s_pinit, 1)
            for j in range(6):
                pool.memset(mr8[:, :, 2 + j:3 + j], -2.0 - j).then_inc(s_pinit, 1)
            pool.memset(cbs0[:, :, E0 - 1:E0], 1.0).then_inc(s_pinit, 1)
            pool.memset(stat[:, :, :, :], 0.0).then_inc(s_pinit, 1)
            pool.wait_ge(s_cst, 16)
            pool.wait_ge(s_pinit, N_INIT)

            def power(ph, i, s_in, s_out_, out_, in_, n=1):
                wait(pool, ph, s_in, i, 1)
                pool.tensor_tensor(out_, in_, neghalf[:, 0:n], ALU.pow).then_inc(sems[s_out_], 1)

            def a0(ph, i):
                if "rms_p" in ph.fires:
                    power(ph, i, "rms_e", "rms_p", rms[:, 2:3], rms[:, 1:2])

            def low(ph, i):
                wait(pool, ph, "ht_m", i, 1)
                dst = HTl[:, :, i, :] if isinstance(i, int) else HTl[:, :, bass.ds(i, 1), :]
                apart(pool, "pool")
                pool.tensor_tensor(dst, rtT[:, :, :], xm[:, :, :], ALU.subtract).then_inc(sems["ht"], 1)

            def a1(ph, i, old):
                if ph in (ATTN1, XATTN1):
                    return
                wait(pool, ph, "k_sb" if ph is MLA0 else "k_a", i, 1)
                masked(ph, i, 0)
                if old and ph in (ATTN0, XATTN0):
                    d2(*old)
                masked(ph, i, 1)

            def e(ph, i):
                if ph is XATTN0:
                    if isinstance(i, int) and i == 0:
                        pool.wait_ge(s_row, 16 * len(ROWS))
                    wait(pool, ph, "xcur", i, 1)
                    wait(pool, ATTN0, "x_out", i, 1)
                    apart(pool, "pool")
                    pool.tensor_tensor(at(X, i), at(X, i), R["bv"][:, :], ALU.add).then_inc(sems["xbv"], 1)

            def d2(ph, i):
                if "bve" in ph.fires:
                    power(ph, i, "bve", "bpw", rstd[:, :], bve[:, :])
                if ph is MLA0:
                    power(ph, i, "hms", "hpw", hrm[:, 2:3], hrm[:, 1:2])
                    wait(pool, ph, "hpw", i, 1)
                    apart(pool, "pool")
                    pool.tensor_tensor(at(H, i), z[:, :], hrm[:, 2:3].to_broadcast([P, D]), ALU.mult).then_inc(sems["hn"], 1)

            def masked(ph, i, c):
                if c == 0:
                    wait(pool, ph, "s_ps", i)
                pool.tensor_tensor(
                    mv[:, c, :, :], raw[:, c, :].unsqueeze(1).to_broadcast([P, 4, P]),
                    CONST[:, C_MASK:C_MASK + 4].unsqueeze(2).to_broadcast([P, 4, P]),
                    ALU.mult).then_inc(sems["mv_sb"], 1)

            def y(ph, i):
                if ph is ATTN1:
                    wait(pool, ph, "k_a", i, 1)
                    masked(ph, i, 0)
                    masked(ph, i, 1)

            def splitter(m):
                b0 = m["u0"] // 2

                def split(n, slot, k):
                    pool.wait_ge(s_bm, n + (b0 + 1))
                    if not isinstance(n, int) or n + b0 >= 2:
                        pool.wait_ge(s_dn, n * 2 + (2 * b0 - 2))
                    pool.tensor_tensor(blkl[slot][:, :], blk[slot][:, :], blkm[:, :], ALU.subtract).then_inc(s_bl, 1)
                return split

            def start(m):
                splitter(m)(0, 0, 1)

            def experts(m, name):
                blocks(pool, m, splitter(m), lambda *a: None)

            def last(ph):
                for h in range(2):
                    wait(pool, ph, "bve", 0, h + 1)
                    pool.tensor_tensor(rstd8[:, 4 * h:4 * h + 4], bve8[:, 4 * h:4 * h + 4], neghalf[:, 0:4],
                                       ALU.pow).then_inc(sems["bpw"], 1)

            def turn(now, before, after, old):
                if readout(before, old):
                    if old and old[0] is ATTN1:
                        d2(*old)
                    if before:
                        d2(*before)
                    if router(old):
                        low(*router(old))
                    return
                if old and not (now and now[0] in (ATTN0, XATTN0)):
                    d2(*old)
                if now:
                    a1(*now, old)
                    y(*now)
                if after:
                    a0(*after)
                    e(*after)
                if router(old):
                    low(*router(old))

            walk(turn, pool, start, experts=experts, last=last)

        @block.scalar
        def _(act):
            def load_table(func, k):
                act.activation(loaded[:, k:k + 1], neghalf[:, 0:1], func, scale=-1.0)

            act.wait_ge(s_pinit, 1)
            load_table(ACT.Exp, 0)
            act.wait_ge(s_cst, 16)

            def wait_src(ph, i):
                before = {"xattn0": ATTN0, "mla0": XATTN0, "attn1": MOE0, "xattn1": ATTN1}
                if ph is ATTN0:
                    act.wait_ge(s_x0, 16)
                    if not isinstance(i, int) or i >= 2:
                        act.wait_ge(s_x1, 16)
                if ph.name in before:
                    if ph is ATTN1:
                        act.wait_ge(sems["x_out"], MOE0.base["x_out"] + 1 + i)
                    else:
                        wait(act, before[ph.name], "x_out", i, 1)

            def router_tokens(ph, i):
                if ph is ROUTE0:
                    wait(act, MLA0, "hn", i, 1)
                else:
                    wait(act, XATTN1, "x_out", i, 1)
                wait(act, ph, "rt_ps", i)
                apart(act, "act")
                act.activation(rcur[:, :], at(H if ph is ROUTE0 else X, i), ACT.Copy).then_inc(sems["rc"], 1)

            def router_xt(ph, i):
                wait(act, ph, "rt_ps", i, 1)
                wait(act, ph, "lg_ps", i)
                wait(act, ph, "ht_m", i)
                wait(act, ph, "ht", i)
                for k in range(KC):
                    ins = act.activation(rtT[:, k, :], router_bank(ph)[:, k * P:k * P + P], ACT.Copy,
                                         scale=col(XT_SCALE["route0"] + k) if ph is ROUTE0 else 1.0)
                ins.then_inc(sems["rt_sb"], 1)

            def high(ph, i):
                wait(act, ph, "ht_m", i, 1)
                dst = HTh[:, :, i, :] if isinstance(i, int) else HTh[:, :, bass.ds(i, 1), :]
                apart(act, "act")
                act.activation(dst, xm[:, :, :], ACT.Copy).then_inc(sems["ht_h"], 1)

            def tokens(ph, i):
                wait_src(ph, i)
                wait(act, ph, "xt_ps", i)
                if "rms_e" in ph.fires:
                    wait(act, ph, "rms_e", i)
                    apart(act, "act")
                    act.activation(junk_a[:, :], at(X, i), ACT.Square,
                                   accum_out=rms[:, 0:1]).then_inc(sems["xc0"], 1)
                else:
                    apart(act, "act")
                    act.activation(xcur[:, :], at(X, i), ACT.Copy).then_inc(sems["xcur"], 1)

            def scaled(ph, i):
                if "rms_e" in ph.fires:
                    wait(act, ph, "rms_p", i, 1)
                    apart(act, "act")
                    act.activation(xcur[:, :], at(X, i), ACT.Copy,
                                   scale=rms[:, 2:3]).then_inc(sems["xcur"], 1)

            def a0(ph, i):
                if isinstance(i, int) and ph is XATTN0:
                    act.wait_ge(s_w["b"], NW["b"])
                wait(act, ph, "xt_ps", i, 1)
                src = M[:, 0:D].rearrange("p (k t) -> p k t", k=KC)
                if ph.name in XT_SCALE:
                    for k in range(KC):
                        ins = act.activation(xT[:, k, :], src[:, k, :], ACT.Copy, scale=col(XT_SCALE[ph.name] + k))
                    ins.then_inc(sems["xt_sb"], 1)
                else:
                    act.activation(xT[:, :, :], src, ACT.Copy).then_inc(sems["xt_sb"], 1)

            def a1(ph, i):
                first = isinstance(i, int) and i == 0
                if first:
                    act.wait_ge(s_pinit, N_INIT)
                    if ph is ATTN0:
                        act.wait_ge(s_lam, 2)
                        act.activation(lam[:, 2:4], lam[:, 0:2], ACT.Exp).then_inc(s_lame, 1)
                t0 = T[0][:, :].rearrange("p (k t) -> p k t", t=P)
                t1 = T[1][:, :].rearrange("p (k t) -> p k t", t=P)
                if ph in (ATTN0, XATTN0):
                    wait(act, ph, "qk_ps", i, 1)
                    wait(act, ph, "mv_sb", i)
                    wait(act, ph, "s_ps", i)
                    if ph is ATTN0:
                        if first:
                            act.wait_ge(s_lam, 4)
                        act.activation(raw[:, :, :], t0[:, KC:2 * KC, :], ACT.Copy).then_inc(sems["k_a"], 1)
                        for r_, rows in enumerate(HALVES):
                            ins = act.activation(stat[rows, :, r_, :], t0[rows, 0:KC, :], ACT.Copy, scale=qscale[rows, 0:1])
                        ins.then_inc(sems["qk_a"], 1)
                    else:
                        for k in range(KC):
                            ins = act.activation(raw[:, k, :], t0[:, KC + k, :], ACT.Identity, bias=col(KB + k))
                        ins.then_inc(sems["k_a"], 1)
                        for k in range(KC):
                            for r_, rows in enumerate(HALVES):
                                ins = act.activation(stat[rows, k, r_, :], t0[rows, k, :], ACT.Identity,
                                                     bias=W["cols"][rows, QB + k:QB + k + 1])
                        ins.then_inc(sems["qk_a"], 1)

            def e(ph, i):
                if ph is XATTN0:
                    wait(act, ph, "rf_ps", i, 1)
                    t1 = T[1][:, :].rearrange("p (k t) -> p k t", t=P)
                    for k in range(2 * KC):
                        ins = act.activation(rT[:, k, :], t1[:, k, :], ACT.Relu, bias=col(FB + k % KC))
                    ins.then_inc(sems["rf_sb"], 1)
                if ph is MLA0:
                    wait(act, ph, "lat_ps", i, 1)
                    wait(act, ph, "v_ps", i)
                    act.activation(latT[:, :], M[:, 256:256 + P], ACT.Copy).then_inc(sems["lat_sb"], 1)
                if ph is ATTN1:
                    values(ph, i)
                    wait(act, ph, "fm_c", i, 1)
                    act.activation(fm2[:, :, :], fm1[:, :, :], ACT.Square).then_inc(sems["fm_q"], 1)

            def values(ph, i):
                if "v_ps" not in ph.fires:
                    return
                wait(act, ph, "v_ps", i, 1)
                dst = VA[:, i, :, 0:HD] if isinstance(i, int) else VA[:, bass.ds(i, 1), :, 0:HD]
                act.activation(dst, M[:, 256:512].rearrange("p (h d) -> p h d", h=NH), ACT.Copy).then_inc(sems["va_sb"], 1)

            def y(ph, i):
                if ph is ATTN1:
                    t1 = T[1][:, :].rearrange("p (k t) -> p k t", t=P)
                    wait(act, ph, "yt_ps", i, 1)
                    wait(act, ph, "mv_sb", i)
                    wait(act, ph, "s_ps", i)
                    act.activation(raw[:, :, :], t1[:, 0:KC, :], ACT.Copy).then_inc(sems["k_a"], 1)
                    for r_, rows in enumerate(HALVES):
                        ins = act.activation(stat[rows, :, r_, :], t1[rows, KC:2 * KC, :], ACT.Copy)
                    ins.then_inc(sems["qk_a"], 1)

            def b(ph, i, h):
                if ph is XATTN1 and h:
                    return
                if ph is XATTN1:
                    wait(act, ph, "mx", i, 1)
                    wait(act, ph, "pt_ps", i)
                    act.activation(PR[:, 0, :], S[:, 0:P], ACT.Exp, scale=1.0 / 16, bias=mxm[:, 1:2], accum_out=recm[:, 0:1]).then_inc(sems["exp"], 1)
                    return
                wait(act, ph, "sub", i, h + 1)
                hs = slice(8 * h, 8 * h + 8)
                if ph is ATTN1:
                    wait(act, ph, "o_ps", i)
                    act.activation(PT[:, hs, :], SM[:, hs, :], ACT.Square, scale=0.25).then_inc(sems["exp"], 1)
                else:
                    wait(act, ph, "pt_ps", i)
                    act.activation(PR[:, hs, :], SM[:, hs, :], ACT.Exp,
                                   scale=1.0 if ph is ATTN0 else 0.25).then_inc(sems["exp"], 1)

            def root(ph, i):
                if ph is ATTN1:
                    wait(act, ph, "fm_e", i, 1)
                    act.activation(fms[:, 3, :], fms[:, 2, :], ACT.Sqrt).then_inc(sems["fm_p"], 1)

            def c(ph, i, part):
                if ph is XATTN1:
                    if part:
                        return
                    wait(act, ph, "pt_ps", i, 1)
                    act.activation(PT[:, 0, :], T[0][:, 0:P], ACT.Copy).then_inc(sems["pt_a"], 1)
                    return
                if ph is ATTN1:
                    return
                q = (0, 2, 3)[part]
                wait(act, ph, "pt_ps", i, q + 1)
                act.activation(PT[:, 4 * q:4 * q + 4, :], T[1 - q % 2][:, :], ACT.Copy).then_inc(sems["pt_a"], 1)

            def d1(ph, i):
                if "ot_ps" in ph.fires:
                    wait(act, ph, "ot_ps", i, 1)
                    act.activation(OT[:, :, :], M[:, 0:D], ACT.Copy).then_inc(sems["ot_sb"], 1)

            def rule(ph):
                if ph is RULE0:
                    n = E0
                    wait(act, ROUTE0, "lg_sb", NB)
                    act.activation(ex[:, :, 0:E0], lg0[:, :, :], ACT.Exp, scale=-1.0).then_inc(sems["lg_e"], 1)
                else:
                    n = E1
                    wait(act, ph, "r3", 0, 1)
                    act.activation(ex[:, :, 0:64], sel[:, :, :], ACT.Exp)
                    act.activation(ex[:, :, 64:65], lg1[:, :, 64:65], ACT.Exp, scale=-1.0).then_inc(sems["lg_e"], 1)
                for h, bank in enumerate((OB, T[1])):
                    wait(act, ph, "cbt_ps", 0, h + 1)
                    act.activation(cbT[0:n, 4 * h:4 * h + 4, :], bank[0:n, :].rearrange("e (b t) -> e b t", b=4),
                                   ACT.Copy).then_inc(sems["cbt_sb"], 1)

            def splitter(m):
                b0 = m["u0"] // 2

                def split(n, slot, k):
                    act.wait_ge(s_bm, n + (b0 + 1))
                    if not isinstance(n, int) or n + b0 >= 2:
                        act.wait_ge(s_dn, n * 2 + (2 * b0 - 2))
                    act.activation(blkh[slot][:, :], blkm[:, :], ACT.Copy).then_inc(s_bh, 1)
                return split

            def start(m):
                splitter(m)(0, 0, 1)

            def experts(m, name):
                def hidden_high(half, u):
                    act.wait_ge(s_hm, u + 1)
                    if not isinstance(u, int) or u >= 2:
                        act.wait_ge(s_dn, u - 1)
                    act.activation(hidh[half][:, :], hidm[half][:, :], ACT.Copy).then_inc(s_hh, 1)

                def unit(half, u, slot, k):
                    act.wait_ge(s_gu, u + 1)
                    if not isinstance(u, int) or u >= 2:
                        act.wait_ge(s_hid, u - 1)
                    act.activation(sil[half][:, :], T[half][:, :], ACT.Silu).then_inc(s_sil, 1)
                    hidden_high(half, u)

                blocks(act, m, splitter(m), unit)
                if name == "moe0":
                    load_table(ACT.Sqrt, 1)

            def turn(now, before, after, old):
                if after and after[0] is XATTN1 and isinstance(after[1], int) and after[1] == 0:
                    load_table(ACT.Exp, 2)
                if readout(before, old):
                    if after:
                        tokens(*after)
                    if before:
                        c(*before, 0)
                    if after:
                        a0(*after)
                    if router(old):
                        router_tokens(*router(old))
                    if now:
                        b(*now, 0)
                    if router(old):
                        router_xt(*router(old))
                        high(*router(old))
                    return
                early = after and after[0] is ATTN1
                if early:
                    tokens(*after)
                    a0(*after)
                if now:
                    a1(*now)
                    y(*now)
                if before:
                    c(*before, 0)
                    b(*before, 1)
                if after and not early:
                    tokens(*after)
                if router(old):
                    router_tokens(*router(old))
                if now and now[0] is not ATTN1:
                    values(*now)
                if before:
                    c(*before, 1)
                if router(old):
                    router_xt(*router(old))
                if before:
                    c(*before, 2)
                if after and not early:
                    scaled(*after)
                    a0(*after)
                if now and now[0] is not ATTN1:
                    b(*now, 0)
                if after:
                    e(*after)
                if before and now and now[0] is ATTN1:
                    d1(*before)
                if now and now[0] is ATTN1:
                    b(*now, 0)
                if after:
                    root(*after)
                if before and not (now and now[0] is ATTN1):
                    d1(*before)
                if router(old):
                    high(*router(old))

            walk(turn, act, start, rule, experts)

        @block.vector
        def _(dve):
            dve.wait_ge(s_cst, 16)
            dve.tensor_copy(identb[:, :], ident).then_inc(s_init, 1)
            dve.tensor_copy(negb[:, :], CONST[:, C_NEG:C_NEG + P]).then_inc(s_init, 1)
            dve.wait_ge(s_row, 16 * len(ROWS))
            lr = R["lam"][:, :].rearrange("p (a n) -> p a n", a=4)
            for j in range(2):
                if j:
                    dve.wait_ge(s_lam, 1)
                dve.tensor_tensor_reduce(out=junk[:, :], in0=lr[:, 2 * j, :], in1=lr[:, 2 * j + 1, :], scale=1.0,
                                         scalar=0.0, op0=ALU.mult, op1=ALU.add,
                                         accum_out=lam[:, j:j + 1]).then_inc(s_lam, 1)
            dve.wait_ge(s_lame, 1)
            dve.tensor_tensor(lam[:, 4:5], lam[:, 2:3], lam[:, 3:4], ALU.subtract).then_inc(s_lam, 1)
            dve.wait_ge(s_lam, 3)
            c8 = float(8 ** -0.5)
            dve.tensor_scalar(lam[:, 5:6], lam[:, 4:5], 0.2, -c8, ALU.add, ALU.mult).then_inc(s_init, 1)
            dve.wait_ge(s_init, 3)
            dve.scalar_tensor_tensor(qscale[:, :], in0=CONST[:, C_SEL + 1:C_SEL + 2], scalar=lam[:, 5:6],
                                     in1=CONST[:, C_SEL:C_SEL + 1], op0=ALU.mult, op1=ALU.add).then_inc(s_lam, 1)

            def a0(ph, i):
                if "rms_e" in ph.fires:
                    wait(dve, ph, "xc0", i, 1)
                    wait(dve, ph, "rms_p", i)
                    dve.tensor_scalar(rms[:, 1:2], rms[:, 0:1], 1.0 / D, EPS, ALU.mult, ALU.add).then_inc(sems["rms_e"], 1)

            def reference_features(ph, i):
                if ph is XATTN0:
                    wait(dve, ph, "rn_ps", i, 1)
                    wait(dve, ph, "xbv", i, 1)
                    dve.tensor_tensor(at(X, i), M[:, 0:D], at(X, i), ALU.add).then_inc(sems["x_ref"], 1)

            def a1(ph, i):
                if ph is MLA0:
                    for s, tb, cc, dst in ((1, T[1], C_SIN, rope2), (0, T[0], C_COS, rope1)):
                        wait(dve, ph, "qk_ps" if s == 0 else "rot_ps", i, 1)
                        dve.tensor_tensor(dst[:, :, :], tb[:, :].rearrange("p (k t) -> p k t", t=P),
                                          CONST[:, cc:cc + P].unsqueeze(1).to_broadcast([P, 2 * KC, P]),
                                          ALU.mult).then_inc(sems["rope_a" if s == 0 else "rope_b"], 1)
                    wait(dve, ph, "rope_a", i, 1)
                    wait(dve, ph, "rope_b", i, 1)
                    wait(dve, ph, "mv_sb", i)
                    wait(dve, ph, "s_ps", i)
                    dve.tensor_tensor(raw[:, :, :], rope1[:, KC:2 * KC, :], rope2[:, KC:2 * KC, :],
                                      ALU.add).then_inc(sems["k_sb"], 1)
                    for r_, rows in enumerate(HALVES):
                        ins = dve.tensor_tensor(stat[rows, :, r_, :], rope1[rows, 0:KC, :], rope2[rows, 0:KC, :], ALU.add)
                    ins.then_inc(sems["q_sb"], 1)

            def bits(ph, i):
                wait(dve, ph, "rt_sb", i, 1)
                wait(dve, ph, "ht_h", i)
                wait(dve, ph, "ht", i)
                dve.tensor_scalar(xm[:, :, :].bitcast(I32), rtT[:, :, :].bitcast(I32), HIGH, None,
                                  ALU.bitwise_and).then_inc(sems["ht_m"], 1)

            def logits(ph, i):
                wait(dve, ph, "lg_ps", i, 1)
                if ph is ROUTE0:
                    dve.tensor_tensor(at(lg0, i), M[:, 256:256 + E0], R["rb"][:, :], ALU.add).then_inc(sems["lg_sb"], 1)
                else:
                    dve.tensor_copy(at(lg1, i), T[1][:, 256:256 + E1]).then_inc(sems["lg_sb"], 1)

            def feature_map(ph, i, part):
                if ph is not ATTN1:
                    return
                src = T[0][:, :].rearrange("p (h d) -> p h d", d=HD)

                def g(c_):
                    return R["gb"][:, c_ * HD:c_ * HD + HD].unsqueeze(1).to_broadcast([P, 2 * NH, HD])

                def per_head(k):
                    return fms[:, k, :].unsqueeze(2).to_broadcast([P, 2 * NH, HD])
                if part == 0:
                    wait(dve, ph, "qk_ps", i, 1)
                    wait(dve, ph, "fm_q", i)
                    wait(dve, ph, "yt_ps", i)
                    dve.tensor_tensor(fm1[:, :, :], src, g(0), ALU.mult).then_inc(sems["fm_g"], 1)
                    wait(dve, ph, "fm_g", i, 1)
                    dve.tensor_tensor(fm2[:, :, :], fm1[:, :, :], g(1), ALU.add).then_inc(sems["fm_b"], 1)
                    wait(dve, ph, "fm_b", i, 1)
                    dve.tensor_reduce(fms[:, 0, :], fm2[:, :, :], AX_X, ALU.add).then_inc(sems["fm_s"], 1)
                    wait(dve, ph, "fm_s", i, 1)
                    dve.scalar_tensor_tensor(fm1[:, :, :], in0=per_head(0), scalar=-1.0 / HD, in1=fm2[:, :, :],
                                             op0=ALU.mult, op1=ALU.add).then_inc(sems["fm_c"], 1)
                if part == 1:
                    wait(dve, ph, "fm_q", i, 1)
                    dve.tensor_reduce(fms[:, 1, :], fm2[:, :, :], AX_X, ALU.add).then_inc(sems["fm_v"], 1)
                    wait(dve, ph, "fm_v", i, 1)
                    dve.tensor_scalar(fms[:, 2, :], fms[:, 1, :], 1.0 / HD, EPS, ALU.mult, ALU.add).then_inc(sems["fm_e"], 1)
                if part == 2:
                    wait(dve, ph, "fm_p", i, 1)
                    dve.reciprocal(fms[:, 0, :], fms[:, 3, :]).then_inc(sems["fm_r"], 1)
                    wait(dve, ph, "fm_r", i, 1)
                    dve.tensor_tensor(fm1[:, :, :], fm1[:, :, :], per_head(0), ALU.mult).then_inc(sems["fm_y"], 1)

            def rule(ph):
                if ph is RULE0:
                    rule0(ph)
                else:
                    rule1(ph)

            def rule0(ph):
                dve.wait_ge(s_pinit, N_INIT)
                wait(dve, ph, "lg_e", 0, 1)
                dve.tensor_scalar(es[:, :, 0:7], ex[:, :, 0:7], 1.0, None, ALU.add).then_inc(sems["r1"], 1)
                wait(dve, ph, "r1", 0, 1)
                dve.reciprocal(p16[:, :, 0:7], es[:, :, 0:7]).then_inc(sems["r2"], 1)
                wait(dve, ph, "r2", 0, 1)
                for i in range(NB):
                    dve.max(m8[:, i, :], p16[:, i, :]).then_inc(sems["r3"], 1)
                wait(dve, ph, "r3", 0, NB)
                dve.tensor_copy(mr8[:, :, 0:2], m8[:, :, 0:2])
                dve.tensor_tensor(rsm[:, 0, :], m8[:, :, 0], m8[:, :, 1], ALU.add).then_inc(sems["r4"], 1)
                wait(dve, ph, "r4", 0, 1)
                for i in range(NB):
                    dve.match_replace(rep0[:, i, :], mr8[:, i, :], p16[:, i, :], 0.0)
                dve.reciprocal(rsm[:, 1, :], rsm[:, 0, :]).then_inc(sems["r5"], 1)
                wait(dve, ph, "r5", 0, 1)
                dve.tensor_tensor(sel[:, :, 0:E0], p16[:, :, 0:E0], rep0[:, :, 0:E0], ALU.subtract).then_inc(sems["r6"], 1)
                wait(dve, ph, "r6", 0, 1)
                dve.tensor_tensor(cbs0[:, :, 0:E0 - 1], sel[:, :, 0:E0 - 1],
                                  rsm[:, 1, :].unsqueeze(2).to_broadcast([P, NB, E0 - 1]), ALU.mult).then_inc(sems["cb"], 1)

            def rule1(ph):
                wait(dve, ROUTE1, "lg_sb", NB)
                for i in range(NB):
                    dve.max(m8[:, i, :], lg1[:, i, 0:64]).then_inc(sems["r1"], 1)
                wait(dve, ph, "r1", 0, NB)
                for i in range(NB):
                    ins = dve.match_replace(rep1[:, i, :], m8[:, i, :], lg1[:, i, 0:64], -3e38)
                ins.then_inc(sems["r2"], 1)
                dve.tensor_tensor(sel[:, :, :], lg1[:, :, 0:64], m8[:, :, 0:1].to_broadcast([P, NB, 64]),
                                  ALU.subtract).then_inc(sems["r3"], 1)
                wait(dve, ph, "r2", 0, 1)
                wait(dve, ph, "lg_e", 0, 1)
                dve.tensor_tensor(sel[:, :, :], lg1[:, :, 0:64], rep1[:, :, :], ALU.not_equal).then_inc(sems["r4"], 1)
                dve.tensor_scalar(rsm[:, 2, :], ex[:, :, 64], 1.0, None, ALU.add)
                wait(dve, ph, "r4", 0, 1)
                dve.tensor_tensor(es[:, :, :], ex[:, :, 0:64], sel[:, :, :], ALU.mult).then_inc(sems["r5"], 1)
                wait(dve, ph, "r5", 0, 1)
                dve.reciprocal(cbs1[:, :, 64], rsm[:, 2, :])
                dve.tensor_reduce(rsm[:, 0, :], es[:, :, :], AX_X, ALU.add).then_inc(sems["r6"], 1)
                wait(dve, ph, "r6", 0, 1)
                dve.reciprocal(rsm[:, 1, :], rsm[:, 0, :]).then_inc(sems["r7"], 1)
                wait(dve, ph, "r7", 0, 1)
                dve.tensor_tensor(cbs1[:, :, 0:64], es[:, :, :], rsm[:, 1, :].unsqueeze(2).to_broadcast([P, NB, 64]),
                                  ALU.mult).then_inc(sems["cb"], 1)

            def b(ph, i, h, after):
                if ph is XATTN1:
                    if h:
                        return

                    if isinstance(i, int) and i == 0:
                        wait(dve, ph, "sub", i)
                    wait(dve, ph, "s_ps", i, 1)
                    wait(dve, ph, "exp", i)
                    dve.tensor_reduce(mxm[:, 0:1], S[:, 0:P], AX_X, ALU.max).then_inc(sems["mxr"], 1)
                    wait(dve, ph, "mxr", i, 1)
                    dve.tensor_scalar(mxm[:, 1:2], mxm[:, 0:1], -1.0 / 16, None, ALU.mult).then_inc(sems["mx"], 1)
                    return
                hs = slice(8 * h, 8 * h + 8)
                s_in = S[:, 1024 * h:1024 * h + 1024].rearrange("p (h t) -> p h t", h=8)
                wait(dve, ph, "s_ps", i, h + 1)
                if ph is ATTN1:
                    wait(dve, ph, "exp", i)
                    dve.tensor_tensor(SM[:, hs, :], s_in, tri.unsqueeze(1).to_broadcast([P, 8, P]),
                                      ALU.mult).then_inc(sems["sub"], 1)
                    return
                dve.tensor_reduce(mx[:, hs], s_in, AX_X, ALU.max).then_inc(sems["mx"], 1)
                if h and after:
                    reference_features(*after)
                wait(dve, ph, "mx", i, h + 1)
                wait(dve, ph, "exp", i)
                dve.tensor_tensor(SM[:, hs, :], s_in, mx[:, hs].unsqueeze(2).to_broadcast([P, 8, P]),
                                  ALU.subtract).then_inc(sems["sub"], 1)

            def c(ph, i, part):
                if ph is XATTN1:
                    if part:
                        return
                    wait(dve, ph, "exp", i, 1)
                    wait(dve, ph, "z_sb", i)
                    dve.reciprocal(recm[:, 1:2], recm[:, 0:1]).then_inc(sems["rec"], 1)
                    wait(dve, ph, "rec", i, 1)
                    v = VALID[:, i:i + 1] if isinstance(i, int) else VALID[:, bass.ds(i, 1)]
                    dve.tensor_tensor(recm[:, 2:3], recm[:, 1:2], v, ALU.mult).then_inc(sems["rv"], 1)
                    return
                if part == 0:
                    if ph is not ATTN1:
                        wait(dve, ph, "pt_ps", i, 2)
                        dve.tensor_copy(PT[:, 4:8, :], T[0][:, :]).then_inc(sems["pt_d"], 1)
                    return
                ob = OB[:, 0:NH * (HD + 1)].rearrange("p (h d) -> p h d", h=NH)
                wait(dve, ph, "o_ps", i, 1)
                den = ob[:, :, HD:HD + 1]
                if ph is ATTN1:
                    dve.tensor_scalar(mx[:, :], den, EPS, None, ALU.add).then_inc(sems["ze"], 1)
                    wait(dve, ph, "ze", i, 1)
                    den = mx[:, :]
                dve.reciprocal(rec[:, :], den).then_inc(sems["rec"], 1)
                wait(dve, ph, "rec", i, 1)
                wait(dve, ph, "z_sb", i)
                dve.tensor_tensor(O[:, :].rearrange("p (h d) -> p h d", h=NH), ob[:, :, 0:HD],
                                  rec[:, :].unsqueeze(2).to_broadcast([P, NH, HD]), ALU.mult).then_inc(sems["o_sb"], 1)

            def layernorm(ph, i):
                wait(dve, ph, "z_sb", i, 1)
                dve.bn_stats(bst[:, :], z[:, :]).then_inc(sems["bst"], 1)
                wait(dve, ph, "bst", i, 1)
                apart(dve, "dve")
                dve.bn_aggr(bag[:, :], bst[:, :]).then_inc(sems["bag"], 1)
                wait(dve, ph, "bag", i, 1)
                dve.tensor_scalar(bve[:, :], bag[:, 1:2], EPS, None, ALU.add).then_inc(sems["bve"], 1)
                wait(dve, ph, "bpw", i, 1)
                dve.tensor_scalar(at(X, i), z[:, :], bag[:, 0:1], rstd[:, 0:1], ALU.subtract, ALU.mult).then_inc(sems["x_out"], 1)

            def d2(ph, i):
                wait(dve, ph, "x_out", i)
                if ph is XATTN0:
                    wait(dve, ph, "o_sb", i, 1)
                    dve.tensor_tensor(z[:, :], O[:, :], at(X, i), ALU.add).then_inc(sems["z_sb"], 1)
                elif ph is XATTN1:
                    wait(dve, ph, "pr_ps", i, 1)
                    wait(dve, ph, "rv", i, 1)
                    dve.scalar_tensor_tensor(z[:, :], in0=OB[:, 0:D], scalar=recm[:, 2:3], in1=at(X, i),
                                             op0=ALU.mult, op1=ALU.add).then_inc(sems["z_sb"], 1)
                elif ph is ATTN0:
                    wait(dve, ph, "pr_ps", i, 1)
                    dve.scalar_tensor_tensor(z[:, :], in0=OB[:, 0:D], scalar=OUT0, in1=at(X, i),
                                             op0=ALU.mult, op1=ALU.add).then_inc(sems["z_sb"], 1)
                elif ph is MLA0:
                    wait(dve, ph, "pr_ps", i, 1)
                    wait(dve, ph, "hn", i)
                    dve.tensor_tensor(z[:, :], OB[:, 0:D], at(X, i), ALU.add).then_inc(sems["z_sb"], 1)
                    wait(dve, ph, "z_sb", i, 1)
                    dve.tensor_tensor(at(X, i), z[:, :], at(X, i), ALU.add).then_inc(sems["xh"], 1)
                    dve.tensor_tensor_reduce(out=junk[:, :], in0=z[:, :], in1=z[:, :], scale=1.0, scalar=0.0,
                                             op0=ALU.mult, op1=ALU.add, accum_out=hrm[:, 0:1]).then_inc(sems["hsq"], 1)
                    wait(dve, ph, "hsq", i, 1)
                    dve.tensor_scalar(hrm[:, 1:2], hrm[:, 0:1], 1.0 / D, EPS, ALU.mult, ALU.add).then_inc(sems["hms"], 1)
                    return
                else:
                    wait(dve, ph, "pr_ps", i, 1)
                    dve.tensor_tensor(z[:, :], OB[:, 0:D], at(X, i), ALU.add).then_inc(sems["z_sb"], 1)
                layernorm(ph, i)

            def splitter(m):
                b0 = m["u0"] // 2

                def split(n, slot, k):
                    dve.wait_ge(s_blk[slot], landed(m["ph"].name, k))
                    if not isinstance(n, int) or n + b0 >= 1:
                        dve.wait_ge(s_bh, n + b0)
                        dve.wait_ge(s_bl, n + b0)
                    dve.tensor_scalar(blkm[:, :].bitcast(I32), blk[slot][:, :].bitcast(I32), HIGH, None,
                                      ALU.bitwise_and).then_inc(s_bm, 1)
                return split

            def start(m):
                splitter(m)(0, 0, 1)

            def experts(m, name):
                ub = [M, OB]

                def unit(half, u, slot, k):
                    later = not isinstance(u, int) or u >= 2
                    dve.wait_ge(s_gu, u + 1)
                    if name == "moe0" and not later:
                        dve.tensor_scalar(hid0[half][:, :], ub[half][:, :], m["scale"], None, ALU.mult).then_inc(s_h0, 1)
                    else:
                        dve.wait_ge(s_wb[slot], spread_in(name, k, slot))
                        if later:
                            dve.wait_ge(s_hid, u - 1)
                        dve.scalar_tensor_tensor(hid0[half][:, :], in0=ub[half][:, :], scalar=m["scale"],
                                                 in1=wb[slot][:, 512 * half:512 * half + 512],
                                                 op0=ALU.mult, op1=ALU.mult).then_inc(s_h0, 1)
                    dve.wait_ge(s_h0, u + 1)
                    dve.wait_ge(s_sil, u + 1)
                    if later:
                        dve.wait_ge(s_hl, u - 1)
                    dve.tensor_tensor(hid[half][:, :], hid0[half][:, :], sil[half][:, :], ALU.mult).then_inc(s_hid, 1)
                    dve.wait_ge(s_hid, u + 1)
                    if later:
                        dve.wait_ge(s_hh, u - 1)
                    dve.tensor_scalar(hidm[half][:, :].bitcast(I32), hid[half][:, :].bitcast(I32), HIGH, None,
                                      ALU.bitwise_and).then_inc(s_hm, 1)
                    dve.wait_ge(s_hm, u + 1)
                    if later:
                        dve.wait_ge(s_dn, u - 1)
                    dve.tensor_tensor(hidl[half][:, :], hid[half][:, :], hidm[half][:, :], ALU.subtract).then_inc(s_hl, 1)

                blocks(dve, m, splitter(m), unit, early=True)

            def last(ph):
                m = MOES[ph.name]

                def normalise(h):
                    wait(dve, ph, "bpw", 0, h + 1)
                    for i in range(4 * h, 4 * h + 4):
                        dve.tensor_scalar(X[:, i, :], S[:, i * D:i * D + D], bag8[:, i, 0:1], rstd8[:, i:i + 1],
                                          ALU.subtract, ALU.mult).then_inc(sems["x_out"], 1)

                for h in range(2):
                    dve.wait_ge(s_dn, m["u0"] + 2 * m["n"] - 1 + h)
                    for i in range(4 * h, 4 * h + 4):
                        dve.bn_stats(bst8[:, i, :], S[:, i * D:i * D + D]).then_inc(sems["bst"], 1)
                    wait(dve, ph, "bst", 0, 4 * h + 4)
                    for i in range(4 * h, 4 * h + 4):
                        dve.bn_aggr(bag8[:, i, :], bst8[:, i, :]).then_inc(sems["bag"], 1)
                    wait(dve, ph, "bag", 0, 4 * h + 4)
                    dve.tensor_scalar(bve8[:, 4 * h:4 * h + 4], bag8[:, 4 * h:4 * h + 4, 1], EPS, None, ALU.add).then_inc(sems["bve"], 1)
                    if h:
                        normalise(0)
                normalise(1)
                if ph is MOE0:
                    dve.wait_ge(s_mk, 16)
                    dve.tensor_copy(MK[:, :, :].rearrange("p b t -> p (b t)"), MKU[:, :].bitcast(U8)).then_inc(s_init, 1)
                    dve.wait_ge(s_init, 4)
                    dve.tensor_reduce(VALID[:, :], MK[:, :, :], AX_X, ALU.max)
                    dve.tensor_scalar(MKN[:, :, :], MK[:, :, :], -NEG, NEG, ALU.mult, ALU.add).then_inc(s_mk2, 1)

            def turn(now, before, after, old):
                if now:
                    a1(*now)
                if before:
                    c(*before, 0)
                if after:
                    a0(*after)
                if after:
                    feature_map(*after, 0)
                if before and before[0] is ATTN1:
                    c(*before, 1)
                if readout(before, old):
                    if now:
                        b(*now, 0, after)
                    if router(old):
                        bits(*router(old))
                    if before:
                        d2(*before)
                    if router(old):
                        logits(*router(old))
                    return
                if router(old):
                    bits(*router(old))
                    logits(*router(old))
                if now:
                    b(*now, 0, after)
                if after:
                    feature_map(*after, 1)
                if before and before[0] is not ATTN1:
                    c(*before, 1)
                if after:
                    feature_map(*after, 2)
                if now:
                    b(*now, 1, after)
                if before:
                    d2(*before)

            walk(turn, dve, start, rule, experts, last)

        @block.tensor
        def _(pe):
            pe.wait_ge(s_cst, 16)

            def mm(out_, lhsT, rhs, start=True, stop=True, **kw):
                return pe.matmul(out_, lhsT, rhs, start=start, stop=stop, **kw)

            def over_k(out_, lhsT, rhs):
                for k in range(KC):
                    ins = mm(out_, lhsT(k), rhs(k), start=(k == 0), stop=(k == KC - 1))
                return ins

            def a0(ph, i):
                wait(pe, ph, "xcur", i, 1)
                wait(pe, ph, "va_sb", i)
                wait(pe, ph, "xt_sb", i)
                for k in range(KC):
                    ins = pe.transpose(M[:, k * P:k * P + P], xcur[:, k * P:k * P + P], ident)
                ins.then_inc(sems["xt_ps"], 1)

            def a1(ph, i):
                first = isinstance(i, int) and i == 0
                t0 = T[0][:, :].rearrange("p (k t) -> p k t", t=P)
                t1 = T[1][:, :].rearrange("p (k t) -> p k t", t=P)
                if ph is ATTN1:
                    return
                wait(pe, ph, "xt_sb", i, 1)
                if ph is XATTN1:
                    cx = CTXT[:, :, i, :] if isinstance(i, int) else CTXT[:, :, bass.ds(i, 1), :]
                    wait(pe, ph, "exp", i)
                    if first:
                        wait(pe, ph, "sub", i)
                        pe.wait_ge(s_mk2, 1)
                    mk = MKN[:, i, :] if isinstance(i, int) else MKN[:, bass.ds(i, 1), :]
                    mm(S[:, 0:P], identb[:, :], mk, stop=False)
                    for k in range(KC):
                        ins = mm(S[:, 0:P], xT[:, k, :], cx[:, k], start=False, stop=(k == KC - 1))
                    ins.then_inc(sems["s_ps"], 1)
                    return
                if ph is ATTN0:
                    w, v = wv("w0_qk"), wv("w0_v")
                    for c in range(KC):
                        ins = over_k(t0[:, c, :], lambda k: w[:, k, c * P:c * P + P], lambda k: xT[:, k, :])
                    ins.then_inc(sems["qk_ps"], 1)
                if ph is XATTN0:
                    wait(pe, ph, "rf_sb", i, 1)
                    for k in range(KC):
                        ins = pe.transpose(M[:, k * P:k * P + P], rT[:, k, :], ident)
                    ins.then_inc(sems["rn_ps"], 1)
                    for n, wn in enumerate(("wx_q", "wx_k")):
                        w = wv(wn)
                        for c in range(KC):
                            ins = over_k(t0[:, KC * n + c, :], lambda k: w[:, k, c * P:c * P + P], lambda k: rT[:, KC * n + k, :])
                    ins.then_inc(sems["qk_ps"], 1)
                    v = wv("wx_v")
                    wait(pe, ph, "x_ref", i, 1)
                if ph is MLA0:
                    kx, up = wv("wm_kx"), wv("wm_up", 3)
                    wait(pe, ph, "lat_sb", i, 1)
                    for c in range(KC):
                        ins = mm(t1[:, c, :], W["wm_qr"][:, c * P:c * P + P], latT[:, :])
                    ins.then_inc(sems["rot_ps"], 1)
                    for c in range(KC):
                        cs = slice(c * P, c * P + P)
                        for k in range(KC):
                            mm(t0[:, KC + c, :], kx[:, k, cs], xT[:, k, :], start=(k == 0), stop=False)
                        mm(t0[:, KC + c, :], up[:, 0, cs], latT[:, :], start=False)
                        ins = mm(t0[:, c, :], up[:, 1, cs], latT[:, :])
                    ins.then_inc(sems["qk_ps"], 1)
                    mm(M[:, 256:512], latT[:, :], up[:, 2, :]).then_inc(sems["v_ps"], 1)
                    return
                src = rT[:, KC:2 * KC, :] if ph is XATTN0 else xT[:, :, :]
                over_k(M[:, 256:512], lambda k: src[:, k, :], lambda k: v[:, k, :]).then_inc(sems["v_ps"], 1)

            def e2(ph, i):
                first = isinstance(i, int) and i == 0
                bank, c0, w = {"attn0": (T[0], KC, "w0_qk"), "mla0": (T[1], 0, "wm_kr")}.get(ph.name, (None, 0, ""))
                if bank is None:
                    return
                if first and ph is ATTN0:
                    pe.wait_ge(s_w["a"], NW["a"])
                w = wv(w)
                wait(pe, ph, "xt_sb", i, 1)
                for c in range(KC):
                    over_k(bank[:, (KC + c) * P:(KC + c) * P + P],
                           lambda k: w[:, k, (c0 + c) * P:(c0 + c) * P + P], lambda k: xT[:, k, :])

            def e(ph, i):
                first = isinstance(i, int) and i == 0
                if ph is XATTN0:
                    if first:
                        pe.wait_ge(s_w["b"], NW["b"])
                        pe.wait_ge(s_ctxt, 16)
                    w, t1 = wv("wx_fc"), T[1][:, :].rearrange("p (k t) -> p k t", t=P)
                    cx = CTXT[:, :, i, :] if isinstance(i, int) else CTXT[:, :, bass.ds(i, 1), :]
                    for c in range(KC):
                        over_k(t1[:, KC + c, :], lambda k: w[:, k, c * P:c * P + P], lambda k: cx[:, k])
                    wait(pe, ph, "xt_sb", i, 1)
                    for c in range(KC):
                        ins = over_k(t1[:, c, :], lambda k: w[:, k, c * P:c * P + P], lambda k: xT[:, k, :])
                    ins.then_inc(sems["rf_ps"], 1)
                if ph is MLA0:
                    if first:
                        pe.wait_ge(s_w["c"], NW["c"])
                    lt = wv("wm_lat")
                    wait(pe, ph, "xt_sb", i, 1)
                    over_k(M[:, 256:256 + P], lambda k: lt[:, k, :], lambda k: xT[:, k, :]).then_inc(sems["lat_ps"], 1)
                if ph is ATTN1:
                    if first:
                        pe.wait_ge(s_w["e"], NW["e"])
                    w, v = wv("w1_qk"), wv("w1_v")
                    wait(pe, ph, "xt_sb", i, 1)
                    wait(pe, ph, "fm_g", i)
                    over_k(T[0][:, :], lambda k: xT[:, k, :], lambda k: w[:, k, :]).then_inc(sems["qk_ps"], 1)
                    over_k(M[:, 256:512], lambda k: xT[:, k, :], lambda k: v[:, k, :]).then_inc(sems["v_ps"], 1)

            def y(ph, i):
                if ph is ATTN1:
                    wait(pe, ph, "fm_y", i, 1)
                    y = fm1[:, :, :].rearrange("p h d -> p (h d)")
                    for c in range(4):
                        ins = pe.transpose(T[1][:, c * P:c * P + P], y[:, c * P:c * P + P], ident)
                    ins.then_inc(sems["yt_ps"], 1)

            def b(ph, i, js):
                if ph is XATTN1:
                    return
                wait(pe, ph, "mv_sb", i, js[0] // 2 + 1)
                if ph is MLA0:
                    wait(pe, ph, "q_sb", i, 1)
                    if isinstance(i, int) and i == 0:
                        pe.wait_ge(s_init, 2)
                else:
                    wait(pe, ph, "qk_a", i, 1)
                wait(pe, ph, "sub", i)
                if ph is ATTN1 and isinstance(i, int):
                    wait(pe, MOE0, "x_out", 0, NB)
                for j in js:
                    c, r = j // 2, j % 2
                    bank = S[:, 512 * j:512 * j + 512]
                    if ph is MLA0:
                        mm(bank, identb[:, :], negb[:, :].unsqueeze(1).to_broadcast([P, 4, P]), stop=False)
                    ins = mm(bank, stat[:, c, r, :], mv[:, c, :, :], start=ph is not MLA0)
                    if j % 2:
                        ins.then_inc(sems["s_ps"], 1)

            def c(ph, i, now, part):
                if ph is XATTN1:
                    if part == 0:
                        wait(pe, ph, "exp", i, 1)
                        pe.transpose(T[0][:, 0:P], PR[:, 0, :], ident).then_inc(sems["pt_ps"], 1)
                    if part != 1:
                        return
                    cx = CTX[:, i, :] if isinstance(i, int) else CTX[:, bass.ds(i, 1), :]
                    if isinstance(i, int):
                        pe.wait_ge(s_ctx, 16)
                    wait(pe, ph, "pt_a", i, 1)
                    wait(pe, ph, "z_sb", i)
                    mm(OB[:, 0:D], PT[:, 0, :], cx).then_inc(sems["pr_ps"], 1)
                    return

                def pv(q):
                    if q == 0:
                        wait(pe, ph, "z_sb", i)
                        wait(pe, ph, "va_sb", i, 1)
                    if ph is ATTN1:
                        wait(pe, ph, "exp", i, q // 2 + 1)
                    else:
                        copied(q)
                    for h in range(4 * q, 4 * q + 4):
                        vv = VA[:, i, h, :] if isinstance(i, int) else VA[:, bass.ds(i, 1), h, :]
                        ins = mm(OB[:, 17 * h:17 * h + 17], PT[:, h, :], vv)
                    if q == 3:
                        ins.then_inc(sems["o_ps"], 1)

                def copied(q):
                    wait(pe, ph, "pt_d" if q == 1 else "pt_a", i, (1, 1, 2, 3)[q])

                def pt(q):
                    if q % 2 == 0:
                        wait(pe, ph, "exp", i, q // 2 + 1)
                    if q < 2:
                        free(now, q)
                    else:
                        copied(q - 2)
                    for h in range(4):
                        ins = pe.transpose(T[1 - q % 2][:, h * P:h * P + P], PR[:, 4 * q + h, :], ident)
                    ins.then_inc(sems["pt_ps"], 1)

                if ph is ATTN1:
                    pv(2 * part)
                    pv(2 * part + 1)
                elif part == 0:
                    pt(0)
                    pt(1)
                    pv(0)
                    pt(2)
                elif part == 1:
                    pv(1)
                    pt(3)
                else:
                    pv(2)
                    pv(3)

            def free(now, q):
                if now:
                    ph, i = now
                    if q:
                        wait(pe, ph, "qk_a", i, 1)
                        wait(pe, ph, "rope_a", i, 1)
                    else:
                        wait(pe, ph, "rope_b", i, 1)

            def d1(ph, i, after):
                if "ot_ps" not in ph.fires:
                    return
                if after:
                    ph2, i2 = after
                    wait(pe, ph2, "xt_sb", i2, 1)
                    if ph2 is MLA0:
                        wait(pe, ph2, "lat_sb", i2, 1)
                    if ph2 is ATTN1:
                        wait(pe, ph2, "va_sb", i2, 1)
                wait(pe, ph, "o_sb", i, 1)
                for k in range(KC):
                    ins = pe.transpose(M[:, k * P:k * P + P], O[:, k * P:k * P + P], ident)
                ins.then_inc(sems["ot_ps"], 1)

            def d2(ph, i):
                if "ot_ps" not in ph.fires:
                    return
                w = wv({"attn0": "w0_o", "mla0": "wm_o", "attn1": "w1_o"}[ph.name])
                wait(pe, ph, "ot_sb", i, 1)
                over_k(OB[:, 0:D], lambda k: OT[:, k, :], lambda k: w[:, k, :]).then_inc(sems["pr_ps"], 1)

            def rule(ph):
                cbs = cbs0 if ph is RULE0 else cbs1
                wait(pe, ph, "cb", 0, 1)
                wait(pe, ph, "z_sb", 0, past=True)
                for i in range(NB):
                    bank = (OB, T[1])[i // 4]
                    ins = pe.transpose(bank[0:cbs.shape[2], i % 4 * P:i % 4 * P + P], cbs[:, i, :], ident)
                    if i % 4 == 3:
                        ins.then_inc(sems["cbt_ps"], 1)

            def stages(m):
                u0, ub = m["u0"], [M, OB]

                def parts3(out_, left, right, start=True, stop=True, **kw):
                    (lh, ll), (rh, rl) = left, right
                    mm(out_, lh, rl, start=start, stop=False, **kw)
                    mm(out_, lh, rh, start=False, stop=False, **kw)
                    return mm(out_, ll, rh, start=False, stop=stop, **kw)

                def gate_up(half, u, slot, n):
                    if half == 0:
                        pe.wait_ge(s_bh, n + (u0 // 2 + 1))
                        pe.wait_ge(s_bl, n + (u0 // 2 + 1))
                    if not isinstance(u, int) or u >= 2:
                        pe.wait_ge(s_sil, u - 1)
                        pe.wait_ge(s_h0, u - 1)
                    w = [b[slot][:, 0:512].rearrange("p (g k n) -> p g k n", g=2, k=KC) for b in (blkh, blkl)]
                    for g, bank in ((1, ub[half]), (0, T[half])):
                        for k in range(KC):
                            ins = parts3(bank[:, :], [w_[:, g, k, :] for w_ in w],
                                         [h_[:, k, 4 * half:4 * half + 4, :] for h_ in (HTh, HTl)],
                                         start=(k == 0), stop=(k == KC - 1))
                    ins.then_inc(s_gu, 1)

                def down(half, u, slot):
                    pe.wait_ge(s_hh, u + 1)
                    pe.wait_ge(s_hl, u + 1)
                    for t in range(4):
                        tok = 4 * half + t
                        ins = parts3(S[:, D * tok:D * tok + D], [h_[half][:, t * P:t * P + P] for h_ in (hidh, hidl)],
                                     [b[slot][:, 512:768] for b in (blkh, blkl)],
                                     start=False, stop=False, skip_group_check=True)
                    ins.then_inc(s_dn, 1)
                return gate_up, down

            def residual(ph, j):
                wait(pe, ph, "exp", 0)
                wait(pe, ph, "sub", 0)
                wait(pe, MLA0 if ph is ROUTE0 else XATTN1, "xh" if ph is ROUTE0 else "x_out", 2 * j + 2)
                mm(S[:, 512 * j:512 * j + 512], ident, X[:, 2 * j:2 * j + 2, :], stop=False, skip_group_check=True)

            def start(m):
                prev = m["prev"]
                residual(prev, 3)
                wait(pe, prev, "ht", NB)
                wait(pe, prev, "ht_h", NB)
                wait(pe, prev, "xt_sb", NB)
                wait(pe, prev, "lg_sb", NB)
                stages(m)[0](0, m["u0"], 0, 0)

            def experts(m, name):
                u0, n_blocks = m["u0"], m["n"]
                gate_up, down = stages(m)
                wait(pe, m["rule"], "cbt_sb", 0, 2)
                gate_up(1, u0 + 1, 0, 0)
                down(0, u0, 0)
                with pe.Fori(0, (n_blocks - 1) // 2) as j:
                    for k in range(4):
                        slot, half = 1 - k // 2, k % 2
                        u = j * 4 + (u0 + 2 + k)
                        gate_up(half, u, slot, j * 2 + (1 + k // 2))
                        down(1 - half, j * 4 + (u0 + 1 + k), (0, 1, 1, 0)[k])
                if n_blocks % 2 == 0:
                    u = u0 + 2 * (n_blocks - 1)
                    gate_up(0, u, 1, n_blocks - 1)
                    down(1, u - 1, 0)
                    gate_up(1, u + 1, 1, n_blocks - 1)
                    down(0, u, 1)
                    down(1, u + 1, 1)
                else:
                    down(1, u0 + 2 * n_blocks - 1, 0)

            def router_xt(ph, i, now):
                wait(pe, ph, "rc", i, 1)
                wait(pe, ph, "lg_sb", i)
                if now:
                    wait(pe, now[0], "va_sb", now[1], 1)
                for k in range(KC):
                    ins = pe.transpose(router_bank(ph)[:, k * P:k * P + P], rcur[:, k * P:k * P + P], ident)
                ins.then_inc(sems["rt_ps"], 1)

            def logits(ph, i):
                n, g = (E0, "d") if ph is ROUTE0 else (E1, "e")
                if isinstance(i, int) and i == 0:
                    pe.wait_ge(s_w[g], NW[g])
                w = wv("w_rt0" if ph is ROUTE0 else "w_rt1")
                wait(pe, ph, "rt_sb", i, 1)
                over_k(router_bank(ph)[:, 256:256 + n], lambda k: rtT[:, k, :], lambda k: w[:, k, :]).then_inc(sems["lg_ps"], 1)

            def turn(now, before, after, old):
                early, rt = after and after[0] is ATTN1, router(old)
                if readout(before, old):
                    if now:
                        a1(*now)
                    if before:
                        c(*before, now, 0)
                    if after:
                        a0(*after)
                    if before:
                        c(*before, now, 1)
                    if rt:
                        router_xt(*rt, None)
                        logits(*rt)
                    if rt and not now:
                        for j in ((0, 1) if before else (2,)):
                            residual(rt[0], j)
                    return
                if early:
                    a0(*after)
                if now:
                    a1(*now)
                    y(*now)
                if early:
                    e(*after)
                if before:
                    c(*before, now, 0)
                if now and not early:
                    b(*now, (0,))
                if rt:
                    router_xt(*rt, now)
                if before:
                    c(*before, now, 1)
                if early:
                    if now:
                        b(*now, (0, 1))
                    if before:
                        d1(*before, after)
                    if now:
                        b(*now, (2, 3))
                else:
                    if now:
                        b(*now, (1,))
                    if rt:
                        logits(*rt)
                    if before and before[0] is not ATTN1:
                        c(*before, now, 2)
                    if rt:
                        wait(pe, rt[0], "lg_sb", rt[1], 1)
                    if after:
                        a0(*after)
                    if after and after[0] is XATTN0:
                        e(*after)
                    if now:
                        b(*now, (2,))
                    if after and after[0] is MLA0:
                        e(*after)
                    if now:
                        b(*now, (3,))
                if before and not early:
                    d1(*before, after)
                if after:
                    e2(*after)
                if before:
                    d2(*before)
                if rt and not now:
                    for j in ((0, 1) if before else (2,)):
                        residual(rt[0], j)

            walk(turn, pe, start, rule, experts)


def constants():
    c = np.zeros((P, C_END), np.float32)
    p, t = np.arange(P)[:, None], np.arange(P)[None, :]
    c[:, C_ID:C_ID + P] = p == t
    c[:, C_TRI:C_TRI + P] = p <= t
    c[:, C_NEG:C_NEG + P] = np.where(t > p, np.float32(NEG), np.float32(0))
    inv = np.float32(1) / np.power(np.float32(10000), np.arange(0, RD, 2, dtype=np.float32) / np.float32(RD))
    ang = np.outer(np.arange(P, dtype=np.float32), inv.astype(np.float32)).astype(np.float32)
    emb = np.concatenate([ang, ang], axis=-1).T
    for row in range(P):
        d = row % HD
        if d < RD:
            c[row, C_COS:C_COS + P] = 1
        else:
            c[row, C_COS:C_COS + P] = np.cos(emb[d - RD])
            c[row, C_SIN:C_SIN + P] = np.sin(emb[d - RD]) * (-1 if d - RD < RD // 2 else 1)
        c[row, C_MASK + row % 64 // HD] = 1
        c[row, C_SEL + (0 if d < RD else 1)] = np.float32(8 ** -0.5) if d < RD else 1
    return c


def kernel(**inputs):
    import concourse.bacc as bacc
    from concourse.bass_utils import run_bass_kernel_spmd as run

    a = {n: np.asarray(v) for n, v in inputs.items()}

    def chunks(w):
        return np.ascontiguousarray(w.reshape(-1, P, w.shape[1]).transpose(1, 0, 2).reshape(P, -1))

    def row(*vs):
        return np.ascontiguousarray(np.concatenate([v.reshape(-1) for v in vs])[None, :])

    h, d = np.arange(NH)[:, None], np.arange(HD)[None, :]
    half = HD // 2
    q_cols = np.where(d < half, h * half + d, 256 + h * half + d - half).reshape(-1)
    wa = a["L0_attn_W_attn"]
    rope = (h * RD + d - RD)[:, RD:]
    swap = np.concatenate([rope[:, RD // 2:], rope[:, :RD // 2]], axis=1)

    def spread(plain, roped, order):
        src = plain if plain is not None else roped
        w = np.zeros((src.shape[0], NH, HD), np.float32)
        if plain is not None:
            w[:, :, :RD] = plain.reshape(-1, NH, RD)
        if roped is not None:
            w[:, :, RD:] = roped[:, order]
        return w.reshape(-1, D)

    kr, qr = a["L0_ffn_rope_k_w"], a["L0_ffn_rope_q_w"]
    up = np.zeros((P, 3, D), np.float32)
    up[:LAT, 0] = spread(a["L0_ffn_k_u_w"], None, None)
    up[LAT:, 1] = spread(a["L0_ffn_q_u_w"], qr, rope)
    up[:LAT, 2] = a["L0_ffn_v_u_w"]
    qrot = np.zeros((P, D), np.float32)
    qrot[LAT:] = spread(None, qr, swap)
    cols = np.zeros((P, 16), np.float32)
    for n, name in enumerate(["L0_ffn_ln1_w", "L0_ffn_ln2_w", "L0_xattn_b_q", "L0_xattn_b_k", "L0_xattn_b_fc"]):
        cols[:, 2 * n:2 * n + 2] = a[name].reshape(KC, P).T
    rt0 = np.zeros((D, E0), np.float32)
    rt0[:, :7] = a["L0_ffn_router_w"]
    rb = np.zeros((E0,), np.float32)
    rb[:7] = a["L0_ffn_router_b"]

    def block(gate, upw, down):
        return np.concatenate([chunks(gate), chunks(upw), down], axis=1)

    blocks0 = np.stack([block(a["L0_ffn_sh_gate"], a["L0_ffn_sh_up"], a["L0_ffn_sh_down"])] +
                       [block(a["L0_ffn_r_gate"][e], a["L0_ffn_r_up"][e], a["L0_ffn_r_down"][e]) for e in range(7)])
    gu, dn = a["L1_ffn_gate_up_proj"], a["L1_ffn_down_proj"]
    none = np.zeros((D, 64), np.float32)
    shared = block(np.concatenate([a["L1_ffn_shared_gate_w"].T, none], axis=1),
                   np.concatenate([a["L1_ffn_shared_up_w"].T, none], axis=1),
                   np.concatenate([a["L1_ffn_shared_down_w"].T, none.T], axis=0))
    blocks1 = np.stack([shared] + [
        block(np.concatenate([gu[e, :64].T, gu[e + 1, :64].T], axis=1),
              np.concatenate([gu[e, 64:].T, gu[e + 1, 64:].T], axis=1),
              np.concatenate([dn[e].T, dn[e + 1].T], axis=0)) for e in range(0, 64, 2)])

    arrays = {
        "x": a["x"], "ctx": a["ctx_2048"], "ctxT": a["ctx_2048"].reshape(-1, D).T,
        "mask": a["mask_BxS2_bk0"].reshape(1, -1).view(np.int32), "consts": constants(),
        "row_lam": row(a["L0_attn_lambda_q1"], a["L0_attn_lambda_k1"], a["L0_attn_lambda_q2"], a["L0_attn_lambda_k2"]),
        "row_bv": row(a["L0_xattn_b_v"]), "row_rb": row(rb), "row_gb": row(a["L1_attn_gamma"], a["L1_attn_beta"]),
        "w0_qk": chunks(np.concatenate([wa[:, q_cols], wa[:, q_cols + 128]], axis=1)),
        "w0_v": chunks(wa[:, 512:]), "w0_o": chunks(a["L0_attn_W_proj"]),
        "wx_fc": chunks(a["L0_xattn_W_fc"].T), "wx_q": chunks(a["L0_xattn_W_q"].T), "wx_k": chunks(a["L0_xattn_W_k"].T),
        "wx_v": chunks(a["L0_xattn_W_v"].reshape(D, D).T),
        "wm_lat": chunks(np.concatenate([a["L0_ffn_kv_d_w"], a["L0_ffn_q_d_w"]], axis=1)),
        "wm_kx": chunks(spread(None, kr, rope)), "wm_kr": chunks(spread(None, kr, swap)),
        "wm_up": up.reshape(P, -1), "wm_qr": qrot, "wm_o": chunks(a["L0_ffn_o_w"]), "w_rt0": chunks(rt0), "cols": cols,
        "w1_qk": chunks(np.concatenate([a["L1_attn_Wq"].T, a["L1_attn_Wk"].T], axis=1)),
        "w1_v": chunks(a["L1_attn_Wv"].T), "w1_o": chunks(a["L1_attn_Wo"].T),
        "w_rt1": chunks(np.concatenate([a["L1_ffn_router_w"].T, a["L1_ffn_shared_expert_gate_w"].T], axis=1)),
        "blocks0": blocks0, "blocks1": blocks1,
    }
    nc = bacc.Bacc("TRN2", target_bir_lowering=False, num_devices=1)
    arrays = {n: np.ascontiguousarray(v) for n, v in arrays.items()}
    t_in = {n: nc.dram_tensor("in_" + n, v.shape, mybir.dt.from_np(v.dtype), kind="ExternalInput").ap()
            for n, v in arrays.items()}
    out = nc.dram_tensor("out_0", (NB, P, D), F32, kind="ExternalOutput").ap()
    build(nc, t_in, out)
    r = run(nc, [{"in_" + n: v for n, v in arrays.items()}], core_ids=[0])
    return r.results[0]["out_0"]
```
